# Optimizing a Trainium2 kernel written in Bass

```python
import numpy as np
import jax
import jax.numpy as jnp

def _softmax(x, axis=-1):
    return jax.nn.softmax(x, axis=axis)

def _gelu(x):
    return jax.nn.gelu(x, approximate=True)

def _silu(x):
    return jax.nn.silu(x)

def _sigmoid(x):
    return jax.nn.sigmoid(x)

def _layernorm(x, axis=-1, eps=1e-05):
    m = jnp.mean(x, axis=axis, keepdims=True)
    v = jnp.var(x, axis=axis, keepdims=True)
    return (x - m) / jnp.sqrt(v + eps)

def _scatter_add(tgt, idx, src, axis=0):
    return tgt.at[idx].add(src)

def _segment_sum(src, seg, n):
    return jax.ops.segment_sum(src, seg, n)
kernel_name = 'mk_flamingo_gated_d4_seqx_r8_a4aa85'

def setup_inputs(seed: int=0):
    np.random.seed(seed)
    _w = jnp.asarray

    def _rec_inputs():
        import jax
        import jax.numpy as jnp
        _rk = jax.random.key(seed)
        x = -0.0002928 + 1 * jax.random.normal(jax.random.fold_in(_rk, 1), (2, 512, 128), jnp.float32)
        _lenS = 512 - jax.random.randint(jax.random.fold_in(_rk, 7), (2,), 0, max(1, 512 // 4) + 1, jnp.int32)
        _lenS2 = 77 - jax.random.randint(jax.random.fold_in(_rk, 8), (2,), 0, max(1, 77 // 4) + 1, jnp.int32)
        _ctx_1024P = jax.random.normal(jax.random.fold_in(_rk, 11), (2, 16, 128), jnp.float32)
        _ctx_1024c = jax.random.dirichlet(jax.random.fold_in(_rk, 511), 0.3 * jnp.ones((16,), jnp.float32), (2, 77))
        _ctx_1024t = jnp.einsum('bsk,bkd->bsd', _ctx_1024c, _ctx_1024P)
        _ctx_1024t = _ctx_1024t * jax.lax.rsqrt(jnp.mean(jnp.square(_ctx_1024t)) + 1e-12) * 0.953939
        ctx_1024 = 4.13588e-05 + 0.999923 * (_ctx_1024t + 0.3 * jax.random.normal(jax.random.fold_in(_rk, 611), (2, 77, 128), jnp.float32))
        _validS = jnp.arange(512)[None, :] < _lenS[:, None]
        _validS2 = jnp.arange(77)[None, :] < _lenS2[:, None]
        _causal = jnp.tril(jnp.ones((512, 512), dtype=bool))
        mask_Bx1x1xS2_ff0 = jnp.where(jnp.ones((2, 1, 1, 77), dtype=bool), 0.0, -1000000000.0).astype(jnp.float32)
        mask_BxS2_ik0 = jnp.where(jnp.broadcast_to(_validS2[:, :], (2, 77)), 0, 1).astype(jnp.int32)
        _g = jax.random.normal(jax.random.fold_in(_rk, 9001), (2, 4), jnp.float32)
        _g = jnp.sign(_g) * jnp.maximum(jnp.abs(_g), 1.0) + (_g == 0) * 1.0
        g_xattn = _g[0]
        g_ffn = _g[1]
        return (x, ctx_1024, mask_Bx1x1xS2_ff0, mask_BxS2_ik0, g_xattn, g_ffn)
    x, ctx_1024, mask_Bx1x1xS2_ff0, mask_BxS2_ik0, g_xattn, g_ffn = _rec_inputs()

    def _L0_xattn_setup():
        import jax, jax.numpy as jnp
        import numpy as np
        DIM = 128
        NUM_HEADS = 16
        DIM_HEAD = 64
        INNER = NUM_HEADS * DIM_HEAD
        SCALE = DIM_HEAD ** (-0.5)

        def _layernorm(x, gamma, beta, eps=1e-05):
            mu = jnp.mean(x, axis=-1, keepdims=True)
            var = jnp.mean(jnp.square(x - mu), axis=-1, keepdims=True)
            return (x - mu) * jax.lax.rsqrt(var + eps) * gamma + beta
        key = jax.random.key(seed)
        ks = jax.random.split(key, 8)
        B, SQ, SK = (2, 256, 512)
        x = jax.random.normal(ks[0], (B, SQ, DIM), dtype=jnp.float32)
        context = jax.random.normal(ks[1], (B, SK, DIM), dtype=jnp.float32)
        ln_gamma = jnp.ones((DIM,), jnp.float32)
        ln_beta = jnp.zeros((DIM,), jnp.float32)
        w_q = jax.random.normal(ks[2], (DIM, INNER), dtype=jnp.float32) / np.sqrt(DIM)
        w_kv = jax.random.normal(ks[3], (DIM, 2 * INNER), dtype=jnp.float32) / np.sqrt(DIM)
        w_out = jax.random.normal(ks[4], (INNER, DIM), dtype=jnp.float32) / np.sqrt(INNER)
        b_out = jnp.zeros((DIM,), jnp.float32)
        gate = jnp.array([0.5], jnp.float32)
        return {'x': x, 'context': context, 'ln_gamma': ln_gamma, 'ln_beta': ln_beta, 'w_q': w_q, 'w_kv': w_kv, 'w_out': w_out, 'b_out': b_out, 'gate': gate}
    _L0_xattn_all = _L0_xattn_setup()
    _L0_xattn_in = {k: v for k, v in _L0_xattn_all.items() if k in ('ln_gamma', 'ln_beta', 'w_q', 'w_kv', 'w_out', 'b_out', 'gate')}
    del _L0_xattn_all

    def _L0_ffn_setup():
        import jax, jax.numpy as jnp
        import numpy as np
        FP8_MAX = 448.0
        SCALE = 1.0
        _FP8_DTYPE = getattr(jnp, 'float8_e4m3fn', jnp.float16)

        def quantize_e4m3(t, scale):
            return jnp.clip(t / scale, -FP8_MAX, FP8_MAX).astype(_FP8_DTYPE)
        key = jax.random.key(seed)
        kx, kw = jax.random.split(key)
        B, N, C, F = (8, 512, 128, 128)
        x = jax.random.normal(kx, (B, N, C), dtype=jnp.float32)
        weight = jax.random.normal(kw, (F, C), dtype=jnp.float32) * 0.02
        bias = jnp.zeros((F,), dtype=jnp.float32)
        return {'x': x, 'weight': weight, 'bias': bias}
    _L0_ffn_all = _L0_ffn_setup()
    _L0_ffn_in = {k: v for k, v in _L0_ffn_all.items() if k in ('weight', 'bias')}
    del _L0_ffn_all

    def _L1_xattn_setup():
        import jax, jax.numpy as jnp
        import numpy as np
        B, T, D, H = (2, 256, 128, 16)
        DH = D // H

        def _heads(x):
            b, t, _ = x.shape
            return x.reshape(b, t, H, DH).transpose(0, 2, 1, 3)
        key = jax.random.key(seed)
        ks = jax.random.split(key, 8)
        s = 0.02
        return {'query_states': jax.random.normal(ks[0], (B, T, D), jnp.float32), 'key_states': jax.random.normal(ks[1], (B, T, D), jnp.float32), 'attention_mask': jnp.zeros((B, 1, 1, T), jnp.float32), 'Wq': jax.random.normal(ks[2], (D, D), jnp.float32) * s, 'bq': jnp.zeros((D,), jnp.float32), 'Wk': jax.random.normal(ks[3], (D, D), jnp.float32) * s, 'bk': jnp.zeros((D,), jnp.float32), 'Wv': jax.random.normal(ks[4], (D, D), jnp.float32) * s, 'bv': jnp.zeros((D,), jnp.float32), 'mask_future': 0}
    _L1_xattn_all = _L1_xattn_setup()
    _L1_xattn_in = {k: v for k, v in _L1_xattn_all.items() if k in ('Wq', 'bq', 'Wk', 'bk', 'Wv', 'bv')}
    del _L1_xattn_all

    def _L1_ffn_setup():
        import jax, jax.numpy as jnp
        import numpy as np
        SQRT_2_PI = 0.7978845608028654
        GELU_COEF = 0.044715
        LN_EPS = 1e-06
        TOP_K = 2

        def gelu_kernel(x):
            inner = SQRT_2_PI * (x + GELU_COEF * x ** 3)
            return 0.5 * x * (1.0 + jnp.tanh(inner))
        key = jax.random.key(seed)
        ks = jax.random.split(key, 8)
        B, S, D, F, E = (2, 256, 128, 512, 8)
        s = lambda d: 1.0 / np.sqrt(d)
        return {'x': jax.random.normal(ks[0], (B, S, D), jnp.float32), 'Wr1': jax.random.normal(ks[1], (D, D // 2), jnp.float32) * s(D), 'br1': jnp.zeros((D // 2,), jnp.float32), 'ln_scale': jnp.ones((D // 2,), jnp.float32), 'ln_bias': jnp.zeros((D // 2,), jnp.float32), 'Wr2': jax.random.normal(ks[2], (D // 2, E), jnp.float32) * s(D // 2), 'br2': jnp.zeros((E,), jnp.float32), 'W1': jax.random.normal(ks[3], (E, D, 2 * F), jnp.float32) * s(D), 'b1': jnp.zeros((E, 2 * F), jnp.float32), 'W2': jax.random.normal(ks[4], (E, F, D), jnp.float32) * s(F), 'b2': jnp.zeros((E, D), jnp.float32)}
    _L1_ffn_all = _L1_ffn_setup()
    _L1_ffn_in = {k: v for k, v in _L1_ffn_all.items() if k in ('Wr1', 'br1', 'ln_scale', 'ln_bias', 'Wr2', 'br2', 'W1', 'b1', 'W2', 'b2')}
    del _L1_ffn_all

    def _L2_xattn_setup():
        import jax, jax.numpy as jnp
        import numpy as np
        H = 16
        D_MODEL = 128
        D_K = D_MODEL // H
        key = jax.random.key(seed)
        ks = jax.random.split(key, 11)
        B, S = (2, 256)
        scale = 1.0 / np.sqrt(D_MODEL)
        inp = {'query': jax.random.normal(ks[0], (B, S, D_MODEL), dtype=jnp.float32), 'key': jax.random.normal(ks[1], (B, S, D_MODEL), dtype=jnp.float32), 'value': jax.random.normal(ks[2], (B, S, D_MODEL), dtype=jnp.float32), 'Wq': jax.random.normal(ks[3], (D_MODEL, D_MODEL), dtype=jnp.float32) * scale, 'bq': jnp.zeros((D_MODEL,), dtype=jnp.float32), 'Wk': jax.random.normal(ks[4], (D_MODEL, D_MODEL), dtype=jnp.float32) * scale, 'bk': jnp.zeros((D_MODEL,), dtype=jnp.float32), 'Wv': jax.random.normal(ks[5], (D_MODEL, D_MODEL), dtype=jnp.float32) * scale, 'bv': jnp.zeros((D_MODEL,), dtype=jnp.float32), 'Wo': jax.random.normal(ks[6], (D_MODEL, D_MODEL), dtype=jnp.float32) * scale, 'bo': jnp.zeros((D_MODEL,), dtype=jnp.float32)}
        return inp
    _L2_xattn_all = _L2_xattn_setup()
    _L2_xattn_in = {k: v for k, v in _L2_xattn_all.items() if k in ('Wq', 'bq', 'Wk', 'bk', 'Wv', 'bv', 'Wo', 'bo')}
    del _L2_xattn_all

    def _L2_ffn_setup():
        import jax, jax.numpy as jnp
        import numpy as np
        FEATURES = 128
        D_IN = 128

        def fp8_gemm_optimized(x, input_scale, kernel, kernel_scale):
            s_in = input_scale[0]
            s_k = kernel_scale[0]
            x_q = (x.astype(jnp.float32) / s_in).astype(jnp.float8_e4m3fn)
            k_q = (kernel.astype(jnp.float32) / s_k).astype(jnp.float8_e4m3fn)
            y = jnp.dot(x_q.astype(jnp.float32), k_q.astype(jnp.float32), preferred_element_type=jnp.float32)
            return y * (s_in * s_k)
        key = jax.random.key(seed)
        kx, kk, kb = jax.random.split(key, 3)
        x = jax.random.normal(kx, (4, 1024, D_IN), dtype=jnp.float32)
        limit = np.sqrt(6.0 / (D_IN + FEATURES)).astype(np.float32)
        kernel = jax.random.uniform(kk, (D_IN, FEATURES), dtype=jnp.float32, minval=-limit, maxval=limit).astype(jnp.bfloat16)
        input_scale = jnp.ones((1,), dtype=jnp.float32)
        kernel_scale = jnp.ones((1,), dtype=jnp.float32)
        bias = jnp.zeros((FEATURES,), dtype=jnp.bfloat16)
        return {'x': x, 'kernel': kernel, 'input_scale': input_scale, 'kernel_scale': kernel_scale, 'bias': bias}
    _L2_ffn_all = _L2_ffn_setup()
    _L2_ffn_in = {k: v for k, v in _L2_ffn_all.items() if k in ('kernel', 'input_scale', 'kernel_scale', 'bias')}
    del _L2_ffn_all

    def _L3_xattn_setup():
        import jax, jax.numpy as jnp
        import numpy as np
        DIM = 128
        NUM_HEADS = 16
        HEAD_DIM = DIM // NUM_HEADS
        key = jax.random.key(seed)
        ks = jax.random.split(key, 8)
        B, Nq, Nkv = (2, 256, 256)
        s = 1.0 / np.sqrt(DIM)
        return {'feat1_query': jax.random.normal(ks[0], (B, Nq, DIM), dtype=jnp.float32), 'feat2_key_value': jax.random.normal(ks[1], (B, Nkv, DIM), dtype=jnp.float32), 'Wq': jax.random.normal(ks[2], (DIM, DIM), dtype=jnp.float32) * s, 'Wk': jax.random.normal(ks[3], (DIM, DIM), dtype=jnp.float32) * s, 'Wv': jax.random.normal(ks[4], (DIM, DIM), dtype=jnp.float32) * s, 'Wo': jax.random.normal(ks[5], (DIM, DIM), dtype=jnp.float32) * s, 'bo': jnp.zeros((DIM,), dtype=jnp.float32), 'mask': jax.random.randint(ks[6], (B, Nkv), 0, 2, dtype=jnp.int32)}
    _L3_xattn_all = _L3_xattn_setup()
    _L3_xattn_in = {k: v for k, v in _L3_xattn_all.items() if k in ('Wq', 'Wk', 'Wv', 'Wo', 'bo')}
    del _L3_xattn_all

    def _L3_ffn_setup():
        import jax, jax.numpy as jnp
        import numpy as np
        LN_EPS = 1e-12
        key = jax.random.key(seed)
        ks = jax.random.split(key, 8)
        B, S, H, I, E = (4, 256, 128, 512, 8)
        sH = 1.0 / np.sqrt(H)
        sI = 1.0 / np.sqrt(I)
        return {'hidden_states': jax.random.normal(ks[0], (B, S, H), dtype=jnp.float32), 'Wr': jax.random.uniform(ks[1], (E, H), jnp.float32, -sH, sH), 'W1': jax.random.uniform(ks[2], (E, H, I), jnp.float32, -sH, sH), 'b1': jax.random.uniform(ks[3], (E, I), jnp.float32, -sH, sH), 'Wo': jax.random.uniform(ks[4], (I, H), jnp.float32, -sI, sI), 'bo': jax.random.uniform(ks[5], (H,), jnp.float32, -sI, sI), 'gamma': jnp.ones((H,), jnp.float32), 'beta': jnp.zeros((H,), jnp.float32)}
    _L3_ffn_all = _L3_ffn_setup()
    _L3_ffn_in = {k: v for k, v in _L3_ffn_all.items() if k in ('Wr', 'W1', 'b1', 'Wo', 'bo', 'gamma', 'beta')}
    del _L3_ffn_all
    return {'x': x, 'ctx_1024': ctx_1024, 'mask_Bx1x1xS2_ff0': mask_Bx1x1xS2_ff0, 'mask_BxS2_ik0': mask_BxS2_ik0, 'g_xattn': g_xattn, 'g_ffn': g_ffn, 'L0_xattn_ln_gamma': _L0_xattn_in['ln_gamma'], 'L0_xattn_ln_beta': _L0_xattn_in['ln_beta'], 'L0_xattn_w_q': _L0_xattn_in['w_q'], 'L0_xattn_w_kv': _L0_xattn_in['w_kv'], 'L0_xattn_w_out': _L0_xattn_in['w_out'], 'L0_xattn_b_out': _L0_xattn_in['b_out'], 'L0_xattn_gate': _L0_xattn_in['gate'], 'L0_ffn_weight': _L0_ffn_in['weight'], 'L0_ffn_bias': _L0_ffn_in['bias'], 'L1_xattn_Wq': _L1_xattn_in['Wq'], 'L1_xattn_bq': _L1_xattn_in['bq'], 'L1_xattn_Wk': _L1_xattn_in['Wk'], 'L1_xattn_bk': _L1_xattn_in['bk'], 'L1_xattn_Wv': _L1_xattn_in['Wv'], 'L1_xattn_bv': _L1_xattn_in['bv'], 'L1_ffn_Wr1': _L1_ffn_in['Wr1'], 'L1_ffn_br1': _L1_ffn_in['br1'], 'L1_ffn_ln_scale': _L1_ffn_in['ln_scale'], 'L1_ffn_ln_bias': _L1_ffn_in['ln_bias'], 'L1_ffn_Wr2': _L1_ffn_in['Wr2'], 'L1_ffn_br2': _L1_ffn_in['br2'], 'L1_ffn_W1': _L1_ffn_in['W1'], 'L1_ffn_b1': _L1_ffn_in['b1'], 'L1_ffn_W2': _L1_ffn_in['W2'], 'L1_ffn_b2': _L1_ffn_in['b2'], 'L2_xattn_Wq': _L2_xattn_in['Wq'], 'L2_xattn_bq': _L2_xattn_in['bq'], 'L2_xattn_Wk': _L2_xattn_in['Wk'], 'L2_xattn_bk': _L2_xattn_in['bk'], 'L2_xattn_Wv': _L2_xattn_in['Wv'], 'L2_xattn_bv': _L2_xattn_in['bv'], 'L2_xattn_Wo': _L2_xattn_in['Wo'], 'L2_xattn_bo': _L2_xattn_in['bo'], 'L2_ffn_kernel': _L2_ffn_in['kernel'], 'L2_ffn_input_scale': _L2_ffn_in['input_scale'], 'L2_ffn_kernel_scale': _L2_ffn_in['kernel_scale'], 'L2_ffn_bias': _L2_ffn_in['bias'], 'L3_xattn_Wq': _L3_xattn_in['Wq'], 'L3_xattn_Wk': _L3_xattn_in['Wk'], 'L3_xattn_Wv': _L3_xattn_in['Wv'], 'L3_xattn_Wo': _L3_xattn_in['Wo'], 'L3_xattn_bo': _L3_xattn_in['bo'], 'L3_ffn_Wr': _L3_ffn_in['Wr'], 'L3_ffn_W1': _L3_ffn_in['W1'], 'L3_ffn_b1': _L3_ffn_in['b1'], 'L3_ffn_Wo': _L3_ffn_in['Wo'], 'L3_ffn_bo': _L3_ffn_in['bo'], 'L3_ffn_gamma': _L3_ffn_in['gamma'], 'L3_ffn_beta': _L3_ffn_in['beta']}

def reference(x, ctx_1024, mask_Bx1x1xS2_ff0, mask_BxS2_ik0, g_xattn, g_ffn, L0_xattn_ln_gamma, L0_xattn_ln_beta, L0_xattn_w_q, L0_xattn_w_kv, L0_xattn_w_out, L0_xattn_b_out, L0_xattn_gate, L0_ffn_weight, L0_ffn_bias, L1_xattn_Wq, L1_xattn_bq, L1_xattn_Wk, L1_xattn_bk, L1_xattn_Wv, L1_xattn_bv, L1_ffn_Wr1, L1_ffn_br1, L1_ffn_ln_scale, L1_ffn_ln_bias, L1_ffn_Wr2, L1_ffn_br2, L1_ffn_W1, L1_ffn_b1, L1_ffn_W2, L1_ffn_b2, L2_xattn_Wq, L2_xattn_bq, L2_xattn_Wk, L2_xattn_bk, L2_xattn_Wv, L2_xattn_bv, L2_xattn_Wo, L2_xattn_bo, L2_ffn_kernel, L2_ffn_input_scale, L2_ffn_kernel_scale, L2_ffn_bias, L3_xattn_Wq, L3_xattn_Wk, L3_xattn_Wv, L3_xattn_Wo, L3_xattn_bo, L3_ffn_Wr, L3_ffn_W1, L3_ffn_b1, L3_ffn_Wo, L3_ffn_bo, L3_ffn_gamma, L3_ffn_beta):
    import jax
    import jax.numpy as jnp

    def _L0_xattn_ref(x, context, ln_gamma, ln_beta, w_q, w_kv, w_out, b_out, gate):
        import jax, jax.numpy as jnp
        import numpy as np
        DIM = 128
        NUM_HEADS = 16
        DIM_HEAD = 64
        INNER = NUM_HEADS * DIM_HEAD
        SCALE = DIM_HEAD ** (-0.5)

        def _layernorm(x, gamma, beta, eps=1e-05):
            mu = jnp.mean(x, axis=-1, keepdims=True)
            var = jnp.mean(jnp.square(x - mu), axis=-1, keepdims=True)
            return (x - mu) * jax.lax.rsqrt(var + eps) * gamma + beta
        B, SQ, _ = x.shape
        SK = context.shape[1]
        xn = _layernorm(x, ln_gamma, ln_beta)
        q = (xn @ w_q).reshape(B, SQ, NUM_HEADS, DIM_HEAD)
        kv = context @ w_kv
        k, v = jnp.split(kv, 2, axis=-1)
        k = k.reshape(B, SK, NUM_HEADS, DIM_HEAD)
        v = v.reshape(B, SK, NUM_HEADS, DIM_HEAD)
        scores = jnp.einsum('bqhd,bkhd->bhqk', q * SCALE, k)
        attn = jax.nn.softmax(scores, axis=-1)
        out = jnp.einsum('bhqk,bkhd->bqhd', attn, v).reshape(B, SQ, INNER)
        out = out @ w_out + b_out
        return out * jnp.tanh(gate[0])

    def _L0_ffn_ref(x, weight, bias):
        import jax, jax.numpy as jnp
        import numpy as np
        FP8_MAX = 448.0
        SCALE = 1.0
        _FP8_DTYPE = getattr(jnp, 'float8_e4m3fn', jnp.float16)

        def quantize_e4m3(t, scale):
            return jnp.clip(t / scale, -FP8_MAX, FP8_MAX).astype(_FP8_DTYPE)
        B, N, C = x.shape
        x2d = x.reshape(B * N, C)
        x_mat = quantize_e4m3(x2d, SCALE).astype(jnp.float16)
        w_mat = quantize_e4m3(weight, SCALE).astype(jnp.float16)
        out2d = (x_mat @ w_mat.T).astype(jnp.float32) * (SCALE * SCALE)
        out2d = out2d + bias
        return out2d.reshape(B, N, -1)

    def _L1_xattn_ref(query_states, key_states, attention_mask, Wq, bq, Wk, bk, Wv, bv, mask_future):
        import jax, jax.numpy as jnp
        import numpy as np
        B, T, D, H = (2, 256, 128, 16)
        DH = D // H

        def _heads(x):
            b, t, _ = x.shape
            return x.reshape(b, t, H, DH).transpose(0, 2, 1, 3)
        q = _heads(query_states @ Wq + bq)
        k = _heads(key_states @ Wk + bk)
        v = _heads(key_states @ Wv + bv)
        scale = 1.0 / jnp.sqrt(jnp.asarray(DH, jnp.float32))
        scores = jnp.einsum('bhqd,bhkd->bhqk', q, k) * scale + attention_mask
        if mask_future:
            t = scores.shape[-1]
            triu = jnp.triu(jnp.ones((t, t), bool))
            scores = jnp.where(triu, -jnp.inf, scores)
        probs = jax.nn.softmax(scores, axis=-1)
        ctx = jnp.einsum('bhqk,bhkd->bhqd', probs, v)
        b, _, t, _ = ctx.shape
        return ctx.transpose(0, 2, 1, 3).reshape(b, t, H * DH)

    def _L1_ffn_ref(x, Wr1, br1, ln_scale, ln_bias, Wr2, br2, W1, b1, W2, b2):
        import jax, jax.numpy as jnp
        import numpy as np
        SQRT_2_PI = 0.7978845608028654
        GELU_COEF = 0.044715
        LN_EPS = 1e-06
        TOP_K = 2

        def gelu_kernel(x):
            inner = SQRT_2_PI * (x + GELU_COEF * x ** 3)
            return 0.5 * x * (1.0 + jnp.tanh(inner))
        E = W1.shape[0]
        h = jnp.einsum('bsd,dk->bsk', x, Wr1) + br1
        mu = jnp.mean(h, axis=-1, keepdims=True)
        var = jnp.mean((h - mu) ** 2, axis=-1, keepdims=True)
        h = (h - mu) * jax.lax.rsqrt(var + LN_EPS) * ln_scale + ln_bias
        h = gelu_kernel(h)
        router_logits = jnp.einsum('bsk,ke->bse', h, Wr2) + br2
        routing_probs = jax.nn.softmax(router_logits, axis=-1)
        top_k_probs, top_k_indices = jax.lax.top_k(routing_probs, TOP_K)
        top_k_probs = top_k_probs / jnp.sum(top_k_probs, axis=-1, keepdims=True)
        expert_mask = jnp.sum(jax.nn.one_hot(top_k_indices, E, dtype=x.dtype) * top_k_probs[..., None], axis=-2)
        output = jnp.zeros_like(x)
        for e in range(E):
            x12 = jnp.einsum('bsd,df->bsf', x, W1[e]) + b1[e]
            x1, x2 = jnp.split(x12, 2, axis=-1)
            g = x1 * gelu_kernel(x2)
            y = jnp.einsum('bsf,fd->bsd', g, W2[e]) + b2[e]
            output = output + y * expert_mask[:, :, e][:, :, None]
        return output

    def _L2_xattn_ref(query, key, value, Wq, bq, Wk, bk, Wv, bv, Wo, bo):
        import jax, jax.numpy as jnp
        import numpy as np
        H = 16
        D_MODEL = 128
        D_K = D_MODEL // H
        B, S, _ = query.shape

        def proj(x, W, b):
            y = jnp.einsum('bsd,ed->bse', x, W) + b
            return y.reshape(B, -1, H, D_K).transpose(0, 2, 1, 3)
        q = proj(query, Wq, bq)
        k = proj(key, Wk, bk)
        v = proj(value, Wv, bv)
        scores = jnp.einsum('bhqd,bhkd->bhqk', q, k) / jnp.sqrt(jnp.float32(D_K))
        p = jax.nn.softmax(scores, axis=-1)
        ctx = jnp.einsum('bhqk,bhkd->bhqd', p, v)
        ctx = ctx.transpose(0, 2, 1, 3).reshape(B, S, H * D_K)
        out = jnp.einsum('bsd,ed->bse', ctx, Wo) + bo
        return out

    def _L2_ffn_ref(x, kernel, input_scale, kernel_scale, bias):
        import jax, jax.numpy as jnp
        import numpy as np
        FEATURES = 128
        D_IN = 128

        def fp8_gemm_optimized(x, input_scale, kernel, kernel_scale):
            s_in = input_scale[0]
            s_k = kernel_scale[0]
            x_q = (x.astype(jnp.float32) / s_in).astype(jnp.float8_e4m3fn)
            k_q = (kernel.astype(jnp.float32) / s_k).astype(jnp.float8_e4m3fn)
            y = jnp.dot(x_q.astype(jnp.float32), k_q.astype(jnp.float32), preferred_element_type=jnp.float32)
            return y * (s_in * s_k)
        dtype = jnp.bfloat16
        x = x.astype(dtype)
        orig_shape = x.shape
        x2 = x.reshape(-1, x.shape[-1])
        y = fp8_gemm_optimized(x2, input_scale, kernel, kernel_scale)
        y = y.astype(dtype) + bias
        return y.reshape(orig_shape[:-1] + (FEATURES,))

    def _L3_xattn_ref(feat1_query, feat2_key_value, Wq, Wk, Wv, Wo, bo, mask):
        import jax, jax.numpy as jnp
        import numpy as np
        DIM = 128
        NUM_HEADS = 16
        HEAD_DIM = DIM // NUM_HEADS
        B, Nq, C = feat1_query.shape
        Nkv = feat2_key_value.shape[1]
        H, Dh = (NUM_HEADS, HEAD_DIM)
        Q = (feat1_query @ Wq.T).reshape(B, Nq, H, Dh).transpose(0, 2, 1, 3)
        K = (feat2_key_value @ Wk.T).reshape(B, Nkv, H, Dh).transpose(0, 2, 1, 3)
        V = (feat2_key_value @ Wv.T).reshape(B, Nkv, H, Dh).transpose(0, 2, 1, 3)
        dots = jnp.einsum('bhqd,bhkd->bhqk', Q, K) / jnp.sqrt(jnp.float32(Dh))
        dots = jnp.where(mask[:, None, None, :] == 0, jnp.float32(-1000000000.0), dots)
        attn = jax.nn.softmax(dots, axis=-1)
        out = jnp.einsum('bhqk,bhkd->bhqd', attn, V)
        out = out.transpose(0, 2, 1, 3).reshape(B, Nq, C)
        return out @ Wo.T + bo

    def _L3_ffn_ref(hidden_states, Wr, W1, b1, Wo, bo, gamma, beta):
        import jax, jax.numpy as jnp
        import numpy as np
        LN_EPS = 1e-12
        B, S, H = hidden_states.shape
        E = Wr.shape[0]
        x = hidden_states.reshape(-1, H)
        router_logits = x @ Wr.T
        expert_idx = jnp.argmax(jax.nn.softmax(router_logits, axis=-1), axis=-1)
        inter = jnp.zeros((x.shape[0], W1.shape[2]), dtype=x.dtype)
        for e in range(E):
            mask = (expert_idx == e)[:, None].astype(x.dtype)
            inter = inter + mask * jax.nn.gelu(x @ W1[e] + b1[e], approximate=False)
        y = inter @ Wo + bo + x
        mu = jnp.mean(y, axis=-1, keepdims=True)
        var = jnp.mean(jnp.square(y - mu), axis=-1, keepdims=True)
        out = (y - mu) * jax.lax.rsqrt(var + LN_EPS) * gamma + beta
        return out.reshape(B, S, H)
    x = x + jnp.tanh(g_xattn[0]) * _L0_xattn_ref(_layernorm(x, axis=-1), ctx_1024, L0_xattn_ln_gamma, L0_xattn_ln_beta, L0_xattn_w_q, L0_xattn_w_kv, L0_xattn_w_out, L0_xattn_b_out, L0_xattn_gate)
    x = x + jnp.tanh(g_ffn[0]) * _L0_ffn_ref(_layernorm(x, axis=-1), L0_ffn_weight, L0_ffn_bias)
    x = x + jnp.tanh(g_xattn[1]) * _L1_xattn_ref(_layernorm(x, axis=-1), ctx_1024, mask_Bx1x1xS2_ff0, L1_xattn_Wq, L1_xattn_bq, L1_xattn_Wk, L1_xattn_bk, L1_xattn_Wv, L1_xattn_bv, 0)
    x = x + jnp.tanh(g_ffn[1]) * _L1_ffn_ref(_layernorm(x, axis=-1), L1_ffn_Wr1, L1_ffn_br1, L1_ffn_ln_scale, L1_ffn_ln_bias, L1_ffn_Wr2, L1_ffn_br2, L1_ffn_W1, L1_ffn_b1, L1_ffn_W2, L1_ffn_b2)
    x = x + jnp.tanh(g_xattn[2]) * _L2_xattn_ref(_layernorm(x, axis=-1), ctx_1024, ctx_1024, L2_xattn_Wq, L2_xattn_bq, L2_xattn_Wk, L2_xattn_bk, L2_xattn_Wv, L2_xattn_bv, L2_xattn_Wo, L2_xattn_bo)
    x = x + jnp.tanh(g_ffn[2]) * _L2_ffn_ref(_layernorm(x, axis=-1), L2_ffn_kernel, L2_ffn_input_scale, L2_ffn_kernel_scale, L2_ffn_bias)
    x = x + jnp.tanh(g_xattn[3]) * _L3_xattn_ref(_layernorm(x, axis=-1), ctx_1024, L3_xattn_Wq, L3_xattn_Wk, L3_xattn_Wv, L3_xattn_Wo, L3_xattn_bo, mask_BxS2_ik0)
    x = x + jnp.tanh(g_ffn[3]) * _L3_ffn_ref(_layernorm(x, axis=-1), L3_ffn_Wr, L3_ffn_W1, L3_ffn_b1, L3_ffn_Wo, L3_ffn_bo, L3_ffn_gamma, L3_ffn_beta)
    return x

_drawn_inputs = setup_inputs


def setup_inputs(seed=0):
    import zlib

    import numpy as np

    out = dict(_drawn_inputs(seed))
    spreads = {'L0_xattn_ln_gamma': (1.0, 0.2),
     'L0_xattn_ln_beta': (0.0, 0.1),
     'L0_xattn_b_out': (0.0, 0.1),
     'L0_ffn_bias': (0.0, 0.1),
     'L1_xattn_bq': (0.0, 0.486),
     'L1_xattn_bk': (0.0, 0.8),
     'L1_xattn_bv': (0.0, 0.1),
     'L1_ffn_br1': (0.0, 0.1),
     'L1_ffn_ln_scale': (1.0, 0.2),
     'L1_ffn_ln_bias': (0.0, 0.1),
     'L1_ffn_br2': (0.0, 0.1),
     'L1_ffn_b1': (0.0, 0.1),
     'L1_ffn_b2': (0.0, 0.1),
     'L2_xattn_bq': (0.0, 0.329),
     'L2_xattn_bk': (0.0, 0.8),
     'L2_xattn_bv': (0.0, 0.1),
     'L2_xattn_bo': (0.0, 0.1),
     'L2_ffn_bias': (0.0, 0.1),
     'L3_xattn_bo': (0.0, 0.1),
     'L3_ffn_gamma': (1.0, 0.2),
     'L3_ffn_beta': (0.0, 0.1)}
    factors = {'L1_xattn_Wq': 3.417, 'L1_xattn_Wk': 3.093, 'L3_ffn_b1': 8.0, 'L3_ffn_bo': 5.309}
    for name, (base, spread) in spreads.items():
        noise = np.random.default_rng([zlib.crc32(name.encode()), seed]).standard_normal(out[name].shape)
        drawn = base * np.exp(spread * noise) if base else spread * noise
        out[name] = jnp.asarray(drawn.astype(out[name].dtype))
    for name, factor in factors.items():
        out[name] = (out[name] * factor).astype(out[name].dtype)
    return out
```

```python
from contextlib import ExitStack

import numpy as np

import concourse.bass as bass
from concourse import mybir

F32 = mybir.dt.float32
BF16 = mybir.dt.bfloat16
F16 = mybir.dt.float16
FP8 = mybir.dt.float8e4
I32 = mybir.dt.int32
ALU = mybir.AluOpType
ACT = mybir.ActivationFunctionType
AX = mybir.AxisListType

P = 128
B = 2
NT = 4
SQ = NT * P
SK = 77
H = 16
HK = H * SK
NL = 4
HEADS = [(0, 5), (5, 10), (10, 16)]
CH = [(c, min(P, HK - c)) for c in range(0, HK, P)]
GROUPS = [(0, 4), (4, 8), (8, 10)]
E = 8
F1 = 512
FT = F1 // P
SCALE0 = 64 ** -0.5
SCALE = 8 ** -0.5
MAGIC = 1.5 * 2.0 ** 20
OVER8 = 7.3e35

KV = {}
SQW = {}
COL = {}
ROW = {}


def _place(table, names):
    at = 0
    for name, width in names:
        table[name] = (at, at + width)
        at += width
    return at


KV_N = _place(KV, [("ctxT", B * SK), ("wk", 1024), ("wv", 1024), ("wqT", 1024), ("wout", 1024)])
SQW_N = _place(SQW, [("ident", P), ("w8T", P), ("wq1", P), ("wk1", P), ("wv1", P)]
               + [(f"w{n}{l}", P) for l in (2, 3) for n in "qkvo"] + [("wr1", 64), ("wr2", E), ("wrT3", E)])
COL_N = _place(COL, [(n, 1) for n in ("ln_g", "ln_b", "bo0", "bq1", "bk1", "bv1", "bq2", "bk2", "bv2", "bo2",
                                      "bo3", "fbo3")]
               + [("b2", E), ("b1", 2 * FT * E), ("headmask", H), ("third", 3)])
ROW_N = _place(ROW, [("fb0", P), ("br1", 64), ("lns", 64), ("lnb", 64), ("br2", E), ("gamma", P), ("beta", P),
                     ("gates", 9), ("s_in", 1), ("s_k", 1), ("mask1", B * SK), ("rank", E)])

ORDER = []


def _order():
    o = ORDER
    for s in (-1, 0):
        for b in range(B):
            o.append(("ln_stats", s, b))
        for b in range(B):
            o.append(("ln_apply", s, b))
    o.append(("kv0", 0))
    for j in range(8):
        if j + 1 < 8:
            o.append(("kv0", j + 1))
        o.append(("kp0", j))
    for b in range(B):
        o.append(("xt", 0, b))
    for b in range(B):
        for g in range(3):
            o.append(("vp", 0, b, g))

    def light(l):
        f = f"f{l}"
        return ([("ln_stats", 2 * l + 1, 0), ("ln_apply", 2 * l + 1, 0), ("xt", 2 * l + 1, 0)]
                + ([("quant", 0)] if l == 2 else []) + [(f, 0)],
                [("ln_stats", 2 * l + 1, 1), ("ln_apply", 2 * l + 1, 1), ("xt", 2 * l + 1, 1)]
                + ([("quant", 1)] if l == 2 else []) + [(f, 1)])

    def head(l, b):
        items = [("ln_stats", 2 * l, b), ("ln_apply", 2 * l, b), ("xt", 2 * l, b), ("q", l, b)]
        return items if l else []

    for l in range(NL):
        first = [0, 1][: B]
        tiles = [(b, i) for b in first for i in range(NT)]
        if l == 0:
            o += head(l, 0) + head(l, 1)
        for k, (b, i) in enumerate(tiles):
            o.append(("S", l, b, i))
            if k >= 1:
                o.append(("N", l, *tiles[k - 1]))
            if k >= 2:
                o.append(("T", l, *tiles[k - 2]))
                if tiles[k - 2][1] == NT - 1:
                    o.append(("PV", l, tiles[k - 2][0]))
                    o.append(("back", l, tiles[k - 2][0]))
        o.append(("N", l, *tiles[-1]))
        o.append(("T", l, *tiles[-2]))
        if l < NL - 1:
            o.append(("kvT", l + 1))
        if l in (0, 2):
            o += light(l)[0]
        else:
            s = 2 * l + 1
            o += [("ln_stats", s, 0), ("ln_apply", s, 0), ("xt", s, 0)]
            o += [("r1", 0)] if l == 1 else [("g1", 0)]
        o.append(("T", l, *tiles[-1]))
        o += [("PV", l, 1), ("back", l, 1)]
        if l in (0, 2):
            o += head(l + 1, 0) + light(l)[1]
            for b in range(B):
                for g in range(3):
                    o.append(("vp", l + 1, b, g))
            o += head(l + 1, 1)
        else:
            s = 2 * l + 1
            if l == 1:
                o += [("r2", 0), ("ln_stats", s, 1), ("ln_apply", s, 1), ("r3", 0), ("xt", s, 1), ("r1", 1), ("r4", 0)]
                for b in range(B):
                    for g in range(3):
                        o.append(("vp", l + 1, b, g))
                o += [("r2", 1), ("r3", 1), ("r4", 1)]
                o += [("moe1",)]
                o += [("back1", 0), ("back1", 1)] + head(2, 0) + head(2, 1)
            else:
                o += [("g2", 0), ("ln_stats", s, 1), ("ln_apply", s, 1), ("xt", s, 1), ("g1", 1)]
                o += [("moe3", 0), ("y3", 0), ("g2", 1), ("moe3", 1), ("z3", 0), ("y3", 1), ("z3", 1)]


_order()


def nth(*item):
    return [i for i in ORDER if i[0] == item[0]].index(item) + 1


def total(kind):
    return len([i for i in ORDER if i[0] == kind])


USES = []
for _i in ORDER:
    _k = _i[0]
    if _k in ("xt", "q", "PV", "r2", "r4", "f0", "f2", "y3"):
        USES.append((_i, "act"))
    elif _k in ("back", "r1", "r3", "g1", "back1", "z3", "kvT"):
        USES.append((_i, "dve"))
    elif _k == "g2":
        USES.append((_i, "act"))
    elif _k == "vp":
        USES.append((_i, "act"))
    elif _k == "kv0":
        USES.append((_i + ("k",), "act"))
        USES.append((_i + ("v",), "dve"))
    elif _k == "kp0":
        USES.append((_i + ("k",), "act"))
        USES.append((_i + ("v",), "dve"))
    elif _k == "moe1":
        for _e in range(E):
            for _b in range(B):
                USES.append((("bc1", _e, _b), "act"))
    elif _k == "moe3":
        for _e in range(E):
            USES.append((("bc3", _i[1], _e), "dve"))
USE = {u: (k, eng, [v[1] for v in USES[:k + 1]].count(eng)) for k, (u, eng) in enumerate(USES)}


def build(nc, x_in, kv_in, sqw_in, col_in, row_in, w1_in, w2_in, w3_in, wo3_in, b13_in, mask3_in, k8_in,
          fb2_in, esel_in, out):
    with ExitStack() as ctx:
        def sb(name, shape, dt=F32):
            return ctx.enter_context(nc.sbuf_tensor(name, shape, dt))

        def sem(name):
            return ctx.enter_context(nc.semaphore(name))

        x = sb("x", [P, B, NT, P])
        xn = sb("xn", [P, B, NT, P])
        xnT = sb("xnT", [P, B, SQ])
        qT = sb("qT", [P, B, SQ])
        oT = sb("oT", [P, B, SQ])
        Kp = sb("Kp", [P, 2, B, HK])
        Vp = sb("Vp", [P, 2, B, len(CH), P])
        probs = sb("probs", [P, 3, HK])
        PT = sb("PT", [P, len(CH), SQ])
        kv = sb("kv", [P, KV_N])
        sqw = sb("sqw", [P, SQW_N])
        col = sb("col", [P, COL_N])
        row = sb("row", [P, ROW_N])
        w1 = sb("w1", [P, E, 2 * F1])
        w2 = sb("w2", [P, E, FT, P])
        esel = sb("esel", [P, E, P], BF16)
        Vb = sb("Vb", [P, B, HK])
        kvs = sb("kvs", [P, 2, B * SK])
        ones3 = sb("ones3", [P, P], BF16)
        maskrow = sb("maskrow", [P, B, HK], BF16)
        mrow = sb("mrow", [P, 6, B * SK])
        mint = sb("mint", [P, B * SK], I32)
        keep3 = sb("keep3", [P, B * SK])
        w8 = sb("w8", [P, P], BF16)
        k8in = sb("k8in", [P, P], BF16)
        k8 = sb("k8", [P, P], BF16)
        fb2 = sb("fb2", [P, P], BF16)
        xq8 = sb("xq8", [P, B, SQ], FP8)
        xb = sb("xb", [P, B, SQ], BF16)
        y16 = sb("y16", [P, SQ], F16)
        y2 = y16[:, :].bitcast(BF16)
        selT = sb("selT", [P, B, SQ], BF16)
        b13s = sb("b13s", [P, F1], BF16)
        tg = sb("tg", [P, 10])
        st = sb("st", [P, B, NT, 6])
        mv = sb("mv", [P, B, NT, 2])
        ve = sb("ve", [P, B, NT])
        rstd = sb("rstd", [P, B, NT])
        mhalf = sb("mhalf", [P, NT])
        mx = sb("mx", [P, 3, H])
        den = sb("den", [P, 3, H])
        rden = sb("rden", [P, 3, H])
        sc = sb("sc", [P, 4])
        lg = sb("lg", [P, B, NT, E])
        oh = sb("oh", [P, 4, NT, E])
        s24 = sb("s24", [P, B, NT, 3, E])
        sbf = sb("sbf", [P, NT, E], BF16)
        m12 = sb("m12", [P, B, 8, NT])

        ffa = PT[:, :, :].rearrange("p c n -> p (c n)")
        gel = ffa[:, 0:2 * SQ].rearrange("p (r n) -> p r n", r=2)
        gg = ffa[:, 2 * SQ:4 * SQ].rearrange("p (r n) -> p r n", r=2)
        pbc = ffa[:, 4 * SQ:6 * SQ].rearrange("p (r n) -> p r n", r=2)
        ytmp = ffa[:, 6 * SQ:8 * SQ].rearrange("p (r n) -> p r n", r=2)
        acc = ffa[:, 8 * SQ:10 * SQ].rearrange("p (r n) -> p r n", r=2)
        inter = ffa[:, 0:FT * SQ].rearrange("p (f n) -> p f n", f=FT)
        xm = ffa[:, 4 * SQ:6 * SQ].rearrange("p (r n) -> p r n", r=2)
        yT3 = ffa[:, 6 * SQ:8 * SQ].rearrange("p (r n) -> p r n", r=2)
        zz = ffa[:, 8 * SQ:10 * SQ].rearrange("p (r i n) -> p r i n", r=2, i=NT)
        nbd = 2 * 2 * B * SK
        kbd = ffa[:, 0:nbd].rearrange("p (r h n) -> p r h n", r=2, h=2)
        vbd = ffa[:, nbd:2 * nbd].rearrange("p (r h n) -> p r h n", r=2, h=2)
        pr = probs[:, :, :].rearrange("p c n -> p (c n)")
        qt = [pr[:, k * SQ:(k + 1) * SQ] for k in range(4)]
        b13 = pr[:, 6 * SQ:7 * SQ]
        hT = ffa[0:64, 8 * SQ:10 * SQ].rearrange("p (r n) -> p r n", r=2)
        hr = pr[:, 4 * SQ:4 * SQ + B * NT * 64].rearrange("p (b i n) -> p b i n", b=B, i=NT)
        hg = pr[:, 5 * SQ:5 * SQ + B * NT * 64].rearrange("p (b i n) -> p b i n", b=B, i=NT)
        w3 = kv[:, 0:E * F1].rearrange("p (e f) -> p e f", e=E)
        wo3 = sb("wo3", [P, FT, P])

        SC = [ctx.enter_context(nc.psum_tensor(f"SC{i}", [P, 512], F32)) for i in range(4)]
        TB = [ctx.enter_context(nc.psum_tensor(f"TB{i}", [P, 512], F32)) for i in range(2)]
        MB = [ctx.enter_context(nc.psum_tensor(f"MB{i}", [P, 512], F32)) for i in range(2)]

        ld_x = sem("ld_x")
        ld_kv = sem("ld_kv")
        ld_sqw = sem("ld_sqw")
        ld_col = sem("ld_col")
        ld_row = sem("ld_row")
        ld_small = sem("ld_small")
        ld_w1 = sem("ld_w1")
        ld_w3 = sem("ld_w3")
        const_ready = sem("const_ready")
        misc_full = sem("misc_full")
        evac_act = sem("evac_act")
        evac_dve = sem("evac_dve")
        dve_chain = sem("dve_chain")
        act_chain = sem("act_chain")
        gates_ready = sem("gates_ready")
        gates_mul = sem("gates_mul")
        var_ready = sem("var_ready")
        rstd_ready = sem("rstd_ready")
        xn_ready = sem("xn_ready")
        x_new = sem("x_new")
        w8_ready = sem("w8_ready")
        mask_ready = sem("mask_ready")
        kbd_zero = sem("kbd_zero")
        blocks_ready = sem("blocks_ready")
        scores_full = sem("scores_full")
        scores_taken = sem("scores_taken")
        exp_ready = sem("exp_ready")
        rden_ready = sem("rden_ready")
        probs_ready = sem("probs_ready")
        pt_full = sem("pt_full")
        pt_copied = sem("pt_copied")
        quant_ready = sem("quant_ready")
        y_rounded = sem("y_rounded")
        h_ready = sem("h_ready")
        hg_ready = sem("hg_ready")
        gap_ready = sem("gap_ready")
        gap_exp = sem("gap_exp")
        sel_ready = sem("sel_ready")
        x12_full = sem("x12_full")
        gelu_ready = sem("gelu_ready")
        g_ready = sem("g_ready")
        y_step = sem("y_step")
        ytmp_ready = sem("ytmp_ready")
        acc_done = sem("acc_done")
        pre3_full = sem("pre3_full")
        inter_ready = sem("inter_ready")
        mm3 = sem("mm3")
        out_ready = sem("out_ready")
        stored = sem("stored")

        def kvc(name):
            return kv[:, KV[name][0]:KV[name][1]]

        def sq(name):
            return sqw[:, SQW[name][0]:SQW[name][1]]

        def colv(name, i=0):
            return col[:, COL[name][0] + i:COL[name][0] + i + 1]

        def rowv(name):
            return row[:, ROW[name][0]:ROW[name][1]]

        def over_tiles(ap, n):
            return ap.rearrange("p (a n) -> p a n", a=1).broadcast_to([P, NT, n])

        ident = sq("ident")
        def bank(item, c):
            return SC[(3 * (nth("S", *item) - 1) + c) % 4]

        def acquire(pe, key):
            k, _, _ = USE[key]
            if k >= 2:
                emptied(pe, USES[k - 2][0])
            return MB[k % 2]

        def emptied(eng, key):
            _, who, n = USE[key]
            eng.wait_ge(evac_act if who == "act" else evac_dve, n)

        def filled(eng, key):
            k, _, _ = USE[key]
            eng.wait_ge(misc_full, k + 1)
            return MB[k % 2]

        block = ctx.enter_context(nc.Block())

        @block.sync
        def _(sp):
            sp.dma_start(x[:, :, :, :], x_in).then_inc(ld_x, 16)
            sp.dma_start(kv[:, :], kv_in).then_inc(ld_kv, 16)
            sp.dma_start(w1[:, :, :], w1_in).then_inc(ld_w1, 16)
            sp.dma_start(w2[:, :, :, :], w2_in).then_inc(ld_w1, 16)
            sp.dma_start(wo3[:, :, :], wo3_in).then_inc(ld_w3, 16)
            emptied(sp, ("kp0", 7, "v"))
            emptied(sp, ("kvT", 3))
            sp.dma_start(w3[:, :, :], w3_in).then_inc(ld_w3, 16)
            for b in range(B):
                sp.wait_ge(out_ready, b + 1)
                sp.dma_start(out[:, b], x[:, b, :, :]).then_inc(stored, 16)
            sp.wait_ge(stored, 16 * B)

        @block.gpsimd
        def _(pool):
            pool.memset(mhalf[:, :], -0.5)
            pool.memset(kbd[:, :, :, :], 0.0)
            pool.memset(vbd[:, :, :, :], 0.0).then_inc(kbd_zero, 1)
            pool.memset(maskrow[:, :, :], 0.0)
            pool.memset(selT[:, :, :], 0.0)
            pool.memset(ones3[:, :], 0.0).then_inc(const_ready, 1)
            pool.wait_ge(const_ready, 1)
            for r in range(3):
                last = pool.memset(ones3[32 * r:32 * r + 1, :], 1.0)
            last.then_inc(const_ready, 1)
            pool.wait_ge(const_ready, 2)
            stats = 0
            for item in ORDER:
                kind = item[0]
                if kind in ("ln_stats", "r1", "z3"):
                    b = item[-1]
                    stats += 1
                    pool.wait_ge(var_ready, stats)
                    pool.tensor_tensor(rstd[:, b, :], ve[:, b, :], mhalf[:, :], ALU.pow).then_inc(rstd_ready, 1)
                elif kind == "N":
                    k = nth(*item) - 1
                    pool.wait_ge(rden_ready, k + 1)
                    pv = probs[:, k % 3, :].rearrange("p (h k) -> p h k", h=H)
                    pool.tensor_tensor(pv, pv, rden[:, k % 3, :].rearrange("p (h a) -> p h a", a=1)
                                       .broadcast_to([P, H, SK]), ALU.mult).then_inc(probs_ready, 1)
                elif kind == "kvT":
                    l = item[1]
                    emptied(pool, item)
                    if l >= 2:
                        pool.wait_ge(scores_full, 3 * nth("S", l - 2, 1, 3))
                        emptied(pool, ("vp", l - 1, 1, 2))
                    else:
                        emptied(pool, ("vp", 0, 1, 2))
                    for which, dst in ((0, Kp[:, l % 2]), (1, Vb)):
                        for b in range(B):
                            last = pool.tensor_tensor(
                                dst[:, b, :].rearrange("p (h k) -> p h k", h=H),
                                kvs[:, which, b * SK:(b + 1) * SK].rearrange("p (a k) -> p a k", a=1)
                                .broadcast_to([P, H, SK]),
                                col[:, COL["headmask"][0]:COL["headmask"][1]].rearrange("p (h a) -> p h a", a=1)
                                .broadcast_to([P, H, SK]), ALU.mult)
                    last.then_inc(blocks_ready, 1)
                elif kind == "moe1":
                    for b in range(B):
                        pool.wait_ge(ytmp_ready, b + 1)
                        pool.tensor_copy(acc[:, b, :], ytmp[:, b, :]).then_inc(acc_done, 1)
                    with pool.Fori(1, E) as e:
                        for b in range(B):
                            pool.wait_ge(ytmp_ready, 2 * e + b + 1)
                            pool.wait_ge(acc_done, 2 * e + b - 1)
                            pool.tensor_tensor(acc[:, b, :], acc[:, b, :], ytmp[:, b, :],
                                               ALU.add).then_inc(acc_done, 1)

        @block.scalar
        def _(act):
            act.dma_start(sqw[:, :], sqw_in).then_inc(ld_sqw, 16)
            act.dma_start(col[:, :], col_in).then_inc(ld_col, 16)
            act.dma_start(row[:, :], row_in.partition_broadcast(P)).then_inc(ld_row, 16)
            act.dma_start(mint[:, :], mask3_in.partition_broadcast(P)).then_inc(ld_small, 16)
            act.dma_start(k8in[:, :], k8_in).then_inc(ld_small, 16)
            act.dma_start(fb2[:, :], fb2_in.partition_broadcast(P)).then_inc(ld_small, 16)
            act.dma_start(esel[:, :, :], esel_in).then_inc(ld_small, 16)
            act.dma_start(b13[:, :], b13_in).then_inc(ld_small, 16)
            act.wait_ge(ld_row, 16)
            act.activation(tg[:, 0:9], rowv("gates"), ACT.Tanh).then_inc(gates_ready, 1)
            act.wait_ge(ld_col, 16)
            for item in ORDER:
                kind = item[0]
                if kind == "kv0":
                    j = item[1]
                    ps = filled(act, item + ("k",))
                    act.wait_ge(kbd_zero, 1)
                    if j >= 2:
                        filled(act, ("kp0", j - 2, "k"))
                    for hh in range(2):
                        last = act.activation(kbd[64 * hh:64 * hh + 64, j % 2, hh, :],
                                              ps[64 * hh:64 * hh + 64, 0:B * SK], ACT.Copy, scale=SCALE0)
                    last.then_inc(evac_act, 1)
                elif kind == "kp0":
                    j = item[1]
                    ps = filled(act, item + ("k",))
                    act.activation(
                        Kp[:, 0].rearrange("p b (h k) -> p h b k", h=H)[:, 2 * j:2 * j + 2],
                        ps[:, 0:4 * SK].rearrange("p (h b k) -> p h b k", h=2, b=B), ACT.Copy).then_inc(evac_act, 1)
                elif kind == "vp":
                    _, l, b, g = item
                    c0, c1 = GROUPS[g]
                    ps = filled(act, item)
                    if l >= 2:
                        filled(act, ("PV", l - 2, 1))
                    n = min(P, CH[c1 - 1][1])
                    if n == P:
                        act.activation(Vp[:, l % 2, b, c0:c1, :], ps[:, 0:P * (c1 - c0)]
                                       .rearrange("p (c n) -> p c n", n=P), ACT.Copy).then_inc(evac_act, 1)
                    else:
                        act.activation(Vp[:, l % 2, b, c0:c1 - 1, :], ps[:, 0:P * (c1 - c0 - 1)]
                                       .rearrange("p (c n) -> p c n", n=P), ACT.Copy)
                        act.activation(Vp[0:n, l % 2, b, c1 - 1, :], ps[0:n, P * (c1 - c0 - 1):P * (c1 - c0)],
                                       ACT.Copy).then_inc(evac_act, 1)
                elif kind == "xt":
                    _, s, b = item
                    ps = filled(act, item)
                    if s == 0:
                        act.activation(xnT[:, b, :], ps[:, :], ACT.Identity, bias=colv("ln_b"),
                                       scale=colv("ln_g")).then_inc(evac_act, 1)
                    elif s == 1:
                        act.activation(xq8[:, b, :], ps[:, :], ACT.Copy, saturate=False).then_inc(evac_act, 1)
                    elif s == 5:
                        act.activation(xb[:, b, :], ps[:, :], ACT.Copy).then_inc(evac_act, 1)
                    else:
                        act.activation(xnT[:, b, :], ps[:, :], ACT.Copy).then_inc(evac_act, 1)
                elif kind == "q":
                    _, l, b = item
                    ps = filled(act, item)
                    if l == 3:
                        act.activation(qT[:, b, :], ps[:, :], ACT.Copy).then_inc(evac_act, 1)
                    else:
                        act.activation(qT[:, b, :], ps[:, :], ACT.Identity,
                                       bias=colv(f"bq{l}")).then_inc(evac_act, 1)
                elif kind == "S":
                    k = nth(*item) - 1
                    act.wait_ge(scores_taken, 3 * k + 3)
                    act.activation(probs[:, k % 3, :], probs[:, k % 3, :], ACT.Exp).then_inc(exp_ready, 1)
                elif kind == "T":
                    _, l, b, i = item
                    k = nth(*item) - 1
                    for g, (c0, c1) in enumerate(GROUPS):
                        act.wait_ge(pt_full, 3 * k + g + 1)
                        ps = TB[(3 * k + g) % 2]
                        n = CH[c1 - 1][1]
                        full = c1 - c0 if n == P else c1 - c0 - 1
                        ins = act.activation(PT[:, c0:c0 + full, i * P:(i + 1) * P],
                                             ps[:, 0:P * full].rearrange("p (c n) -> p c n", n=P), ACT.Copy)
                        if n < P:
                            ins = act.activation(PT[0:n, c1 - 1, i * P:(i + 1) * P],
                                                 ps[0:n, P * full:P * full + P], ACT.Copy)
                        ins.then_inc(pt_copied, 1)
                elif kind == "PV":
                    _, l, b = item
                    ps = filled(act, item)
                    if l == 1:
                        act.activation(oT[:, b, :], ps[:, :], ACT.Copy).then_inc(evac_act, 1)
                    else:
                        act.activation(oT[:, b, :], ps[:, :], ACT.Identity, bias=colv(f"bo{l}")).then_inc(evac_act, 1)
                elif kind == "f0":
                    ps = filled(act, item)
                    if item[1]:
                        act.wait_ge(x_new, nth_x("f0", item[1] - 1))
                    act.activation(y16[:, :], ps[:, :], ACT.Copy).then_inc(evac_act, 1)
                elif kind == "f2":
                    ps = filled(act, item)
                    if item[1]:
                        act.wait_ge(x_new, nth_x("f2", item[1] - 1))
                    act.activation(y2, ps[:, :], ACT.Copy, scale=sc[:, 1:2]).then_inc(evac_act, 1)
                elif kind == "r1":
                    act.wait_ge(h_ready, item[1] + 1)
                    act.activation(hg[:, item[1]], hr[:, item[1]], ACT.Gelu_apprx_tanh).then_inc(hg_ready, 1)
                elif kind == "r2":
                    ps = filled(act, item)
                    act.activation(hT[:, item[1], :], ps[0:64, :], ACT.Copy).then_inc(evac_act, 1)
                elif kind == "r3":
                    b = item[1]
                    act.wait_ge(gap_ready, b + 1)
                    act.activation(m12[:, b, 3, :], m12[:, b, 2, :], ACT.Exp).then_inc(gap_exp, 1)
                elif kind in ("r4", "g2"):
                    ps = filled(act, item)
                    act.activation(selT[0:3 * E, item[1], :], ps[0:3 * E, :], ACT.Copy).then_inc(evac_act, 1)
                elif kind == "moe1":
                    base = USE[("bc1", 0, 0)][2] - 1
                    full = USE[("bc1", 0, 0)][0]

                    def step(e, s, first):
                        b, j = divmod(s, FT)
                        if j == 0:
                            act.wait_ge(misc_full, 2 * e + (full + b + 1))
                            if not first:
                                act.wait_ge(ytmp_ready, 2 * e + b - 1)
                            act.activation(pbc[:, b, :], MB[(full + b) % 2][:, :], ACT.Copy).then_inc(evac_act, 1)
                        act.wait_ge(x12_full, 8 * e + s + 1)
                        if not (first and s < 2):
                            act.wait_ge(g_ready, 8 * e + s - 1)
                        act.activation(gel[:, s % 2, :], SC[2 * (s % 2) + 1][:, :], ACT.Gelu_apprx_tanh,
                                       bias=col[:, bass.ds(e * 2 * FT + (COL["b1"][0] + FT + j), 1)]
                                       ).then_inc(gelu_ready, 1)

                    for s in range(2 * FT):
                        step(0, s, True)
                    for e in range(1, E):
                        for s in range(2 * FT):
                            step(e, s, False)
                elif kind == "moe3":
                    b = item[1]
                    for f in range(FT):
                        act.wait_ge(pre3_full, FT * b + f + 1)
                        if b and f == 0:
                            filled(act, ("y3", b - 1))
                        act.activation(inter[:, f, :], SC[f][:, :], ACT.Gelu).then_inc(inter_ready, 1)
                elif kind == "y3":
                    ps = filled(act, item)
                    act.activation(yT3[:, item[1], :], ps[:, :], ACT.Identity, bias=colv("fbo3")).then_inc(evac_act, 1)

        @block.vector
        def _(dve):
            count = [0]
            updates = [0]
            stats = [0]

            def link(ins):
                count[0] += 1
                ins.then_inc(dve_chain, 1)
                dve.wait_ge(dve_chain, count[0])

            def round8(dst, src, tmp):
                bits = tmp[0].bitcast(I32)
                link(dve.tensor_scalar(bits, src.bitcast(I32), 0x7F800000, None, ALU.bitwise_and))
                link(dve.tensor_scalar(tmp[0], tmp[0], 2.0 ** -6, MAGIC, ALU.max, ALU.mult))
                link(dve.tensor_tensor(tmp[1], src, tmp[0], ALU.add))
                link(dve.tensor_tensor(tmp[1], tmp[1], tmp[0], ALU.subtract))
                link(dve.tensor_scalar(tmp[2], tmp[1], OVER8, 0.0, ALU.mult, ALU.mult))
                return dve.tensor_tensor(dst, tmp[1], tmp[2], ALU.add)

            def batch_stats(src, b, eps):
                for i in range(NT):
                    ins = dve.bn_stats(st[:, b, i, :], src(i))
                link(ins)
                for i in range(NT):
                    ins = dve.bn_aggr(mv[:, b, i, :], st[:, b, i, :])
                link(ins)
                dve.tensor_scalar(ve[:, b, :], mv[:, b, :, 1], eps, None, ALU.add).then_inc(var_ready, 1)
                stats[0] += 1
                return stats[0]

            def normalise(dst, src, b, nth_stats):
                dve.wait_ge(rstd_ready, nth_stats)
                for i in range(NT):
                    ins = dve.tensor_scalar(dst(i), src(i), mv[:, b, i, 0:1], rstd[:, b, i:i + 1],
                                            ALU.subtract, ALU.mult)
                return ins

            def update(b, y, gate):
                updates[0] += 1
                return dve.scalar_tensor_tensor(out=x[:, b].rearrange("p i n -> p (i n)"), in0=y, scalar=gate,
                                                in1=x[:, b].rearrange("p i n -> p (i n)"),
                                                op0=ALU.mult, op1=ALU.add)

            dve.wait_ge(ld_row, 16)
            dve.wait_ge(gates_ready, 1)
            link(dve.tensor_tensor(tg[:, 9:10], tg[:, 0:1], tg[:, 8:9], ALU.mult))
            link(dve.reciprocal(sc[:, 0:1], rowv("s_in")))
            dve.tensor_tensor(sc[:, 1:2], rowv("s_in"), rowv("s_k"), ALU.mult)
            link(dve.reciprocal(sc[:, 2:3], rowv("s_k")))
            dve.wait_ge(ld_x, 16)
            pending = {}
            for item in ORDER:
                kind = item[0]
                if kind == "ln_stats":
                    _, s, b = item
                    src = xn if s == 0 else x
                    pending[b] = batch_stats(lambda i: src[:, b, i, :], b, 1e-5)
                elif kind == "ln_apply":
                    _, s, b = item
                    src = xn if s == 0 else x
                    if s > 0:
                        filled(dve, ("xt", s - 1, b))
                    ins = normalise(lambda i: xn[:, b, i, :], lambda i: src[:, b, i, :], b, pending[b])
                    if s == -1:
                        link(ins)
                    else:
                        ins.then_inc(xn_ready, 1)
                elif kind == "kv0":
                    j = item[1]
                    ps = filled(dve, item + ("v",))
                    dve.wait_ge(kbd_zero, 1)
                    if j >= 2:
                        filled(dve, ("kp0", j - 2, "v"))
                    for hh in range(2):
                        last = dve.tensor_copy(vbd[64 * hh:64 * hh + 64, j % 2, hh, :],
                                               ps[64 * hh:64 * hh + 64, 0:B * SK])
                    last.then_inc(evac_dve, 1)
                elif kind == "kp0":
                    j = item[1]
                    ps = filled(dve, item + ("v",))
                    dve.tensor_copy(Vb[:, :, :].rearrange("p b (h k) -> p h b k", h=H)[:, 2 * j:2 * j + 2],
                                    ps[:, 0:4 * SK].rearrange("p (h b k) -> p h b k", h=2, b=B)
                                    ).then_inc(evac_dve, 1)
                    if j == 7:
                        dve.wait_ge(ld_sqw, 16)
                        dve.wait_ge(ld_small, 80)
                        t = [qt[k][:, 0:P] for k in range(4)]
                        link(dve.tensor_scalar(t[3], sq("w8T"), 448.0, -448.0, ALU.min, ALU.max))
                        link(round8(w8[:, :], t[3], t))
                        link(dve.tensor_scalar(t[3], k8in[:, :], sc[:, 2:3], None, ALU.mult))
                        link(round8(k8[:, :], t[3], t))
                        parts = [qt[0], qt[1], qt[2]]
                        third = [col[:, COL["third"][0] + r:COL["third"][0] + r + 1] for r in range(3)]
                        bf = b13s
                        link(dve.tensor_copy(bf[:, :], b13[:, :]))
                        link(dve.tensor_copy(parts[0], bf[:, :]))
                        link(dve.tensor_tensor(b13[:, :], b13[:, :], parts[0], ALU.subtract))
                        link(dve.tensor_copy(bf[:, :], b13[:, :]))
                        link(dve.tensor_copy(parts[1], bf[:, :]))
                        link(dve.tensor_tensor(parts[2], b13[:, :], parts[1], ALU.subtract))
                        link(dve.tensor_scalar(parts[0], parts[0], third[0], None, ALU.mult))
                        link(dve.scalar_tensor_tensor(out=parts[0], in0=parts[1], scalar=third[1], in1=parts[0],
                                                      op0=ALU.mult, op1=ALU.add))
                        link(dve.scalar_tensor_tensor(out=bf[:, :], in0=parts[2], scalar=third[2], in1=parts[0],
                                                      op0=ALU.mult, op1=ALU.add))
                        link(dve.tensor_copy(mrow[:, 0, :], mint[:, :]))
                        dve.tensor_scalar(keep3[:, :], mrow[:, 0, :], 0.0, None, ALU.not_equal).then_inc(w8_ready, 1)
                        dve.wait_ge(w8_ready, 1)
                elif kind == "kvT":
                    l = item[1]
                    ps = filled(dve, item)
                    if l >= 2:
                        dve.wait_ge(blocks_ready, l - 1)
                    k_ps, v_ps = ps[:, 0:B * SK], ps[:, 256:256 + B * SK]
                    if l < 3:
                        dve.tensor_scalar(kvs[:, 0, :], k_ps, colv(f"bk{l}"), SCALE, ALU.add, ALU.mult)
                        dve.tensor_scalar(kvs[:, 1, :], v_ps, colv(f"bv{l}"), None, ALU.add).then_inc(evac_dve, 1)
                    else:
                        dve.scalar_tensor_tensor(out=kvs[:, 0, :], in0=k_ps, scalar=SCALE, in1=keep3[:, :],
                                                 op0=ALU.mult, op1=ALU.mult)
                        dve.tensor_copy(kvs[:, 1, :], v_ps).then_inc(evac_dve, 1)
                    if l in (1, 3):
                        if l == 1:
                            link(dve.tensor_scalar(mrow[:, 0, :], rowv("mask1"), -3e38, 3e38, ALU.max, ALU.min))
                        else:
                            dve.wait_ge(scores_full, 3 * nth("S", 1, 1, 3))
                            link(dve.tensor_scalar(mrow[:, 0, :], keep3[:, :], 1e9, -1e9, ALU.mult, ALU.add))
                        bfs = [mrow[:, r, :].bitcast(BF16)[:, 0:B * SK] for r in (3, 4, 5)]
                        link(dve.tensor_copy(bfs[0], mrow[:, 0, :]))
                        link(dve.tensor_tensor(mrow[:, 1, :], mrow[:, 0, :], bfs[0], ALU.subtract))
                        link(dve.tensor_copy(bfs[1], mrow[:, 1, :]))
                        link(dve.tensor_tensor(mrow[:, 2, :], mrow[:, 1, :], bfs[1], ALU.subtract))
                        link(dve.tensor_copy(bfs[2], mrow[:, 2, :]))
                        dve.wait_ge(const_ready, 2)
                        for r in range(3):
                            for b in range(B):
                                last = dve.tensor_copy(
                                    maskrow[32 * r:32 * r + 1, b, :].rearrange("p (h k) -> p h k", h=H),
                                    bfs[r][32 * r:32 * r + 1, b * SK:(b + 1) * SK]
                                    .rearrange("p (a k) -> p a k", a=1).broadcast_to([1, H, SK]))
                        last.then_inc(mask_ready, 1)
                elif kind == "S":
                    k = nth(*item) - 1
                    r = k % 3
                    for c, (h0, h1) in enumerate(HEADS):
                        dve.wait_ge(scores_full, 3 * k + c + 1)
                        ins = dve.tensor_reduce(mx[:, r, h0:h1], bank(item[1:], c)[:, 0:SK * (h1 - h0)]
                                                .rearrange("p (h k) -> p h k", k=SK), AX.X, ALU.max)
                    link(ins)
                    if k >= 3:
                        dve.wait_ge(pt_full, 3 * (k - 2))
                    for c, (h0, h1) in enumerate(HEADS):
                        dve.tensor_tensor(
                            probs[:, r, SK * h0:SK * h1].rearrange("p (h k) -> p h k", k=SK),
                            bank(item[1:], c)[:, 0:SK * (h1 - h0)].rearrange("p (h k) -> p h k", k=SK),
                            mx[:, r, h0:h1].rearrange("p (h a) -> p h a", a=1).broadcast_to([P, h1 - h0, SK]),
                            ALU.subtract).then_inc(scores_taken, 1)
                elif kind == "N":
                    k = nth(*item) - 1
                    r = k % 3
                    dve.wait_ge(exp_ready, k + 1)
                    link(dve.tensor_reduce(den[:, r, :], probs[:, r, :].rearrange("p (h k) -> p h k", k=SK),
                                           AX.X, ALU.add))
                    dve.reciprocal(rden[:, r, :], den[:, r, :]).then_inc(rden_ready, 1)
                elif kind == "back":
                    _, l, b = item
                    ps = filled(dve, item)
                    update(b, ps[:, :], tg[:, 9:10] if l == 0 else tg[:, l:l + 1]).then_inc(evac_dve, 1)
                    emptied(dve, item)
                elif kind in ("f0", "f2"):
                    b = item[1]
                    emptied(dve, item)
                    if kind == "f0":
                        yy = qt[0]
                        link(dve.tensor_tensor(yy.rearrange("p (i n) -> p i n", n=P),
                                               y16[:, :].rearrange("p (i n) -> p i n", n=P),
                                               over_tiles(rowv("fb0"), P), ALU.add))
                        update(b, yy, tg[:, 4:5]).then_inc(x_new, 1)
                    else:
                        link(dve.tensor_tensor(y2.rearrange("p (i n) -> p i n", n=P),
                                               y2.rearrange("p (i n) -> p i n", n=P),
                                               over_tiles(fb2[:, :], P), ALU.add))
                        update(b, y2, tg[:, 6:7]).then_inc(x_new, 1)
                    dve.wait_ge(x_new, nth_x(kind, b))
                elif kind == "quant":
                    b = item[1]
                    emptied(dve, ("xt", 5, b))
                    link(dve.tensor_scalar(qt[3], xb[:, b, :], sc[:, 0:1], None, ALU.mult))
                    round8(xb[:, b, :], qt[3], qt).then_inc(quant_ready, 1)
                elif kind == "r1":
                    b = item[1]
                    ps = filled(dve, item)
                    dve.tensor_tensor(hr[:, b], ps[:, 0:NT * 64].rearrange("p (i n) -> p i n", n=64),
                                      over_tiles(rowv("br1"), 64), ALU.add).then_inc(evac_dve, 1)
                    emptied(dve, item)
                    n = batch_stats(lambda i: hr[:, b, i, :], b, 1e-6)
                    link(normalise(lambda i: hr[:, b, i, :], lambda i: hr[:, b, i, :], b, n))
                    link(dve.tensor_tensor(hr[:, b], hr[:, b], over_tiles(rowv("lns"), 64), ALU.mult))
                    dve.tensor_tensor(hr[:, b], hr[:, b], over_tiles(rowv("lnb"), 64), ALU.add).then_inc(h_ready, 1)
                elif kind in ("r3", "g1"):
                    b = item[1]
                    ps = filled(dve, item)
                    logits = ps[:, 0:NT * E].rearrange("p (i e) -> p i e", e=E)
                    rank = over_tiles(rowv("rank"), E)

                    def over_experts(ap):
                        return ap.rearrange("p (i a) -> p i a", a=1).broadcast_to([P, NT, E])

                    def first_max(v, best, dst, tmp):
                        link(dve.tensor_reduce(best, v, AX.X, ALU.max))
                        link(dve.tensor_tensor(dst, v, over_experts(best), ALU.is_equal))
                        link(dve.tensor_tensor(dst, dst, rank, ALU.mult))
                        link(dve.tensor_reduce(tmp, dst, AX.X, ALU.max))
                        return dve.tensor_tensor(dst, dst, over_experts(tmp), ALU.is_equal)

                    if kind == "r3":
                        dve.tensor_tensor(lg[:, b], logits, over_tiles(rowv("br2"), E), ALU.add).then_inc(evac_dve, 1)
                    else:
                        dve.tensor_copy(lg[:, b], logits).then_inc(evac_dve, 1)
                    emptied(dve, item)
                    m = [m12[:, b, q, :] for q in range(8)]
                    link(first_max(lg[:, b], m[0], oh[:, 0], m[1]))
                    if kind == "r3":
                        link(dve.scalar_tensor_tensor(out=lg[:, b], in0=oh[:, 0], scalar=-3e38, in1=lg[:, b],
                                                      op0=ALU.mult, op1=ALU.add))
                        link(first_max(lg[:, b], m[4], oh[:, 1], m[1]))
                        dve.tensor_tensor(m[2], m[4], m[0], ALU.subtract).then_inc(gap_ready, 1)
                        dve.wait_ge(gap_exp, b + 1)
                        link(dve.tensor_scalar(m[5], m[3], 1.0, None, ALU.add))
                        link(dve.reciprocal(m[6], m[5]))
                        link(dve.tensor_tensor(m[7], m[3], m[6], ALU.mult))
                        link(dve.tensor_tensor(oh[:, 0], oh[:, 0], over_experts(m[6]), ALU.mult))
                        link(dve.tensor_tensor(oh[:, 1], oh[:, 1], over_experts(m[7]), ALU.mult))
                        link(dve.tensor_tensor(oh[:, 0], oh[:, 0], oh[:, 1], ALU.add))
                        for part in range(3):
                            link(dve.tensor_copy(sbf[:, :, :], oh[:, 0]))
                            ins = dve.tensor_copy(s24[:, b, :, part, :], sbf[:, :, :])
                            if part < 2:
                                link(ins)
                                link(dve.tensor_tensor(oh[:, 0], oh[:, 0], s24[:, b, :, part, :], ALU.subtract))
                        ins.then_inc(sel_ready, 1)
                    else:
                        for part in range(3):
                            ins = dve.tensor_copy(s24[:, b, :, part, :], oh[:, 0])
                        ins.then_inc(sel_ready, 1)
                elif kind == "moe1":
                    base = USE[("bc1", 0, 0)][2] - 1

                    def combine(e, b, first):
                        dve.wait_ge(y_step, 8 * e + FT * b + FT)
                        dve.wait_ge(evac_act, 2 * e + (base + b + 1))
                        if not first:
                            dve.wait_ge(acc_done, 2 * e + b - 1)
                        dve.scalar_tensor_tensor(out=ytmp[:, b, :], in0=TB[b][:, :],
                                                 scalar=col[:, bass.ds(e + COL["b2"][0], 1)], in1=pbc[:, b, :],
                                                 op0=ALU.add, op1=ALU.mult).then_inc(ytmp_ready, 1)

                    def body(e, first):
                        for s in range(2 * FT):
                            b, j = divmod(s, FT)
                            dve.wait_ge(gelu_ready, 8 * e + s + 1)
                            if not (first and s < 2):
                                dve.wait_ge(y_step, 8 * e + s - 1)
                            dve.scalar_tensor_tensor(out=gg[:, s % 2, :], in0=SC[2 * (s % 2)][:, :],
                                                     scalar=col[:, bass.ds(e * 2 * FT + (COL["b1"][0] + j), 1)],
                                                     in1=gel[:, s % 2, :], op0=ALU.add,
                                                     op1=ALU.mult).then_inc(g_ready, 1)
                            if s == FT:
                                combine(e, 0, first)
                        combine(e, 1, first)

                    body(0, True)
                    with dve.Fori(1, E) as e:
                        body(e, False)
                elif kind == "back1":
                    b = item[1]
                    ps = filled(dve, item)
                    update(b, ps[:, :], tg[:, 5:6]).then_inc(evac_dve, 1)
                    emptied(dve, item)
                elif kind == "moe3":
                    b = item[1]
                    for e in range(E):
                        n = E * b + e
                        ps = filled(dve, ("bc3", b, e))
                        if b and e < 2:
                            dve.wait_ge(pre3_full, FT)
                        elif n >= 2:
                            dve.wait_ge(mm3, n - 1 - b)
                        dve.scalar_tensor_tensor(out=xm[:, n % 2, :], in0=ps[:, :], scalar=1.0, in1=xnT[:, b, :],
                                                 op0=ALU.min, op1=ALU.mult).then_inc(evac_dve, 1)
                elif kind == "z3":
                    b = item[1]
                    ps = filled(dve, item)
                    dve.tensor_tensor(zz[:, b], ps[:, :].rearrange("p (i n) -> p i n", n=P), xn[:, b],
                                      ALU.add).then_inc(evac_dve, 1)
                    emptied(dve, item)
                    n = batch_stats(lambda i: zz[:, b, i, :], b, 1e-12)
                    link(normalise(lambda i: zz[:, b, i, :], lambda i: zz[:, b, i, :], b, n))
                    link(dve.tensor_tensor(zz[:, b], zz[:, b], over_tiles(rowv("gamma"), P), ALU.mult))
                    link(dve.tensor_tensor(zz[:, b], zz[:, b], over_tiles(rowv("beta"), P), ALU.add))
                    update(b, zz[:, b].rearrange("p i n -> p (i n)"), tg[:, 7:8]).then_inc(out_ready, 1)

        @block.tensor
        def _(pe):
            pe.wait_ge(ld_sqw, 16)
            for item in ORDER:
                kind = item[0]
                if kind == "kv0":
                    j = item[1]
                    pe.wait_ge(ld_kv, 16)
                    for which in "kv":
                        ps = acquire(pe, item + (which,))
                        pe.matmul(ps[:, 0:B * SK], kvc("w" + which)[:, j * P:(j + 1) * P], kvc("ctxT"),
                                  start=True, stop=True).then_inc(misc_full, 1)
                elif kind == "kp0":
                    j = item[1]
                    for which, w, src in (("k", "wqT", kbd), ("v", "wout", vbd)):
                        ps = acquire(pe, item + (which,))
                        emptied(pe, ("kv0", j, which))
                        wj = kvc(w)[:, j * P:(j + 1) * P]
                        pe.matmul(ps[:, 0:4 * SK], wj, src[:, j % 2].rearrange("p h n -> p (h n)"),
                                  start=True, stop=True).then_inc(misc_full, 1)
                elif kind == "vp":
                    _, l, b, g = item
                    c0, c1 = GROUPS[g]
                    ps = acquire(pe, item)
                    if l == 0:
                        emptied(pe, ("kp0", 7, "v"))
                    else:
                        pe.wait_ge(blocks_ready, l)
                    for c in range(c0, c1):
                        k0, n = CH[c]
                        dst = ps[0:n, P * (c - c0):P * (c - c0) + P]
                        src = Vb[:, b, k0:k0 + n]
                        if l < 2:
                            ins = pe.transpose(dst, src, ident)
                        else:
                            ins = pe.matmul(dst, src, sq(f"wo{l}"), start=True, stop=True)
                    ins.then_inc(misc_full, 1)
                elif kind == "xt":
                    _, s, b = item
                    ps = acquire(pe, item)
                    pe.wait_ge(xn_ready, nth("ln_apply", s, b) - B)
                    for i in range(NT):
                        ins = pe.transpose(ps[:, i * P:(i + 1) * P], xn[:, b, i, :], ident)
                    ins.then_inc(misc_full, 1)
                elif kind == "q":
                    _, l, b = item
                    ps = acquire(pe, item)
                    emptied(pe, ("xt", 2 * l, b))
                    pe.matmul(ps[:, :], sq(f"wq{l}"), xnT[:, b, :], start=True, stop=True).then_inc(misc_full, 1)
                elif kind == "kvT":
                    l = item[1]
                    ps = acquire(pe, item)
                    pe.matmul(ps[:, 0:B * SK], sq(f"wk{l}"), kvc("ctxT"), start=True, stop=True)
                    pe.matmul(ps[:, 256:256 + B * SK], sq(f"wv{l}"), kvc("ctxT"),
                              start=True, stop=True).then_inc(misc_full, 1)
                elif kind == "S":
                    _, l, b, i = item
                    k = nth(*item) - 1
                    if i == 0:
                        emptied(pe, ("q", l, b) if l else ("xt", 0, b))
                    if l == 0 and k == 0:
                        emptied(pe, ("kp0", 7, "k"))
                    if l and b == 0 and i == 0:
                        pe.wait_ge(blocks_ready, l)
                        if l in (1, 3):
                            pe.wait_ge(mask_ready, (l + 1) // 2)
                        if l == 2:
                            pe.wait_ge(g_ready, 8 * E)
                    q = (qT if l else xnT)[:, b, i * P:(i + 1) * P]
                    for c, (h0, h1) in enumerate(HEADS):
                        n = 3 * k + c
                        if n >= 4:
                            pe.wait_ge(scores_taken, n - 3)
                        dst = bank(item[1:], c)[:, 0:SK * (h1 - h0)]
                        masked = l in (1, 3)
                        ins = pe.matmul(dst, q, Kp[:, l % 2, b, SK * h0:SK * h1], start=True, stop=not masked)
                        if masked:
                            ins = pe.matmul(dst, ones3[:, :], maskrow[:, b, SK * h0:SK * h1], start=False, stop=True)
                        ins.then_inc(scores_full, 1)
                elif kind == "T":
                    _, l, b, i = item
                    k = nth(*item) - 1
                    pe.wait_ge(probs_ready, k + 1)
                    if l == 2 and k == nth("T", 2, 0, 0) - 1:
                        pe.wait_ge(ytmp_ready, 2 * E)
                    for g, (c0, c1) in enumerate(GROUPS):
                        n = 3 * k + g
                        if n >= 2:
                            pe.wait_ge(pt_copied, n - 1)
                        for c in range(c0, c1):
                            k0, m = CH[c]
                            ins = pe.transpose(TB[n % 2][0:m, P * (c - c0):P * (c - c0) + P],
                                               probs[:, k % 3, k0:k0 + m], ident)
                        ins.then_inc(pt_full, 1)
                elif kind == "PV":
                    _, l, b = item
                    ps = acquire(pe, item)
                    pe.wait_ge(pt_copied, 3 * nth("T", l, b, NT - 1))
                    emptied(pe, ("vp", l, b, 2))
                    for c, (k0, m) in enumerate(CH):
                        ins = pe.matmul(ps[:, :], Vp[0:m, l % 2, b, c, :], PT[0:m, c, :],
                                        start=(c == 0), stop=(c == len(CH) - 1))
                    ins.then_inc(misc_full, 1)
                elif kind == "back":
                    _, l, b = item
                    ps = acquire(pe, item)
                    emptied(pe, ("PV", l, b))
                    for i in range(NT):
                        ins = pe.transpose(ps[:, i * P:(i + 1) * P], oT[:, b, i * P:(i + 1) * P], ident)
                    ins.then_inc(misc_full, 1)
                elif kind in ("f0", "f2"):
                    b = item[1]
                    ps = acquire(pe, item)
                    pe.wait_ge(w8_ready, 1)
                    if kind == "f0":
                        emptied(pe, ("xt", 1, b))
                    else:
                        pe.wait_ge(quant_ready, b + 1)
                    src, w = (xq8, w8) if kind == "f0" else (xb, k8)
                    for i in range(NT):
                        ins = pe.matmul(ps[:, i * P:(i + 1) * P], src[:, b, i * P:(i + 1) * P], w[:, :],
                                        start=True, stop=True)
                    ins.then_inc(misc_full, 1)
                elif kind in ("r1", "g1"):
                    b = item[1]
                    ps = acquire(pe, item)
                    emptied(pe, ("xt", 3 if kind == "r1" else 7, b))
                    w, n = (sq("wr1"), 64) if kind == "r1" else (sq("wrT3"), E)
                    for i in range(NT):
                        ins = pe.matmul(ps[:, i * n:(i + 1) * n], xnT[:, b, i * P:(i + 1) * P], w,
                                        start=True, stop=True)
                    ins.then_inc(misc_full, 1)
                elif kind == "r2":
                    b = item[1]
                    ps = acquire(pe, item)
                    pe.wait_ge(hg_ready, b + 1)
                    for i in range(NT):
                        ins = pe.transpose(ps[0:64, i * P:(i + 1) * P], hg[:, b, i, :], ident)
                    ins.then_inc(misc_full, 1)
                elif kind == "r3":
                    b = item[1]
                    ps = acquire(pe, item)
                    emptied(pe, ("r2", b))
                    for i in range(NT):
                        ins = pe.matmul(ps[:, i * E:(i + 1) * E], hT[:, b, i * P:(i + 1) * P], sq("wr2")[0:64, :],
                                        start=True, stop=True)
                    ins.then_inc(misc_full, 1)
                elif kind in ("r4", "g2"):
                    b = item[1]
                    ps = acquire(pe, item)
                    pe.wait_ge(sel_ready, b + 1 + (B if kind == "g2" else 0))
                    for i in range(NT):
                        ins = pe.transpose(ps[0:3 * E, i * P:(i + 1) * P],
                                           s24[:, b, i].rearrange("p t e -> p (t e)"), ident)
                    ins.then_inc(misc_full, 1)
                elif kind == "moe1":
                    pe.wait_ge(ld_w1, 32)
                    pe.wait_ge(scores_taken, 3 * nth("S", 1, 1, 3))
                    pe.wait_ge(pt_copied, 3 * nth("T", 1, 1, 3))
                    base = USE[("bc1", 0, 0)][2] - 1
                    full = USE[("bc1", 0, 0)][0]

                    def up(e, s):
                        b, j = divmod(s, FT)
                        for half in range(2):
                            ins = pe.matmul(SC[2 * (s % 2) + half][:, :],
                                            w1[:, e, half * F1 + j * P:half * F1 + (j + 1) * P], xnT[:, b, :],
                                            start=True, stop=True)
                        ins.then_inc(x12_full, 1)

                    def body(e, first, last):
                        for s in range(2 * FT):
                            b, j = divmod(s, FT)
                            if j == 0:
                                if first:
                                    acquire(pe, ("bc1", 0, b))
                                    emptied(pe, ("r4", b))
                                else:
                                    pe.wait_ge(evac_act, 2 * e + (base + b - 1))
                                pe.matmul(MB[(full + b) % 2][:, :], esel[:, e, :], selT[:, b, :],
                                          start=True, stop=True).then_inc(misc_full, 1)
                            if not (last and s == 2 * FT - 1):
                                if not (first and s == 0):
                                    pe.wait_ge(g_ready, 8 * e + s)
                                up(e if s + 1 < 2 * FT else e + 1, (s + 1) % (2 * FT))
                            pe.wait_ge(g_ready, 8 * e + s + 1)
                            if j == 0 and not first:
                                pe.wait_ge(ytmp_ready, 2 * e + b - 1)
                            pe.matmul(TB[b][:, :], w2[:, e, j, :], gg[:, s % 2, :], start=(j == 0),
                                      stop=(j == FT - 1)).then_inc(y_step, 1)

                    up(0, 0)
                    body(0, True, False)
                    for e in range(1, E):
                        body(e, False, e == E - 1)
                elif kind == "back1":
                    b = item[1]
                    ps = acquire(pe, item)
                    pe.wait_ge(acc_done, 2 * E - 1 + b)
                    for i in range(NT):
                        ins = pe.transpose(ps[:, i * P:(i + 1) * P], acc[:, b, i * P:(i + 1) * P], ident)
                    ins.then_inc(misc_full, 1)
                elif kind == "moe3":
                    b = item[1]
                    if b == 0:
                        pe.wait_ge(ld_w3, 32)
                        pe.wait_ge(scores_taken, 3 * nth("S", 3, 1, 3))
                    emptied(pe, ("g2", b))

                    def share(e):
                        ps = acquire(pe, ("bc3", b, e))
                        pe.matmul(ps[:, :], esel[:, e, :], selT[:, b, :], start=True,
                                  stop=True).then_inc(misc_full, 1)

                    share(0)
                    for f in range(FT):
                        if b:
                            pe.wait_ge(inter_ready, f + 1)
                        pe.matmul(SC[f][:, :], b13s[:, f * P:(f + 1) * P], selT[:, b, :], start=True, stop=False)
                    for e in range(E):
                        if e + 1 < E:
                            share(e + 1)
                        emptied(pe, ("bc3", b, e))
                        for f in range(FT):
                            ins = pe.matmul(SC[f][:, :], w3[:, e, f * P:(f + 1) * P], xm[:, (E * b + e) % 2, :],
                                            start=False, stop=(e == E - 1))
                            if e == E - 1 and f < FT - 1:
                                ins.then_inc(pre3_full, 1)
                        if e < E - 1:
                            ins.then_inc(mm3, 1)
                        else:
                            ins.then_inc(pre3_full, 1)
                elif kind == "y3":
                    b = item[1]
                    ps = acquire(pe, item)
                    for f in range(FT):
                        pe.wait_ge(inter_ready, FT * b + f + 1)
                        ins = pe.matmul(ps[:, :], wo3[:, f, :], inter[:, f, :], start=(f == 0), stop=(f == FT - 1))
                    ins.then_inc(misc_full, 1)
                elif kind == "z3":
                    b = item[1]
                    ps = acquire(pe, item)
                    emptied(pe, ("y3", b))
                    for i in range(NT):
                        ins = pe.transpose(ps[:, i * P:(i + 1) * P], yT3[:, b, i * P:(i + 1) * P], ident)
                    ins.then_inc(misc_full, 1)


def nth_x(kind, b):
    return [i for i in ORDER if i[0] in ("f0", "f2")].index((kind, b)) + 1


def kernel(**inputs):
    import numpy as _np
    import concourse.bacc as _bacc
    from concourse import mybir as _mybir
    from concourse.bass_utils import run_bass_kernel_spmd as _run

    a = {k: _np.asarray(v) for k, v in inputs.items()}
    f32 = _np.float32

    def tiles(w):
        n = w.shape[0] // P
        return w.reshape(n, P, w.shape[1]).transpose(1, 0, 2).reshape(P, n * w.shape[1])

    def padded(w, rows=P):
        z = _np.zeros((rows,) + w.shape[1:], w.dtype)
        z[: w.shape[0]] = w
        return z

    wkv = a["L0_xattn_w_kv"]
    kvp = _np.concatenate([a["ctx_1024"].reshape(B * SK, P).T, wkv[:, :1024], wkv[:, 1024:],
                           tiles(a["L0_xattn_w_q"].T), tiles(a["L0_xattn_w_out"])], axis=1)
    eye = _np.eye(P, dtype=f32)
    sqwp = _np.concatenate(
        [eye, a["L0_ffn_weight"].T, a["L1_xattn_Wq"], a["L1_xattn_Wk"], a["L1_xattn_Wv"]]
        + [a[f"L{l}_xattn_W{n}"].T for l in (2, 3) for n in "qkvo"]
        + [a["L1_ffn_Wr1"], padded(a["L1_ffn_Wr2"]), a["L3_ffn_Wr"].T], axis=1)
    heads = _np.zeros((P, H), f32)
    for h in range(H):
        heads[8 * h:8 * h + 8, h] = 1.0
    third = _np.zeros((P, 3), f32)
    for r in range(3):
        third[E * r:E * r + E, r] = 1.0
    vec = ["L0_xattn_ln_gamma", "L0_xattn_ln_beta", "L0_xattn_b_out", "L1_xattn_bq", "L1_xattn_bk", "L1_xattn_bv",
           "L2_xattn_bq", "L2_xattn_bk", "L2_xattn_bv", "L2_xattn_bo", "L3_xattn_bo", "L3_ffn_bo"]
    colp = _np.concatenate([a[n].reshape(P, 1) for n in vec]
                           + [a["L1_ffn_b2"].T, a["L1_ffn_b1"].reshape(E, 2 * FT, P).transpose(2, 0, 1)
                              .reshape(P, 2 * FT * E), heads, third], axis=1)
    rowp = _np.concatenate([a["L0_ffn_bias"], a["L1_ffn_br1"], a["L1_ffn_ln_scale"], a["L1_ffn_ln_bias"],
                            a["L1_ffn_br2"], a["L3_ffn_gamma"], a["L3_ffn_beta"], a["g_xattn"], a["g_ffn"],
                            a["L0_xattn_gate"], a["L2_ffn_input_scale"], a["L2_ffn_kernel_scale"],
                            a["mask_Bx1x1xS2_ff0"].reshape(-1), _np.arange(E, 0, -1).astype(f32)]).reshape(1, -1)
    sel = _np.zeros((P, E, P), f32)
    for e in range(E):
        for r in range(3):
            sel[E * r + e, e, :] = 1.0
    bf = a["L2_ffn_kernel"].dtype
    arrays = {
        "x_in": a["x"].reshape(B, NT, P, P).transpose(2, 0, 1, 3),
        "kv_in": kvp, "sqw_in": sqwp, "col_in": colp, "row_in": rowp,
        "w1_in": a["L1_ffn_W1"].transpose(1, 0, 2),
        "w2_in": a["L1_ffn_W2"].reshape(E, FT, P, P).transpose(2, 0, 1, 3),
        "w3_in": a["L3_ffn_W1"].transpose(1, 0, 2),
        "wo3_in": a["L3_ffn_Wo"].reshape(FT, P, P).transpose(1, 0, 2),
        "b13_in": padded(_np.concatenate([a["L3_ffn_b1"]] * 3, axis=0)),
        "mask3_in": a["mask_BxS2_ik0"].reshape(1, -1),
        "k8_in": a["L2_ffn_kernel"], "fb2_in": a["L2_ffn_bias"].reshape(1, -1),
        "esel_in": sel.astype(bf),
    }
    arrays = {k: _np.ascontiguousarray(v) for k, v in arrays.items()}
    nc = _bacc.Bacc("TRN2", target_bir_lowering=False, num_devices=1)
    args = [nc.dram_tensor(k, v.shape, _mybir.dt.from_np(v.dtype), kind="ExternalInput").ap()
            for k, v in arrays.items()]
    out = nc.dram_tensor("out", (P, B, NT, P), _mybir.dt.float32, kind="ExternalOutput").ap()
    build(nc, *args, out)
    r = _run(nc, [arrays], core_ids=[0])
    return r.results[0]["out"].transpose(1, 2, 0, 3).reshape(B, SQ, P)
```

```python
from contextlib import ExitStack

import numpy as np

import concourse.bass as bass
from concourse import mybir

F32 = mybir.dt.float32
F32R = mybir.dt.float32r
BF16 = mybir.dt.bfloat16
F16 = mybir.dt.float16
FP8 = mybir.dt.float8e4
I32 = mybir.dt.int32
ALU = mybir.AluOpType
ACT = mybir.ActivationFunctionType
AX = mybir.AxisListType

P = 128
B = 2
NT = 4
SQ = NT * P
U = 4
UT = B * NT // U
UQ = UT * P
SK = 77
H = 16
HK = H * SK
NL = 4
HEADS = [(0, 5), (5, 10), (10, 16)]
CH = [(c, min(P, HK - c)) for c in range(0, HK, P)]
GROUPS = [(0, 4), (4, 8), (8, 10)]
E = 8
F1 = 512
FT = F1 // P
SCALE0 = 64 ** -0.5
SCALE = 8 ** -0.5
MAGIC = 1.5 * 2.0 ** 20
OVER8 = 7.3e35

KV = {}
SQW = {}
COL = {}
ROW = {}


def _place(table, names):
    at = 0
    for name, width in names:
        table[name] = (at, at + width)
        at += width
    return at


KV_N = _place(KV, [("ctxT", B * SK)] + [(f"j{j}", 4 * P) for j in range(8)])
SQW_N = _place(SQW, [("ident", P), ("w8T", P), ("wq1", P), ("wk1", P), ("wv1", P)]
               + [(f"w{n}{l}", P) for l in (2, 3) for n in "qkvo"] + [("wr1", 64), ("wr2", E), ("wrT3", E)])
COL_N = _place(COL, [(n, 1) for n in ("ln_g", "ln_b", "bo0", "bq1", "bk1", "bv1", "bq2", "bk2", "bv2", "bo2",
                                      "bo3", "fbo3")]
               + [("b2", E), ("b1", 2 * FT * E), ("headmask", H), ("third", 3)])
ROW_N = _place(ROW, [("fb0", P), ("br1", 64), ("lns", 64), ("lnb", 64), ("br2", E), ("gamma", P), ("beta", P),
                     ("gates", 9), ("s_in", 1), ("s_k", 1), ("mask1", B * SK), ("rank", E)])

ORDER = []


def _order():
    o = ORDER

    def stats(s, u):
        return [("ln_stats", s, u)]

    def apply(s, u):
        return [("ln_apply", s, u), ("xt", s, u)]

    for s in (-1, 0):
        for u in range(U):
            o.extend(stats(s, u))
        for u in range(U):
            o.append(("ln_apply", s, u))
    o.append(("kv0", 0))
    for j in range(8):
        if j + 1 < 8:
            o.append(("kv0", j + 1))
        o.append(("kp0", j))
        if j < U:
            o.append(("xt", 0, j))
    for b in range(B):
        for g in range(3):
            o.append(("vp", 0, b, g))

    def between(l, u):
        s = 2 * l + 1
        at = {(1, "v"): [("PV", l, u)], (1, "b"): [("back", l, u)] + stats(s, u), (2, "a"): apply(s, u)}
        if l in (0, 2):
            if l == 2:
                at[2, "a"].append(("quant", u))
            at[2, "b"] = [(f"f{l}", u)] + stats(s + 1, u)
            at[3, "a"] = [("ln_apply", s + 1, u)]
            at[3, "b"] = [("xt", s + 1, u)]
            at[4, "e"] = [("q", l + 1, u)]
        elif u % (U // B) == U // B - 1:
            b = u // (U // B)
            if l == 1:
                at[2, "b"] = [("r1", b)]
                at[3, "a"] = [("r2", b)]
                at[3, "b"] = [("r3", b), ("xsplit", b)] + ([("wsplit",)] if b == 0 else [])
                at[4, "a"] = [("r3b", b)]
                at[5, "e"] = [("r4", b)]
            else:
                at[2, "b"] = [("g1", b)]
                at[3, "a"] = [("g2", b)]
        return at

    def prepare(l, k0):
        at = {(0, "a"): [("kvT", l)], (0, "b"): [("blk", l, 1, 0)], (1, "b"): [("blk", l, 1, 1)],
              (2, "b"): [("blk", l, 0, 0)], (4, "b"): [("blk", l, 0, 1)]}
        for n in range(6):
            at[2 + n, "e"] = [("vp", l, n // 3, n % 3)]
        if l in (1, 3):
            for b in range(B):
                at[5 + b, "b"] = [("mrow", l, b)]
        return {(k0 + k, slot): items for (k, slot), items in at.items()}

    def attentions(layers, plan):
        tiles = [(l, u, i) for l in layers for u in range(U) for i in range(UT)]

        def add(stages, k0=0):
            for (k, slot), items in stages.items():
                plan[k0 + k, slot] = plan.get((k0 + k, slot), []) + items

        for n, l in enumerate(layers):
            if l + 1 < NL:
                add(prepare(l + 1, n * U * UT))
            if n == 0 and l:
                for u in range(U):
                    add({(max(2 * u - 1, -1), "b"): [("q", l, u)]})
            for u in range(U):
                add(between(l, u), (n * U + u) * UT + UT)
        o.extend(plan.pop((-1, "b"), []))
        for k in range(len(tiles) + 1):
            if k < len(tiles):
                o.append(("S", *tiles[k]))
            values = plan.pop((k, "v"), [])
            if values:
                o.extend([("X", *tiles[k])] if k < len(tiles) else [])
                o.extend(values)
            if k:
                o.append(("T", *tiles[k - 1]))
            o.extend(plan.pop((k, "e"), []))
            if k < len(tiles) and not values:
                o.append(("X", *tiles[k]))
            o.extend(plan.pop((k, "a"), []))
            if k < len(tiles):
                o.append(("N", *tiles[k]))
            o.extend(plan.pop((k, "b"), []))
            if k == 1 and layers[0] == 0:
                o.append(("conv8",))
        slots = ("v", "e", "a", "b")
        return [plan[n] for n in sorted(plan, key=lambda n: (n[0], slots.index(n[1])))]

    def weave(segments, chains):
        for n, segment in enumerate(segments):
            if chains:
                o.extend(chains.pop(0))
            o.append(segment)
        for items in chains:
            o.extend(items)

    def belongs(item, b):
        return (item[-1] if item[0] in ("r1", "r2", "r3", "r3b", "r4", "g1", "g2", "xsplit") else item[-1] // (U // B)) == b

    rest = attentions([0, 1], {})
    while rest and any(belongs(i, 0) for items in rest for i in items):
        o.extend(rest.pop(0))
    weave([("moe1", 0, 0, 1), ("moe1", 0, 1, 2), ("moe1", 0, 2, 3), ("moe1", 0, 3, 4), ("moe1", 0, 4, 8)],
          [[], rest[0], rest[1] + rest[2], rest[3] + rest[4], *rest[5:]])
    weave([("moe1", 1, 0, 1), ("moe1", 1, 1, 2), ("moe1", 1, 2, 3), ("moe1", 1, 3, 4), ("moe1", 1, 4, 8)],
          [[], [("back1", 0)] + stats(4, 0) + [("back1", 1)] + stats(4, 1), apply(4, 0) + apply(4, 1), [("conv3",)]])
    rest = attentions([2, 3], {(0, "a"): [("back1", 2)] + stats(4, 2) + [("back1", 3)] + stats(4, 3),
                               (0, "b"): [("ln_apply", 4, 2), ("ln_apply", 4, 3)],
                               (1, "e"): [("xt", 4, 2), ("xt", 4, 3)]})
    while rest and any(belongs(i, 0) for items in rest for i in items):
        o.extend(rest.pop(0))
    weave([("moe3", 0, 0, 2), ("moe3", 0, 2, 4), ("moe3", 0, 4, 6), ("moe3", 0, 6, 8)], rest)
    o.extend([("y3", 0), ("moe3", 1, 0, 4), ("z3", 0), ("moe3", 1, 4, 8), ("norm3", 0), ("y3", 1), ("z3", 1),
              ("norm3", 1)])


_order()


def nth(*item):
    return [i for i in ORDER if i[0] == item[0]].index(item) + 1


def masked(e0, e1):
    return range(e0 + (e0 > 0), min(e1 + 1, E))


def total(kind):
    return len([i for i in ORDER if i[0] == kind])


USES = []
for _i in ORDER:
    _k = _i[0]
    if _k in ("xt", "q", "PV", "r2", "r4", "f0", "f2", "y3"):
        USES.append((_i, "act"))
    elif _k in ("back", "r1", "r3", "g1", "back1", "z3", "kvT"):
        USES.append((_i, "dve"))
    elif _k == "g2":
        USES.append((_i, "act"))
    elif _k == "vp":
        USES.append((_i, "act"))
    elif _k == "kv0":
        USES.append((_i + ("k",), "act"))
        USES.append((_i + ("v",), "dve"))
    elif _k == "kp0":
        USES.append((_i + ("k",), "act"))
        USES.append((_i + ("v",), "dve"))
    elif _k == "moe1":
        for _e in range(*_i[2:]):
            USES.append((("bc1", _i[1], _e), "act"))
    elif _k == "moe3":
        for _e in masked(*_i[2:]):
            USES.append((("bc3", _i[1], _e), "dve"))
USE = {u: (k, eng, [v[1] for v in USES[:k + 1]].count(eng)) for k, (u, eng) in enumerate(USES)}


def build(nc, x_in, kv_in, sqw_in, col_in, row_in, w1_in, w2_in, w3_in, wo3_in, b13_in, mask3_in, k8_in,
          fb2_in, esel_in, out):
    with ExitStack() as ctx:
        def sb(name, shape, dt=F32):
            return ctx.enter_context(nc.sbuf_tensor(name, shape, dt))

        def sem(name):
            return ctx.enter_context(nc.semaphore(name))

        x = sb("x", [P, B * NT, P])
        xn = sb("xn", [P, B * NT, P])
        xnT = sb("xnT", [P, U, UQ])
        oT = sb("oT", [P, UQ])
        scr = sb("scr", [P, 2, SQ])
        Kp = [sb("Kp0", [P, B, HK]), None]
        Vp = sb("Vp", [P, 2, B, len(CH), P])
        PT = sb("PT", [P, 2, len(CH), UQ])
        kv = sb("kv", [P, KV_N])
        sqw = sb("sqw", [P, SQW_N])
        col = sb("col", [P, COL_N])
        row = sb("row", [P, ROW_N])
        w1 = sb("w1", [P, E, 2 * F1])
        w2 = sb("w2", [P, E, FT, P])
        esel = sb("esel", [P, E, P], BF16)
        kvs = sb("kvs", [P, 2, B * SK])
        ones3 = sb("ones3", [P, P], BF16)
        maskrow = sb("maskrow", [P, B, HK], BF16)
        mrow = sb("mrow", [P, B * SK])
        msplit = sb("msplit", [P, 2, B * SK], BF16)
        msel = sb("msel", [P, B * SK], BF16)
        mint = sb("mint", [P, B * SK], I32)
        keep3 = sb("keep3", [P, B * SK])
        w8 = sb("w8", [P, P], BF16)
        k8in = sb("k8in", [P, P], BF16)
        k8 = sb("k8", [P, P], BF16)
        fb2 = sb("fb2", [P, P], BF16)
        xb = sb("xb", [P, U, UQ], BF16)
        xq8 = xb[:, 0:U // 2, :].rearrange("p u n -> p (u n)").bitcast(FP8).rearrange("p (u n) -> p u n", u=U)
        y16 = sb("y16", [P, UQ], F16)
        y2 = y16[:, :].bitcast(BF16)
        selT = sb("selT", [P, B, SQ], BF16)
        b13s = sb("b13s", [P, F1], BF16)
        tg = sb("tg", [P, 10])
        st = sb("st", [P, B * NT, 6])
        mv = sb("mv", [P, B * NT, 2])
        ve = sb("ve", [P, B * NT])
        rstd = sb("rstd", [P, B * NT])
        mhalf = sb("mhalf", [P, NT])
        mx = sb("mx", [P, 3, H])
        den = sb("den", [P, 3, H])
        rden = sb("rden", [P, 3, H])
        sc = sb("sc", [P, 4])
        lg = sb("lg", [P, B, NT, E])
        oh = sb("oh", [P, 2, NT, E])
        s24 = sb("s24", [P, B, NT, 3, E])
        sbf = sb("sbf", [P, NT, E], BF16)
        m12 = sb("m12", [P, B, 8, NT])

        ffa = PT[:, :, :, :].rearrange("p r c n -> p (r c n)")
        gel = ffa[:, 0:2 * SQ].rearrange("p (r n) -> p r n", r=2)
        gg = ffa[:, 2 * SQ:4 * SQ].rearrange("p (r n) -> p r n", r=2)
        pbc = ffa[:, 4 * SQ:6 * SQ].rearrange("p (r n) -> p r n", r=2)
        ytmp = ffa[:, 6 * SQ:8 * SQ].rearrange("p (r n) -> p r n", r=2)
        acc = ffa[:, 8 * SQ:10 * SQ].rearrange("p (r n) -> p r n", r=2)
        inter = ffa[:, 0:FT * SQ].rearrange("p (f n) -> p f n", f=FT)
        xm = ffa[:, 4 * SQ:6 * SQ].rearrange("p (r n) -> p r n", r=2)
        yT3 = ffa[:, 6 * SQ:8 * SQ].rearrange("p (r n) -> p r n", r=2)
        zz = ffa[:, 8 * SQ:10 * SQ].rearrange("p (r i n) -> p r i n", r=2, i=NT)
        nbd = 2 * 2 * B * SK
        kbd = ffa[:, 0:nbd].rearrange("p (r h n) -> p r h n", r=2, h=2)
        vbd = ffa[:, nbd:2 * nbd].rearrange("p (r h n) -> p r h n", r=2, h=2)
        b13 = scr[:, 0, :]
        hr = scr[:, 0, :].rearrange("p (b i n) -> p b i n", b=B, i=NT)
        hT = scr[0:64, 1, :]
        w3 = kv[:, 0:E * F1].rearrange("p (e f) -> p e f", e=E)
        wo3 = sb("wo3", [P, FT, P])

        with ExitStack() as attention:
            place = lambda name, shape: attention.enter_context(nc.sbuf_tensor(name, shape, F32))
            Vb = place("Vb", [P, B, HK])
            Kp[1] = place("Kp1", [P, B, HK])
            probs = place("probs", [P, 3, HK])
        w_hi = sb("w_hi", [P, 2, 2 * F1], F32R)
        sb("gap_v", [P, B * HK - 4 * F1])
        w_lo = sb("w_lo", [P, 2, 2 * F1], F32R)
        sb("gap_k", [P, B * HK - 4 * F1 + HK])
        x_part = sb("x_part", [P, B, HK], F32R)
        x_hi = [x_part[:, b, 0:SQ] for b in range(B)]
        x_lo = [x_part[:, b, SQ:2 * SQ] for b in range(B)]

        SC = [ctx.enter_context(nc.psum_tensor(f"SC{i}", [P, 512], F32)) for i in range(4)]
        TB = [ctx.enter_context(nc.psum_tensor(f"TB{i}", [P, 512], F32)) for i in range(2)]
        MB = [ctx.enter_context(nc.psum_tensor(f"MB{i}", [P, 512], F32)) for i in range(2)]

        ld_x = sem("ld_x")
        ld_kv = sem("ld_kv")
        ld_kvj = [sem(f"ld_kv{j}") for j in range(4)]
        ld_ident = sem("ld_ident")
        ld_b13 = sem("ld_b13")
        ld_sqw = sem("ld_sqw")
        ld_col = sem("ld_col")
        ld_row = sem("ld_row")
        ld_small = sem("ld_small")
        ld_w1 = sem("ld_w1")
        ld_w3 = sem("ld_w3")
        w_high = sem("w_high")
        w_split = sem("w_split")
        x_split = sem("x_split")
        const_ready = sem("const_ready")
        misc_full = sem("misc_full")
        evac_act = sem("evac_act")
        evac_dve = sem("evac_dve")
        dve_chain = sem("dve_chain")
        act_chain = sem("act_chain")
        gates_ready = sem("gates_ready")
        gates_mul = sem("gates_mul")
        var_ready = sem("var_ready")
        rstd_ready = sem("rstd_ready")
        xn_ready = sem("xn_ready")
        x_new = sem("x_new")
        w8_ready = sem("w8_ready")
        mask_split = sem("mask_split")
        mask_ready = sem("mask_ready")
        kbd_zero = sem("kbd_zero")
        blocks_ready = sem("blocks_ready")
        scores_full = sem("scores_full")
        scores_taken = sem("scores_taken")
        exp_ready = sem("exp_ready")
        rden_ready = sem("rden_ready")
        probs_ready = sem("probs_ready")
        pt_full = sem("pt_full")
        pt_copied = sem("pt_copied")
        quant_ready = sem("quant_ready")
        y_rounded = sem("y_rounded")
        h_ready = sem("h_ready")
        hg_ready = sem("hg_ready")
        gap_ready = sem("gap_ready")
        gap_exp = sem("gap_exp")
        sel_ready = sem("sel_ready")
        x12_full = sem("x12_full")
        gelu_ready = sem("gelu_ready")
        g_ready = sem("g_ready")
        y_step = sem("y_step")
        ytmp_ready = sem("ytmp_ready")
        acc_done = sem("acc_done")
        pre3_full = sem("pre3_full")
        inter_ready = sem("inter_ready")
        mm3 = sem("mm3")
        out_ready = sem("out_ready")
        stored = sem("stored")

        ctxT = kv[:, 0:KV["ctxT"][1]]

        def weight0(name, j):
            at = KV[f"j{j}"][0] + P * ["k", "v", "q", "out"].index(name)
            return kv[:, at:at + P]

        def sq(name):
            return sqw[:, SQW[name][0]:SQW[name][1]]

        def colv(name, i=0):
            return col[:, COL[name][0] + i:COL[name][0] + i + 1]

        def rowv(name):
            return row[:, ROW[name][0]:ROW[name][1]]

        def over_tiles(ap, n, tiles=UT):
            return ap.rearrange("p (a n) -> p a n", a=1).broadcast_to([P, tiles, n])

        def batch(ap, b):
            return ap[:, b * U // B:(b + 1) * U // B, :].rearrange("p u n -> p (u n)")

        ident = sq("ident")
        def bank(item, c):
            return SC[(3 * (nth("S", *item) - 1) + c) % 4]

        def acquire(pe, key):
            k, _, _ = USE[key]
            if k >= 2:
                emptied(pe, USES[k - 2][0])
            return MB[k % 2]

        def emptied(eng, key):
            _, who, n = USE[key]
            eng.wait_ge(evac_act if who == "act" else evac_dve, n)

        def filled(eng, key):
            k, _, _ = USE[key]
            eng.wait_ge(misc_full, k + 1)
            return MB[k % 2]

        block = ctx.enter_context(nc.Block())

        @block.sync
        def _(sp):
            sp.dma_start(x[:, :, :], x_in).then_inc(ld_x, 16)
            sp.dma_start(kv[:, 0:KV["j0"][0]], kv_in[:, 0:KV["j0"][0]]).then_inc(ld_kv, 16)
            for j in range(0, 8, 2):
                at = slice(KV[f"j{j}"][0], KV[f"j{j + 1}"][1])
                sp.dma_start(kv[:, at], kv_in[:, at]).then_inc(ld_kvj[j // 2], 16)
            sp.dma_start(sqw[:, P:], sqw_in[:, P:]).then_inc(ld_sqw, 16)
            emptied(sp, ("kv0", 1, "v"))
            sp.dma_start(w1[:, :, :], w1_in).then_inc(ld_w1, 16)
            sp.dma_start(w2[:, :, :, :], w2_in).then_inc(ld_w1, 16)
            sp.dma_start(wo3[:, :, :], wo3_in).then_inc(ld_w3, 16)
            emptied(sp, ("r4", B - 1))
            sp.dma_start(b13, b13_in).then_inc(ld_b13, 16)
            emptied(sp, ("kp0", 7, "v"))
            emptied(sp, ("kvT", 3))
            sp.dma_start(w3[:, :, :], w3_in).then_inc(ld_w3, 16)
            for b in range(B):
                sp.wait_ge(out_ready, b + 1)
                sp.dma_start(out[:, b * NT:(b + 1) * NT], x[:, b * NT:(b + 1) * NT, :]).then_inc(stored, 16)
            sp.wait_ge(stored, 16 * B)

        @block.gpsimd
        def _(pool):
            pool.memset(mhalf[:, :], -0.5)
            pool.memset(kbd[:, :, :, :], 0.0)
            pool.memset(vbd[:, :, :, :], 0.0).then_inc(kbd_zero, 1)
            pool.memset(maskrow[:, :, :], 0.0)
            pool.memset(selT[:, :, :], 0.0)
            pool.memset(ones3[:, :], 0.0).then_inc(const_ready, 1)
            pool.wait_ge(const_ready, 1)
            for r in range(3):
                pool.memset(ones3[32 * r:32 * r + 1, :], 1.0).then_inc(const_ready, 1)
                pool.wait_ge(const_ready, r + 2)
            stats = 0

            def low_part(m):
                pool.wait_ge(w_high, m + 1)
                if m >= 2:
                    pool.wait_ge(x12_full, FT * (m - 1))
                pool.tensor_tensor(w_lo[:, m % 2], w1[:, m % E, :], w_hi[:, m % 2].bitcast(F32),
                                   ALU.subtract).then_inc(w_split, 1)

            for item in ORDER:
                kind = item[0]
                if kind in ("ln_stats", "r1", "norm3"):
                    n = UT if kind == "ln_stats" else NT
                    at = slice(item[-1] * n, (item[-1] + 1) * n)
                    stats += 1
                    pool.wait_ge(var_ready, stats)
                    pool.tensor_tensor(rstd[:, at], ve[:, at], mhalf[:, 0:n], ALU.pow).then_inc(rstd_ready, 1)
                elif kind == "N":
                    k = nth(*item) - 1
                    pool.wait_ge(rden_ready, k + 1)
                    pv = probs[:, k % 3, :].rearrange("p (h k) -> p h k", h=H)
                    pool.tensor_tensor(pv, pv, rden[:, k % 3, :].rearrange("p (h a) -> p h a", a=1)
                                       .broadcast_to([P, H, SK]), ALU.mult).then_inc(probs_ready, 1)
                elif kind == "blk":
                    _, l, which, b = item
                    emptied(pool, ("kvT", l))
                    if which == 0 and l >= 2:
                        pool.wait_ge(scores_full, 3 * nth("S", l - 2, U - 1, UT - 1))
                    if which == 1:
                        filled(pool, ("vp", l - 1, 1, 2))
                    dst = (Kp[l % 2], Vb)[which]
                    pool.tensor_tensor(
                        dst[:, b, :].rearrange("p (h k) -> p h k", h=H),
                        kvs[:, which, b * SK:(b + 1) * SK].rearrange("p (a k) -> p a k", a=1)
                        .broadcast_to([P, H, SK]),
                        col[:, COL["headmask"][0]:COL["headmask"][1]].rearrange("p (h a) -> p h a", a=1)
                        .broadcast_to([P, H, SK]), ALU.mult).then_inc(blocks_ready, 1)
                elif kind == "mrow":
                    _, l, b = item
                    pool.wait_ge(mask_split, (l + 1) // 2)
                    if l == 3 and b == 0:
                        pool.wait_ge(scores_full, 3 * nth("S", 1, U - 1, UT - 1))
                    pool.tensor_copy(maskrow[:, b, :].rearrange("p (h k) -> p h k", h=H),
                                     msel[:, b * SK:(b + 1) * SK].rearrange("p (a k) -> p a k", a=1)
                                     .broadcast_to([P, H, SK])).then_inc(mask_ready, 1)
                elif kind == "moe1":
                    _, b, e0, e1 = item

                    def add(e, par, first):
                        pool.wait_ge(ytmp_ready, e + (E * b + 1))
                        if first:
                            pool.tensor_copy(acc[:, b, :], ytmp[:, par, :]).then_inc(acc_done, 1)
                        else:
                            pool.wait_ge(acc_done, e + E * b)
                            pool.tensor_tensor(acc[:, b, :], acc[:, b, :], ytmp[:, par, :],
                                               ALU.add).then_inc(acc_done, 1)

                    for e in range(e0, e1):
                        if E * b + e + 1 < B * E:
                            low_part(E * b + e + 1)
                        add(e, e % 2, e == 0)
                elif kind == "wsplit":
                    pool.wait_ge(scores_full, 3 * nth("S", 1, U - 1, UT - 1))
                    low_part(0)

        @block.scalar
        def _(act):
            act.dma_start(sqw[:, 0:P], sqw_in[:, 0:P]).then_inc(ld_ident, 16)
            act.dma_start(col[:, :], col_in).then_inc(ld_col, 16)
            act.dma_start(row[:, :], row_in.partition_broadcast(P)).then_inc(ld_row, 16)
            act.dma_start(mint[:, :], mask3_in.partition_broadcast(P)).then_inc(ld_small, 16)
            act.dma_start(k8in[:, :], k8_in).then_inc(ld_small, 16)
            act.dma_start(fb2[:, :], fb2_in.partition_broadcast(P)).then_inc(ld_small, 16)
            act.dma_start(esel[:, :, :], esel_in).then_inc(ld_small, 16)
            act.wait_ge(ld_row, 16)
            act.activation(tg[:, 0:9], rowv("gates"), ACT.Tanh).then_inc(gates_ready, 1)
            act.wait_ge(ld_col, 16)

            def high_part(m):
                act.activation(w_hi[:, m % 2], w1[:, m % E, :], ACT.Copy).then_inc(w_high, 1)

            for item in ORDER:
                kind = item[0]
                if kind == "kv0":
                    j = item[1]
                    ps = filled(act, item + ("k",))
                    act.wait_ge(kbd_zero, 1)
                    if j >= 2:
                        filled(act, ("kp0", j - 2, "k"))
                    for hh in range(2):
                        last = act.activation(kbd[64 * hh:64 * hh + 64, j % 2, hh, :],
                                              ps[64 * hh:64 * hh + 64, 0:B * SK], ACT.Copy, scale=SCALE0)
                    last.then_inc(evac_act, 1)
                elif kind == "kp0":
                    j = item[1]
                    ps = filled(act, item + ("k",))
                    act.activation(
                        Kp[0][:, :, :].rearrange("p b (h k) -> p h b k", h=H)[:, 2 * j:2 * j + 2],
                        ps[:, 0:4 * SK].rearrange("p (h b k) -> p h b k", h=2, b=B), ACT.Copy).then_inc(evac_act, 1)
                elif kind == "vp":
                    _, l, b, g = item
                    c0, c1 = GROUPS[g]
                    ps = filled(act, item)
                    if l >= 2:
                        filled(act, ("PV", l - 2, U - 1))
                    n = min(P, CH[c1 - 1][1])
                    if n == P:
                        act.activation(Vp[:, l % 2, b, c0:c1, :], ps[:, 0:P * (c1 - c0)]
                                       .rearrange("p (c n) -> p c n", n=P), ACT.Copy).then_inc(evac_act, 1)
                    else:
                        act.activation(Vp[:, l % 2, b, c0:c1 - 1, :], ps[:, 0:P * (c1 - c0 - 1)]
                                       .rearrange("p (c n) -> p c n", n=P), ACT.Copy)
                        act.activation(Vp[0:n, l % 2, b, c1 - 1, :], ps[0:n, P * (c1 - c0 - 1):P * (c1 - c0)],
                                       ACT.Copy).then_inc(evac_act, 1)
                elif kind == "xt":
                    _, s, u = item
                    ps = filled(act, item)
                    if s == 0:
                        act.activation(xnT[:, u, :], ps[:, 0:UQ], ACT.Identity, bias=colv("ln_b"),
                                       scale=colv("ln_g")).then_inc(evac_act, 1)
                    elif s == 1:
                        act.activation(xq8[:, u, :], ps[:, 0:UQ], ACT.Copy, saturate=False).then_inc(evac_act, 1)
                    elif s == 5:
                        act.activation(xb[:, u, :], ps[:, 0:UQ], ACT.Copy).then_inc(evac_act, 1)
                    else:
                        act.activation(xnT[:, u, :], ps[:, 0:UQ], ACT.Copy).then_inc(evac_act, 1)
                elif kind == "q":
                    _, l, u = item
                    ps = filled(act, item)
                    if l == 3:
                        act.activation(xnT[:, u, :], ps[:, 0:UQ], ACT.Copy).then_inc(evac_act, 1)
                    else:
                        act.activation(xnT[:, u, :], ps[:, 0:UQ], ACT.Identity,
                                       bias=colv(f"bq{l}")).then_inc(evac_act, 1)
                elif kind == "X":
                    k = nth(*item) - 1
                    act.wait_ge(scores_taken, 3 * k + 3)
                    act.activation(probs[:, k % 3, :], probs[:, k % 3, :], ACT.Exp).then_inc(exp_ready, 1)
                elif kind == "T":
                    _, l, u, i = item
                    k = nth(*item) - 1
                    half = nth("PV", l, u) % 2
                    for g, (c0, c1) in enumerate(GROUPS):
                        act.wait_ge(pt_full, 3 * k + g + 1)
                        ps = TB[(3 * k + g) % 2]
                        n = CH[c1 - 1][1]
                        full = c1 - c0 if n == P else c1 - c0 - 1
                        ins = act.activation(PT[:, half, c0:c0 + full, i * P:(i + 1) * P],
                                             ps[:, 0:P * full].rearrange("p (c n) -> p c n", n=P), ACT.Copy)
                        if n < P:
                            ins = act.activation(PT[0:n, half, c1 - 1, i * P:(i + 1) * P],
                                                 ps[0:n, P * full:P * full + P], ACT.Copy)
                        ins.then_inc(pt_copied, 1)
                elif kind == "PV":
                    _, l, b = item
                    ps = filled(act, item)
                    if l == 1:
                        act.activation(oT[:, :], ps[:, 0:UQ], ACT.Copy).then_inc(evac_act, 1)
                    else:
                        act.activation(oT[:, :], ps[:, 0:UQ], ACT.Identity, bias=colv(f"bo{l}")).then_inc(evac_act, 1)
                elif kind == "f0":
                    ps = filled(act, item)
                    if nth_f(*item) > 1:
                        act.wait_ge(x_new, nth_f(*item) - 1)
                    act.activation(y16[:, :], ps[:, 0:UQ], ACT.Copy).then_inc(evac_act, 1)
                elif kind == "f2":
                    ps = filled(act, item)
                    act.wait_ge(x_new, nth_f(*item) - 1)
                    act.activation(y2, ps[:, 0:UQ], ACT.Copy, scale=sc[:, 1:2]).then_inc(evac_act, 1)
                elif kind == "r1":
                    act.wait_ge(h_ready, nth(*item))
                    act.activation(hr[:, item[1]], hr[:, item[1]], ACT.Gelu_apprx_tanh).then_inc(hg_ready, 1)
                elif kind == "r2":
                    ps = filled(act, item)
                    act.activation(hT, ps[0:64, :], ACT.Copy).then_inc(evac_act, 1)
                elif kind == "r3":
                    b = item[1]
                    act.wait_ge(gap_ready, nth(*item))
                    act.activation(m12[:, b, 3, :], m12[:, b, 2, :], ACT.Exp).then_inc(gap_exp, 1)
                elif kind in ("r4", "g2"):
                    ps = filled(act, item)
                    act.activation(selT[0:3 * E, item[1], :], ps[0:3 * E, :], ACT.Copy).then_inc(evac_act, 1)
                elif kind == "moe1":
                    _, b, e0, e1 = item
                    for e in range(e0, e1):
                        m = E * b + e
                        ps = filled(act, ("bc1", b, e))
                        if m >= 2:
                            act.wait_ge(ytmp_ready, m - 1)
                        act.activation(pbc[:, m % 2, :], ps[:, :], ACT.Copy).then_inc(evac_act, 1)
                        for j in range(FT):
                            n = FT * m + j
                            act.wait_ge(x12_full, n + 1)
                            if n >= 2:
                                act.wait_ge(g_ready, n - 1)
                            act.activation(gel[:, n % 2, :], SC[2 * (n % 2) + 1][:, :], ACT.Gelu_apprx_tanh,
                                           bias=colv("b1", 2 * FT * e + FT + j)).then_inc(gelu_ready, 1)
                            if j == 1 and m + 1 < B * E:
                                high_part(m + 1)
                elif kind == "wsplit":
                    act.wait_ge(ld_w1, 32)
                    filled(act, ("vp", 2, B - 1, 2))
                    high_part(0)
                elif kind == "moe3" and item[3] == E:
                    b = item[1]
                    for f in range(FT):
                        if f < FT - 1:
                            act.wait_ge(pre3_full, (FT - 1) * b + f + 1)
                        else:
                            act.wait_ge(mm3, E * (b + 1))
                        if b and f == 0:
                            filled(act, ("y3", b - 1))
                        act.activation(inter[:, f, :], SC[f][:, :], ACT.Gelu).then_inc(inter_ready, 1)
                elif kind == "y3":
                    ps = filled(act, item)
                    act.activation(yT3[:, item[1], :], ps[:, :], ACT.Identity, bias=colv("fbo3")).then_inc(evac_act, 1)

        @block.vector
        def _(dve):
            count = [0]
            stats = [0]

            def link(ins):
                count[0] += 1
                ins.then_inc(dve_chain, 1)
                dve.wait_ge(dve_chain, count[0])

            def round8(dst, u, t):
                link(dve.tensor_scalar(t.bitcast(I32), u.bitcast(I32), 0x7F800000, None, ALU.bitwise_and))
                link(dve.tensor_scalar(t, t, 2.0 ** -6, MAGIC, ALU.max, ALU.mult))
                link(dve.tensor_tensor(u, u, t, ALU.add))
                link(dve.tensor_tensor(u, u, t, ALU.subtract))
                link(dve.tensor_scalar(t, u, OVER8, 0.0, ALU.mult, ALU.mult))
                return dve.tensor_tensor(dst, u, t, ALU.add)

            def row_stats(src, tiles, eps):
                for t in tiles:
                    ins = dve.bn_stats(st[:, t, :], src(t))
                link(ins)
                for t in tiles:
                    ins = dve.bn_aggr(mv[:, t, :], st[:, t, :])
                link(ins)
                at = slice(tiles[0], tiles[-1] + 1)
                dve.tensor_scalar(ve[:, at], mv[:, at, 1], eps, None, ALU.add).then_inc(var_ready, 1)
                stats[0] += 1
                return stats[0]

            def normalise(dst, src, tiles, nth_stats):
                dve.wait_ge(rstd_ready, nth_stats)
                for t in tiles:
                    ins = dve.tensor_scalar(dst(t), src(t), mv[:, t, 0:1], rstd[:, t:t + 1],
                                            ALU.subtract, ALU.mult)
                return ins

            def unit(u):
                return range(u * UT, (u + 1) * UT)

            def update(tiles, y, gate):
                at = x[:, tiles[0]:tiles[-1] + 1, :].rearrange("p i n -> p (i n)")
                return dve.scalar_tensor_tensor(out=at, in0=y, scalar=gate, in1=at, op0=ALU.mult, op1=ALU.add)

            def over_experts(ap):
                return ap.rearrange("p (i a) -> p i a", a=1).broadcast_to([P, NT, E])

            dve.wait_ge(ld_row, 16)
            dve.wait_ge(gates_ready, 1)
            link(dve.tensor_tensor(tg[:, 9:10], tg[:, 0:1], tg[:, 8:9], ALU.mult))
            link(dve.reciprocal(sc[:, 0:1], rowv("s_in")))
            dve.tensor_tensor(sc[:, 1:2], rowv("s_in"), rowv("s_k"), ALU.mult)
            link(dve.reciprocal(sc[:, 2:3], rowv("s_k")))
            dve.wait_ge(ld_x, 16)
            pending = {}
            for item in ORDER:
                kind = item[0]
                if kind == "ln_stats":
                    _, s, u = item
                    src = xn if s == 0 else x
                    pending[u] = row_stats(lambda t: src[:, t, :], unit(u), 1e-5)
                elif kind == "ln_apply":
                    _, s, u = item
                    src = xn if s == 0 else x
                    if s > 0:
                        filled(dve, ("xt", s - 1, u))
                    ins = normalise(lambda t: xn[:, t, :], lambda t: src[:, t, :], unit(u), pending[u])
                    if s == -1:
                        link(ins)
                    else:
                        ins.then_inc(xn_ready, 1)
                elif kind == "kv0":
                    j = item[1]
                    ps = filled(dve, item + ("v",))
                    dve.wait_ge(kbd_zero, 1)
                    if j >= 2:
                        filled(dve, ("kp0", j - 2, "v"))
                    for hh in range(2):
                        last = dve.tensor_copy(vbd[64 * hh:64 * hh + 64, j % 2, hh, :],
                                               ps[64 * hh:64 * hh + 64, 0:B * SK])
                    last.then_inc(evac_dve, 1)
                elif kind == "kp0":
                    j = item[1]
                    ps = filled(dve, item + ("v",))
                    dve.tensor_copy(Vb[:, :, :].rearrange("p b (h k) -> p h b k", h=H)[:, 2 * j:2 * j + 2],
                                    ps[:, 0:4 * SK].rearrange("p (h b k) -> p h b k", h=2, b=B)
                                    ).then_inc(evac_dve, 1)
                elif kind == "conv8":
                    dve.wait_ge(ld_sqw, 16)
                    u, t = scr[:, 0, 0:P], scr[:, 1, 0:P]
                    link(dve.tensor_scalar(u, sq("w8T"), 448.0, -448.0, ALU.min, ALU.max))
                    round8(w8[:, :], u, t).then_inc(w8_ready, 1)
                    dve.wait_ge(w8_ready, 1)
                elif kind == "conv3":
                    dve.wait_ge(ld_b13, 16)
                    total3 = scr[:, 1, :]
                    third = [colv("third", r) for r in range(3)]
                    link(dve.tensor_copy(b13s[:, :], b13))
                    dve.tensor_scalar(total3, b13s[:, :], third[0], None, ALU.mult)
                    link(dve.tensor_tensor(b13, b13, b13s[:, :], ALU.subtract))
                    link(dve.tensor_copy(b13s[:, :], b13))
                    link(dve.scalar_tensor_tensor(out=total3, in0=b13s[:, :], scalar=third[1], in1=total3,
                                                  op0=ALU.mult, op1=ALU.add))
                    link(dve.tensor_tensor(b13, b13, b13s[:, :], ALU.subtract))
                    link(dve.scalar_tensor_tensor(out=b13s[:, :], in0=b13, scalar=third[2], in1=total3,
                                                  op0=ALU.mult, op1=ALU.add))
                    dve.wait_ge(ld_small, 64)
                    u, t = scr[:, 0, 0:P], scr[:, 1, 0:P]
                    link(dve.tensor_scalar(u, k8in[:, :], sc[:, 2:3], None, ALU.mult))
                    round8(k8[:, :], u, t).then_inc(w8_ready, 1)
                    dve.wait_ge(w8_ready, 2)
                elif kind == "kvT":
                    l = item[1]
                    ps = filled(dve, item)
                    if l >= 2:
                        dve.wait_ge(blocks_ready, 4 * (l - 1))
                    if l == 3:
                        dve.wait_ge(ld_small, 64)
                        link(dve.tensor_copy(mrow[:, :], mint[:, :]))
                        link(dve.tensor_scalar(keep3[:, :], mrow[:, :], 0.0, None, ALU.not_equal))
                    k_ps, v_ps = ps[:, 0:B * SK], ps[:, 256:256 + B * SK]
                    if l < 3:
                        dve.tensor_scalar(kvs[:, 0, :], k_ps, colv(f"bk{l}"), SCALE, ALU.add, ALU.mult)
                        dve.tensor_scalar(kvs[:, 1, :], v_ps, colv(f"bv{l}"), None, ALU.add).then_inc(evac_dve, 1)
                    else:
                        dve.scalar_tensor_tensor(out=kvs[:, 0, :], in0=k_ps, scalar=SCALE, in1=keep3[:, :],
                                                 op0=ALU.mult, op1=ALU.mult)
                        dve.tensor_copy(kvs[:, 1, :], v_ps).then_inc(evac_dve, 1)
                    if l in (1, 3):
                        if l == 1:
                            link(dve.tensor_scalar(mrow[:, :], rowv("mask1"), -3e38, 3e38, ALU.max, ALU.min))
                        else:
                            dve.wait_ge(mask_ready, B)
                            link(dve.tensor_scalar(mrow[:, :], keep3[:, :], 1e9, -1e9, ALU.mult, ALU.add))
                        link(dve.tensor_copy(msplit[:, 0, :], mrow[:, :]))
                        link(dve.tensor_tensor(mrow[:, :], mrow[:, :], msplit[:, 0, :], ALU.subtract))
                        link(dve.tensor_copy(msplit[:, 1, :], mrow[:, :]))
                        link(dve.tensor_tensor(mrow[:, :], mrow[:, :], msplit[:, 1, :], ALU.subtract))
                        for r in range(2):
                            dve.tensor_copy(msel[32 * r:32 * r + 32, :], msplit[32 * r:32 * r + 32, r, :])
                        dve.tensor_copy(msel[64:P, :], mrow[64:P, :]).then_inc(mask_split, 1)
                elif kind == "S":
                    k = nth(*item) - 1
                    r = k % 3
                    for c, (h0, h1) in enumerate(HEADS):
                        dve.wait_ge(scores_full, 3 * k + c + 1)
                        ins = dve.tensor_reduce(mx[:, r, h0:h1], bank(item[1:], c)[:, 0:SK * (h1 - h0)]
                                                .rearrange("p (h k) -> p h k", k=SK), AX.X, ALU.max)
                    link(ins)
                    if k >= 3:
                        dve.wait_ge(pt_full, 3 * (k - 2))
                    for c, (h0, h1) in enumerate(HEADS):
                        dve.tensor_tensor(
                            probs[:, r, SK * h0:SK * h1].rearrange("p (h k) -> p h k", k=SK),
                            bank(item[1:], c)[:, 0:SK * (h1 - h0)].rearrange("p (h k) -> p h k", k=SK),
                            mx[:, r, h0:h1].rearrange("p (h a) -> p h a", a=1).broadcast_to([P, h1 - h0, SK]),
                            ALU.subtract).then_inc(scores_taken, 1)
                elif kind == "N":
                    k = nth(*item) - 1
                    r = k % 3
                    dve.wait_ge(exp_ready, k + 1)
                    link(dve.tensor_reduce(den[:, r, :], probs[:, r, :].rearrange("p (h k) -> p h k", k=SK),
                                           AX.X, ALU.add))
                    dve.reciprocal(rden[:, r, :], den[:, r, :]).then_inc(rden_ready, 1)
                elif kind == "back":
                    _, l, u = item
                    ps = filled(dve, item)
                    update(unit(u), ps[:, 0:UQ], tg[:, 9:10] if l == 0 else tg[:, l:l + 1]).then_inc(evac_dve, 1)
                    emptied(dve, item)
                elif kind in ("f0", "f2"):
                    u = item[1]
                    emptied(dve, item)
                    if kind == "f0":
                        yy = scr[:, 0, 0:UQ]
                        link(dve.tensor_tensor(yy.rearrange("p (i n) -> p i n", n=P),
                                               y16[:, :].rearrange("p (i n) -> p i n", n=P),
                                               over_tiles(rowv("fb0"), P), ALU.add))
                        update(unit(u), yy, tg[:, 4:5]).then_inc(x_new, 1)
                    else:
                        link(dve.tensor_tensor(y2.rearrange("p (i n) -> p i n", n=P),
                                               y2.rearrange("p (i n) -> p i n", n=P),
                                               over_tiles(fb2[:, :], P), ALU.add))
                        update(unit(u), y2, tg[:, 6:7]).then_inc(x_new, 1)
                    dve.wait_ge(x_new, nth_f(*item))
                elif kind == "quant":
                    u = item[1]
                    emptied(dve, ("xt", 5, u))
                    link(dve.tensor_scalar(scr[:, 0, 0:UQ], xb[:, u, :], sc[:, 0:1], None, ALU.mult))
                    round8(xb[:, u, :], scr[:, 0, 0:UQ], scr[:, 1, 0:UQ]).then_inc(quant_ready, 1)
                elif kind == "r1":
                    b = item[1]
                    ps = filled(dve, item)
                    dve.tensor_tensor(hr[:, b], ps[:, 0:NT * 64].rearrange("p (i n) -> p i n", n=64),
                                      over_tiles(rowv("br1"), 64, NT), ALU.add).then_inc(evac_dve, 1)
                    emptied(dve, item)
                    rows = lambda t: hr[:, b, t % NT, :]
                    n = row_stats(rows, range(b * NT, (b + 1) * NT), 1e-6)
                    link(normalise(rows, rows, range(b * NT, (b + 1) * NT), n))
                    link(dve.tensor_tensor(hr[:, b], hr[:, b], over_tiles(rowv("lns"), 64, NT), ALU.mult))
                    dve.tensor_tensor(hr[:, b], hr[:, b], over_tiles(rowv("lnb"), 64, NT), ALU.add).then_inc(h_ready, 1)
                elif kind in ("r3", "g1"):
                    b = item[1]
                    ps = filled(dve, item)
                    logits = ps[:, 0:NT * E].rearrange("p (i e) -> p i e", e=E)
                    rank = over_tiles(rowv("rank"), E, NT)

                    def first_max(v, best, dst, tmp):
                        link(dve.tensor_reduce(best, v, AX.X, ALU.max))
                        link(dve.tensor_tensor(dst, v, over_experts(best), ALU.is_equal))
                        link(dve.tensor_tensor(dst, dst, rank, ALU.mult))
                        link(dve.tensor_reduce(tmp, dst, AX.X, ALU.max))
                        return dve.tensor_tensor(dst, dst, over_experts(tmp), ALU.is_equal)

                    if kind == "r3":
                        dve.tensor_tensor(lg[:, b], logits, over_tiles(rowv("br2"), E, NT), ALU.add).then_inc(evac_dve, 1)
                    else:
                        dve.tensor_copy(lg[:, b], logits).then_inc(evac_dve, 1)
                    emptied(dve, item)
                    m = [m12[:, b, q, :] for q in range(8)]
                    link(first_max(lg[:, b], m[0], oh[:, 0], m[1]))
                    if kind == "r3":
                        link(dve.scalar_tensor_tensor(out=lg[:, b], in0=oh[:, 0], scalar=-3e38, in1=lg[:, b],
                                                      op0=ALU.mult, op1=ALU.add))
                        link(first_max(lg[:, b], m[4], oh[:, 1], m[1]))
                        dve.tensor_tensor(m[2], m[4], m[0], ALU.subtract).then_inc(gap_ready, 1)
                    else:
                        for part in range(3):
                            ins = dve.tensor_copy(s24[:, b, :, part, :], oh[:, 0])
                        ins.then_inc(sel_ready, 1)
                elif kind == "xsplit":
                    b = item[1]
                    emptied(dve, ("xt", 3, (b + 1) * U // B - 1))
                    dve.wait_ge(pt_full, 3 * nth("T", 1, U // B + b, 1 - b))
                    link(dve.tensor_copy(x_hi[b], batch(xnT, b)))
                    dve.tensor_tensor(x_lo[b], batch(xnT, b), x_hi[b].bitcast(F32), ALU.subtract).then_inc(x_split, 1)
                elif kind == "r3b":
                    b = item[1]
                    m = [m12[:, b, q, :] for q in range(8)]
                    dve.wait_ge(gap_exp, nth(*item))
                    link(dve.tensor_scalar(m[5], m[3], 1.0, None, ALU.add))
                    link(dve.reciprocal(m[6], m[5]))
                    link(dve.tensor_tensor(m[7], m[3], m[6], ALU.mult))
                    link(dve.tensor_tensor(oh[:, 0], oh[:, 0], over_experts(m[6]), ALU.mult))
                    link(dve.tensor_tensor(oh[:, 1], oh[:, 1], over_experts(m[7]), ALU.mult))
                    link(dve.tensor_tensor(oh[:, 0], oh[:, 0], oh[:, 1], ALU.add))
                    for part in range(3):
                        link(dve.tensor_copy(sbf[:, :, :], oh[:, 0]))
                        ins = dve.tensor_copy(s24[:, b, :, part, :], sbf[:, :, :])
                        if part < 2:
                            link(ins)
                            link(dve.tensor_tensor(oh[:, 0], oh[:, 0], s24[:, b, :, part, :], ALU.subtract))
                    ins.then_inc(sel_ready, 1)
                elif kind == "moe1":
                    _, b, e0, e1 = item
                    taken = USE["bc1", b, e0][2]

                    def expert(e, par, first):
                        for j in range(FT):
                            dve.wait_ge(gelu_ready, FT * e + (FT * E * b + j + 1))
                            if not (first and b == 0 and j < 2):
                                dve.wait_ge(y_step, FT * e + (FT * E * b + j - 1))
                            dve.scalar_tensor_tensor(out=gg[:, j % 2, :], in0=SC[2 * (j % 2)][:, :],
                                                     scalar=col[:, bass.ds(e * 2 * FT + (COL["b1"][0] + j), 1)],
                                                     in1=gel[:, j % 2, :], op0=ALU.add,
                                                     op1=ALU.mult).then_inc(g_ready, 1)
                        dve.wait_ge(y_step, FT * e + (FT * E * b + FT))
                        dve.wait_ge(evac_act, e + (taken - e0))
                        if not (b == 0 and e0 < 2):
                            dve.wait_ge(acc_done, e + (E * b - 1))
                        dve.scalar_tensor_tensor(out=ytmp[:, par, :], in0=TB[par][:, :],
                                                 scalar=col[:, bass.ds(e + COL["b2"][0], 1)], in1=pbc[:, par, :],
                                                 op0=ALU.add, op1=ALU.mult).then_inc(ytmp_ready, 1)

                    if e1 - e0 > 1:
                        with dve.Fori(e0, e1, 2) as e:
                            expert(e, 0, False)
                            expert(e + 1, 1, False)
                    else:
                        expert(e0, e0 % 2, e0 == 0)
                elif kind == "back1":
                    u = item[1]
                    ps = filled(dve, item)
                    update(unit(u), ps[:, 0:UQ], tg[:, 5:6]).then_inc(evac_dve, 1)
                    emptied(dve, item)
                elif kind == "moe3":
                    b = item[1]
                    for e in masked(*item[2:]):
                        n = E * b + e
                        ps = filled(dve, ("bc3", b, e))
                        if n >= 2:
                            dve.wait_ge(mm3, n - 1)
                        dve.scalar_tensor_tensor(out=xm[:, n % 2, :], in0=ps[:, :], scalar=1.0, in1=batch(xnT, b),
                                                 op0=ALU.min, op1=ALU.mult).then_inc(evac_dve, 1)
                elif kind == "z3":
                    b = item[1]
                    ps = filled(dve, item)
                    dve.tensor_tensor(zz[:, b], ps[:, :].rearrange("p (i n) -> p i n", n=P),
                                      xn[:, b * NT:(b + 1) * NT, :], ALU.add).then_inc(evac_dve, 1)
                    emptied(dve, item)
                elif kind == "norm3":
                    b = item[1]
                    tiles = range(b * NT, (b + 1) * NT)
                    rows = lambda t: zz[:, b, t % NT, :]
                    n = row_stats(rows, tiles, 1e-12)
                    for t in tiles:
                        ins = dve.scalar_tensor_tensor(out=rows(t), in0=rows(t), scalar=mv[:, t, 0:1],
                                                       in1=rowv("gamma"), op0=ALU.subtract, op1=ALU.mult)
                    link(ins)
                    dve.wait_ge(rstd_ready, n)
                    for t in tiles:
                        ins = dve.scalar_tensor_tensor(out=rows(t), in0=rows(t), scalar=rstd[:, t:t + 1],
                                                       in1=rowv("beta"), op0=ALU.mult, op1=ALU.add)
                    link(ins)
                    update(tiles, zz[:, b].rearrange("p i n -> p (i n)"), tg[:, 7:8]).then_inc(out_ready, 1)

        @block.tensor
        def _(pe):
            pe.wait_ge(ld_ident, 16)
            pe.wait_ge(ld_kv, 16)
            for item in ORDER:
                kind = item[0]
                if kind == "kv0":
                    j = item[1]
                    if j % 2 == 0:
                        pe.wait_ge(ld_kvj[j // 2], 16)
                    for which in "kv":
                        ps = acquire(pe, item + (which,))
                        pe.matmul(ps[:, 0:B * SK], weight0(which, j), ctxT,
                                  start=True, stop=True).then_inc(misc_full, 1)
                elif kind == "kp0":
                    j = item[1]
                    for which, w, src in (("k", "q", kbd), ("v", "out", vbd)):
                        ps = acquire(pe, item + (which,))
                        emptied(pe, ("kv0", j, which))
                        pe.matmul(ps[:, 0:4 * SK], weight0(w, j), src[:, j % 2].rearrange("p h n -> p (h n)"),
                                  start=True, stop=True).then_inc(misc_full, 1)
                elif kind == "vp":
                    _, l, b, g = item
                    c0, c1 = GROUPS[g]
                    ps = acquire(pe, item)
                    if l == 0:
                        emptied(pe, ("kp0", 7, "v"))
                    else:
                        pe.wait_ge(blocks_ready, 4 * (l - 1) + b + 1)
                    for c in range(c0, c1):
                        k0, n = CH[c]
                        dst = ps[0:n, P * (c - c0):P * (c - c0) + P]
                        src = Vb[:, b, k0:k0 + n]
                        if l < 2:
                            ins = pe.transpose(dst, src, ident)
                        else:
                            ins = pe.matmul(dst, src, sq(f"wo{l}"), start=True, stop=True)
                    ins.then_inc(misc_full, 1)
                elif kind == "xt":
                    _, s, u = item
                    ps = acquire(pe, item)
                    pe.wait_ge(xn_ready, nth("ln_apply", s, u) - U)
                    for i in range(UT):
                        ins = pe.transpose(ps[:, i * P:(i + 1) * P], xn[:, u * UT + i, :], ident)
                    ins.then_inc(misc_full, 1)
                elif kind == "q":
                    _, l, u = item
                    ps = acquire(pe, item)
                    emptied(pe, ("xt", 2 * l, u))
                    pe.matmul(ps[:, 0:UQ], sq(f"wq{l}"), xnT[:, u, :], start=True, stop=True).then_inc(misc_full, 1)
                elif kind == "kvT":
                    l = item[1]
                    ps = acquire(pe, item)
                    pe.wait_ge(ld_sqw, 16)
                    pe.matmul(ps[:, 0:B * SK], sq(f"wk{l}"), ctxT, start=True, stop=True)
                    pe.matmul(ps[:, 256:256 + B * SK], sq(f"wv{l}"), ctxT,
                              start=True, stop=True).then_inc(misc_full, 1)
                elif kind == "S":
                    _, l, u, i = item
                    k = nth(*item) - 1
                    if i == 0:
                        emptied(pe, ("q", l, u) if l else ("xt", 0, u))
                    if l == 0 and k == 0:
                        emptied(pe, ("kp0", 7, "k"))
                    if l and u == 0 and i == 0:
                        pe.wait_ge(blocks_ready, 4 * l)
                        if l in (1, 3):
                            pe.wait_ge(mask_ready, B * (l + 1) // 2)
                        if l == 2:
                            pe.wait_ge(g_ready, B * E * FT)
                    q = xnT[:, u, i * P:(i + 1) * P]
                    for c, (h0, h1) in enumerate(HEADS):
                        n = 3 * k + c
                        if n >= 4:
                            pe.wait_ge(scores_taken, n - 3)
                        dst = bank(item[1:], c)[:, 0:SK * (h1 - h0)]
                        masked = l in (1, 3)
                        ins = pe.matmul(dst, q, Kp[l % 2][:, u * B // U, SK * h0:SK * h1], start=True, stop=not masked)
                        if masked:
                            ins = pe.matmul(dst, ones3[:, :], maskrow[:, u * B // U, SK * h0:SK * h1], start=False, stop=True)
                        ins.then_inc(scores_full, 1)
                elif kind == "T":
                    _, l, u, i = item
                    k = nth(*item) - 1
                    pe.wait_ge(probs_ready, k + 1)
                    if l == 2 and u == 0 and i == 0:
                        pe.wait_ge(ytmp_ready, B * E)
                    for g, (c0, c1) in enumerate(GROUPS):
                        n = 3 * k + g
                        if n >= 2:
                            pe.wait_ge(pt_copied, n - 1)
                        for c in range(c0, c1):
                            k0, m = CH[c]
                            ins = pe.transpose(TB[n % 2][0:m, P * (c - c0):P * (c - c0) + P],
                                               probs[:, k % 3, k0:k0 + m], ident)
                        ins.then_inc(pt_full, 1)
                elif kind == "PV":
                    _, l, u = item
                    ps = acquire(pe, item)
                    emptied(pe, ("vp", l, u * B // U, 2))
                    half = nth(*item) % 2
                    starts = [c0 for c0, _ in GROUPS]
                    for c, (k0, m) in enumerate(CH):
                        if c in starts:
                            pe.wait_ge(pt_copied, 3 * (nth("T", l, u, UT - 1) - 1) + starts.index(c) + 1)
                        ins = pe.matmul(ps[:, 0:UQ], Vp[0:m, l % 2, u * B // U, c, :], PT[0:m, half, c, :],
                                        start=(c == 0), stop=(c == len(CH) - 1))
                    ins.then_inc(misc_full, 1)
                elif kind == "back":
                    _, l, u = item
                    ps = acquire(pe, item)
                    emptied(pe, ("PV", l, u))
                    for i in range(UT):
                        ins = pe.transpose(ps[:, i * P:(i + 1) * P], oT[:, i * P:(i + 1) * P], ident)
                    ins.then_inc(misc_full, 1)
                elif kind in ("f0", "f2"):
                    u = item[1]
                    ps = acquire(pe, item)
                    pe.wait_ge(w8_ready, 1 if kind == "f0" else 2)
                    if kind == "f0":
                        emptied(pe, ("xt", 1, u))
                    else:
                        pe.wait_ge(quant_ready, nth("quant", u))
                    src, w = (xq8, w8) if kind == "f0" else (xb, k8)
                    for i in range(UT):
                        ins = pe.matmul(ps[:, i * P:(i + 1) * P], src[:, u, i * P:(i + 1) * P], w[:, :],
                                        start=True, stop=True)
                    ins.then_inc(misc_full, 1)
                elif kind in ("r1", "g1"):
                    b = item[1]
                    ps = acquire(pe, item)
                    emptied(pe, ("xt", 3 if kind == "r1" else 7, (b + 1) * U // B - 1))
                    w, n = (sq("wr1"), 64) if kind == "r1" else (sq("wrT3"), E)
                    for i in range(NT):
                        ins = pe.matmul(ps[:, i * n:(i + 1) * n], batch(xnT, b)[:, i * P:(i + 1) * P], w,
                                        start=True, stop=True)
                    ins.then_inc(misc_full, 1)
                elif kind == "r2":
                    b = item[1]
                    ps = acquire(pe, item)
                    pe.wait_ge(hg_ready, nth("r1", b))
                    for i in range(NT):
                        ins = pe.transpose(ps[0:64, i * P:(i + 1) * P], hr[:, b, i, :], ident)
                    ins.then_inc(misc_full, 1)
                elif kind == "r3":
                    b = item[1]
                    ps = acquire(pe, item)
                    emptied(pe, ("r2", b))
                    for i in range(NT):
                        ins = pe.matmul(ps[:, i * E:(i + 1) * E], hT[:, i * P:(i + 1) * P], sq("wr2")[0:64, :],
                                        start=True, stop=True)
                    ins.then_inc(misc_full, 1)
                elif kind in ("r4", "g2"):
                    b = item[1]
                    ps = acquire(pe, item)
                    pe.wait_ge(sel_ready, nth("g1", b) + B if kind == "g2" else nth("r3", b))
                    for i in range(NT):
                        ins = pe.transpose(ps[0:3 * E, i * P:(i + 1) * P],
                                           s24[:, b, i].rearrange("p t e -> p (t e)"), ident)
                    ins.then_inc(misc_full, 1)
                elif kind == "moe1":
                    _, b, e0, e1 = item

                    def up(n):
                        e, j = divmod(n - FT * E * b, FT)
                        if n >= 2:
                            pe.wait_ge(g_ready, n - 1)
                        if j == 0:
                            pe.wait_ge(w_split, E * b + e + 1)
                        for half in range(2):
                            at = slice(half * F1 + j * P, half * F1 + (j + 1) * P)
                            hi, lo = w_hi[:, e % 2, at], w_lo[:, e % 2, at]
                            dst = SC[2 * (n % 2) + half][:, :]
                            pe.matmul(dst, hi, x_hi[b], start=True, stop=False)
                            pe.matmul(dst, hi, x_lo[b], start=False, stop=False)
                            ins = pe.matmul(dst, lo, x_hi[b], start=False, stop=True)
                        ins.then_inc(x12_full, 1)

                    if e0 == 0:
                        if b == 0:
                            pe.wait_ge(ld_w1, 32)
                            pe.wait_ge(ld_small, 64)
                            pe.wait_ge(scores_taken, 3 * nth("S", 1, U - 1, UT - 1))
                            pe.wait_ge(pt_copied, 3 * nth("T", 1, U - 1, UT - 1))
                        pe.wait_ge(x_split, b + 1)
                        up(FT * E * b)
                    for e in range(e0, e1):
                        m = E * b + e
                        ps = acquire(pe, ("bc1", b, e))
                        emptied(pe, ("r4", b))
                        pe.matmul(ps[:, :], esel[:, e, :], selT[:, b, :], start=True,
                                  stop=True).then_inc(misc_full, 1)
                        for j in range(FT):
                            n = FT * m + j
                            if not (e == E - 1 and j == FT - 1):
                                up(n + 1)
                            pe.wait_ge(g_ready, n + 1)
                            if j == 0 and m >= 2:
                                pe.wait_ge(ytmp_ready, m - 1)
                            pe.matmul(TB[m % 2][:, :], w2[:, e, j, :], gg[:, n % 2, :], start=(j == 0),
                                      stop=(j == FT - 1)).then_inc(y_step, 1)
                elif kind == "back1":
                    u = item[1]
                    ps = acquire(pe, item)
                    b, within = divmod(u * UQ, SQ)
                    pe.wait_ge(acc_done, E * (b + 1))
                    for i in range(UT):
                        at = within + i * P
                        ins = pe.transpose(ps[:, i * P:(i + 1) * P], acc[:, b, at:at + P], ident)
                    ins.then_inc(misc_full, 1)
                elif kind == "moe3":
                    _, b, e0, e1 = item
                    if b == 0 and e0 == 0:
                        pe.wait_ge(ld_w3, 32)
                        pe.wait_ge(scores_taken, 3 * nth("S", 3, U - 1, UT - 1))

                    def share(e):
                        ps = acquire(pe, ("bc3", b, e))
                        pe.matmul(ps[:, :], esel[:, e, :], selT[:, b, :], start=True,
                                  stop=True).then_inc(misc_full, 1)

                    emptied(pe, ("g2", b))
                    if e0 == 0:
                        share(0)
                        for f in range(FT):
                            if b:
                                pe.wait_ge(inter_ready, f + 1)
                            pe.matmul(SC[f][:, :], b13s[:, f * P:(f + 1) * P], selT[:, b, :],
                                      start=True, stop=False)
                    for e in range(e0, e1):
                        if e + 1 < E:
                            share(e + 1)
                        emptied(pe, ("bc3", b, e))
                        for f in range(FT):
                            ins = pe.matmul(SC[f][:, :], w3[:, e, f * P:(f + 1) * P], xm[:, e % 2, :],
                                            start=False, stop=(e == E - 1))
                            if e == E - 1 and f < FT - 1:
                                ins.then_inc(pre3_full, 1)
                        ins.then_inc(mm3, 1)
                elif kind == "y3":
                    b = item[1]
                    ps = acquire(pe, item)
                    for f in range(FT):
                        pe.wait_ge(inter_ready, FT * b + f + 1)
                        ins = pe.matmul(ps[:, :], wo3[:, f, :], inter[:, f, :], start=(f == 0), stop=(f == FT - 1))
                    ins.then_inc(misc_full, 1)
                elif kind == "z3":
                    b = item[1]
                    ps = acquire(pe, item)
                    emptied(pe, ("y3", b))
                    for i in range(NT):
                        ins = pe.transpose(ps[:, i * P:(i + 1) * P], yT3[:, b, i * P:(i + 1) * P], ident)
                    ins.then_inc(misc_full, 1)


def nth_f(*item):
    return [i for i in ORDER if i[0] in ("f0", "f2")].index(item) + 1


def kernel(**inputs):
    import numpy as _np
    import concourse.bacc as _bacc
    from concourse import mybir as _mybir
    from concourse.bass_utils import run_bass_kernel_spmd as _run

    a = {k: _np.asarray(v) for k, v in inputs.items()}
    f32 = _np.float32

    def tiles(w):
        n = w.shape[0] // P
        return w.reshape(n, P, w.shape[1]).transpose(1, 0, 2).reshape(P, n * w.shape[1])

    def padded(w, rows=P):
        z = _np.zeros((rows,) + w.shape[1:], w.dtype)
        z[: w.shape[0]] = w
        return z

    wkv = a["L0_xattn_w_kv"]
    four = [wkv[:, :1024], wkv[:, 1024:], tiles(a["L0_xattn_w_q"].T), tiles(a["L0_xattn_w_out"])]
    kvp = _np.concatenate([a["ctx_1024"].reshape(B * SK, P).T]
                          + [w[:, j * P:(j + 1) * P] for j in range(8) for w in four], axis=1)
    eye = _np.eye(P, dtype=f32)
    sqwp = _np.concatenate(
        [eye, a["L0_ffn_weight"].T, a["L1_xattn_Wq"], a["L1_xattn_Wk"], a["L1_xattn_Wv"]]
        + [a[f"L{l}_xattn_W{n}"].T for l in (2, 3) for n in "qkvo"]
        + [a["L1_ffn_Wr1"], padded(a["L1_ffn_Wr2"]), a["L3_ffn_Wr"].T], axis=1)
    heads = _np.zeros((P, H), f32)
    for h in range(H):
        heads[8 * h:8 * h + 8, h] = 1.0
    third = _np.zeros((P, 3), f32)
    for r in range(3):
        third[E * r:E * r + E, r] = 1.0
    vec = ["L0_xattn_ln_gamma", "L0_xattn_ln_beta", "L0_xattn_b_out", "L1_xattn_bq", "L1_xattn_bk", "L1_xattn_bv",
           "L2_xattn_bq", "L2_xattn_bk", "L2_xattn_bv", "L2_xattn_bo", "L3_xattn_bo", "L3_ffn_bo"]
    colp = _np.concatenate([a[n].reshape(P, 1) for n in vec]
                           + [a["L1_ffn_b2"].T, a["L1_ffn_b1"].reshape(E, 2 * FT, P).transpose(2, 0, 1)
                              .reshape(P, 2 * FT * E), heads, third], axis=1)
    rowp = _np.concatenate([a["L0_ffn_bias"], a["L1_ffn_br1"], a["L1_ffn_ln_scale"], a["L1_ffn_ln_bias"],
                            a["L1_ffn_br2"], a["L3_ffn_gamma"], a["L3_ffn_beta"], a["g_xattn"], a["g_ffn"],
                            a["L0_xattn_gate"], a["L2_ffn_input_scale"], a["L2_ffn_kernel_scale"],
                            a["mask_Bx1x1xS2_ff0"].reshape(-1), _np.arange(E, 0, -1).astype(f32)]).reshape(1, -1)
    sel = _np.zeros((P, E, P), f32)
    for e in range(E):
        for r in range(3):
            sel[E * r + e, e, :] = 1.0
    bf = a["L2_ffn_kernel"].dtype
    arrays = {
        "x_in": a["x"].reshape(B * NT, P, P).transpose(1, 0, 2),
        "kv_in": kvp, "sqw_in": sqwp, "col_in": colp, "row_in": rowp,
        "w1_in": a["L1_ffn_W1"].transpose(1, 0, 2),
        "w2_in": a["L1_ffn_W2"].reshape(E, FT, P, P).transpose(2, 0, 1, 3),
        "w3_in": a["L3_ffn_W1"].transpose(1, 0, 2),
        "wo3_in": a["L3_ffn_Wo"].reshape(FT, P, P).transpose(1, 0, 2),
        "b13_in": padded(_np.concatenate([a["L3_ffn_b1"]] * 3, axis=0)),
        "mask3_in": a["mask_BxS2_ik0"].reshape(1, -1),
        "k8_in": a["L2_ffn_kernel"], "fb2_in": a["L2_ffn_bias"].reshape(1, -1),
        "esel_in": sel.astype(bf),
    }
    arrays = {k: _np.ascontiguousarray(v) for k, v in arrays.items()}
    nc = _bacc.Bacc("TRN2", target_bir_lowering=False, num_devices=1)
    args = [nc.dram_tensor(k, v.shape, _mybir.dt.from_np(v.dtype), kind="ExternalInput").ap()
            for k, v in arrays.items()]
    out = nc.dram_tensor("out", (P, B * NT, P), _mybir.dt.float32, kind="ExternalOutput").ap()
    build(nc, *args, out)
    r = _run(nc, [arrays], core_ids=[0])
    return r.results[0]["out"].transpose(1, 0, 2).reshape(B, SQ, P)
```

```python
from contextlib import ExitStack

import numpy as np

import concourse.bass as bass
from concourse import mybir

F32 = mybir.dt.float32
F32R = mybir.dt.float32r
BF16 = mybir.dt.bfloat16
F16 = mybir.dt.float16
FP8 = mybir.dt.float8e4
I32 = mybir.dt.int32
ALU = mybir.AluOpType
ACT = mybir.ActivationFunctionType
AX = mybir.AxisListType

P = 128
B = 2
NT = 4
SQ = NT * P
U = 4
UT = B * NT // U
UQ = UT * P
SK = 77
H = 16
HK = H * SK
NL = 4
HEADS = [(0, 5), (5, 10), (10, 16)]
HALVES = [(0, SK * HEADS[1][1]), (SK * HEADS[1][1], HK)]
CH = [(c, min(P, HK - c)) for c in range(0, HK, P)]
GROUPS = [(0, 4), (4, 8), (8, 10)]
E = 8
F1 = 512
FT = F1 // P
SCALE0 = 64 ** -0.5
SCALE = 8 ** -0.5
MAGIC = 1.5 * 2.0 ** 20
OVER8 = 7.3e35

KV = {}
SQW = {}
COL = {}
ROW = {}


def _place(table, names):
    at = 0
    for name, width in names:
        table[name] = (at, at + width)
        at += width
    return at


KV_N = _place(KV, [("ctxT", B * SK)] + [(f"j{j}", 4 * P) for j in range(8)])
SQW_N = _place(SQW, [("ident", P), ("w8T", P), ("wq1", P), ("wk1", P), ("wv1", P)]
               + [(f"w{n}{l}", P) for l in (2, 3) for n in "qkvo"] + [("wr1", 64), ("wr2", E), ("wrT3", E)])
COL_N = _place(COL, [(n, 1) for n in ("ln_g", "ln_b", "bo0", "bq1", "bk1", "bv1", "bq2", "bk2", "bv2", "bo2",
                                      "bo3", "fbo3")]
               + [("b2", E), ("b1", 2 * FT * E), ("headmask", H), ("third", 3)])
ROW_N = _place(ROW, [("fb0", P), ("br1", 64), ("lns", 64), ("lnb", 64), ("br2", E), ("gamma", P), ("beta", P),
                     ("gates", 9), ("s_in", 1), ("s_k", 1), ("mask1", B * SK), ("rank", E)])

ORDER = []


def _order():
    o = ORDER

    def stats(s, u):
        return [("ln_stats", s, u)]

    def apply(s, u):
        return [("ln_apply", s, u), ("xt", s, u)]

    def first_norms(u):
        return [stats(-1, u), [("ln_apply", -1, u)] + stats(0, u), [("ln_apply", 0, u)]]

    steps = first_norms(0) + first_norms(1) + first_norms(2)[:2]
    steps[3].append(("xt", 0, 0))
    steps[6].append(("xt", 0, 1))
    o.append(("kv0", 0))
    for j in range(8):
        if j + 1 < 8:
            o.append(("kv0", j + 1))
        o.append(("kp0", j))
        if steps:
            o.extend(steps.pop(0))

    def between(l, u):
        s = 2 * l + 1
        at = {(1, "v"): [("PV", l, u)], (1, "t"): [("backT", l, u)], (1, "c"): [("back", l, u)] + stats(s, u),
              (2, "a"): apply(s, u)}
        if l in (0, 2):
            if l == 0:
                at[2, "b"] = [("f0", u)] + stats(s + 1, u)
                at[3, "a"] = [("ln_apply", s + 1, u)]
                at[3, "b"] = [("xt", s + 1, u)]
                at[4, "t"] = [("q", l + 1, u)]
            else:
                at[2, "b"] = [("quant", u)]
                at[3, "b"] = [("f2", u)] + stats(s + 1, u)
                at[4, "a"] = [("ln_apply", s + 1, u)]
                at[4, "b"] = [("xt", s + 1, u)]
                at[5, "e"] = [("q", l + 1, u)]
        elif u % (U // B) != U // B - 1:
            at[2, "a"] = [("ln_apply", s, u)]
            at[3, "b"] = [("xt", s, u)]
        else:
            b = u // (U // B)
            if l == 1:
                at[2, "b"] = [("r1", b), ("r1b", b)]
                at[3, "a"] = [("r2", b)]
                at[3, "b"] = [("r3", b), ("r3x", b), ("xsplit", b)]
                at[4, "a"] = [("r3b", b)]
                at[5, "e"] = [("r4", b)]
                if b == 0:
                    at[4, "b"] = [("wsplit",)]
            else:
                at[2, "b"] = [("g1", b)]
                at[3, "a"] = [("g2", b), ("xsplit3", b)]
        return at

    def prepare(l, k0):
        late = 1 if l == 1 else 0
        at = {(late, "a"): [("kvT", l)], (late, "b"): [("blk", l, 1, 0)], (1 + late, "b"): [("blk", l, 1, 1)],
              (2 + late, "b"): [("blk", l, 0, 0)], (4, "b"): [("blk", l, 0, 1)]}
        for n in range(6):
            k = min(2 + late + n, 7)
            at[k, "e"] = at.get((k, "e"), []) + [("vp", l, n // 3, n % 3)]
        if l in (1, 3):
            for b in range(B):
                at[5 + b, "b"] = [("mrow", l, b)]
        if l == NL - 1:
            del at[0, "a"]
        return {(k0 + k, slot): items for (k, slot), items in at.items()}

    def attentions(layers, plan):
        tiles = [(l, u, i) for l in layers for u in range(U) for i in range(UT)]

        def add(stages, k0=0):
            for (k, slot), items in stages.items():
                plan[k0 + k, slot] = plan.get((k0 + k, slot), []) + items

        if layers[0] == 0:
            add({(0, "a"): [("vp", 0, b, g) for b in range(B) for g in range(3)]})
            third, fourth = first_norms(2), first_norms(3)
            add({(0, "b"): third[2], (1, "e"): [("xt", 0, 2)], (1, "b"): fourth[0], (2, "b"): fourth[1],
                 (3, "b"): fourth[2], (4, "e"): [("xt", 0, 3)]})
        for n, l in enumerate(layers):
            if l == NL - 1:
                for part in range(4):
                    add({(n * U * UT + 2 * part, "b"): [("w3split", part)]})
            if l + 1 < NL:
                add(prepare(l + 1, n * U * UT))
            if n == 0 and l:
                for u in range(U):
                    add({(max(2 * u - 1, -1), "b"): [("q", l, u)]})
            for u in range(U):
                add(between(l, u), (n * U + u) * UT + UT)
        o.extend(plan.pop((-1, "b"), []))
        for k in range(len(tiles) + 1):
            if k < len(tiles):
                o.append(("S", *tiles[k]))
            values = plan.pop((k, "v"), [])
            if values:
                o.extend([("X", *tiles[k])] if k < len(tiles) else [])
                o.extend(values)
            if k:
                o.append(("T", *tiles[k - 1]))
            o.extend(plan.pop((k, "t"), []))
            o.extend(plan.pop((k, "e"), []))
            if k < len(tiles) and not values:
                o.append(("X", *tiles[k]))
            o.extend(plan.pop((k, "a"), []))
            if k < len(tiles):
                o.append(("N", *tiles[k]))
            o.extend(plan.pop((k, "c"), []))
            o.extend(plan.pop((k, "b"), []))
            if k == 1 and layers[0] == 0:
                o.append(("conv8",))
        slots = ("v", "t", "e", "a", "c", "b")
        left = [[i for i in plan[n] if i[0] != "backT"]
                for n in sorted(plan, key=lambda n: (n[0], slots.index(n[1])))]
        for items in left:
            for i in [i for i in items if i[0] == "back"]:
                items.insert(items.index(i), ("backT",) + i[1:])
        return [items for items in left if items]

    def weave(segments, chains):
        for segment in segments:
            if chains:
                o.extend(chains.pop(0))
            o.append(segment)
        for items in chains:
            o.extend(items)

    def belongs(item, b):
        return (item[-1] if item[0][0] in "rg" or item[0][:6] == "xsplit" else item[-1] // (U // B)) == b

    rest = attentions([0, 1], {})
    while rest and any(belongs(i, 0) for items in rest for i in items):
        o.extend(rest.pop(0))
    u = U - 1
    weave([("moe1", 0, e, e + 1) for e in range(E)],
          [[], [("xt", 3, u - 1), ("backT", 1, u), ("back", 1, u)] + stats(3, u), apply(3, u) + [("convk",)],
           [("r1", 1)], [("r1b", 1)], [("r2", 1), ("r3", 1)], [("xsplit", 1), ("r3x", 1)], [("r3b", 1)]])
    o.append(("r4", 1))
    weave([("moe1", 1, 0, 1), ("moe1", 1, 1, 2), ("moe1", 1, 2, 3), ("moe1", 1, 3, 4), ("moe1", 1, 4, 8)],
          [[], [("back1", 0)] + stats(4, 0) + [("back1", 1)] + stats(4, 1), apply(4, 0) + apply(4, 1),
           [("conv3a",)], [("conv3b",), ("kvT", 3)]])
    rest = attentions([2, 3], {(0, "a"): [("back1", 2)] + stats(4, 2) + [("back1", 3)] + stats(4, 3),
                               (0, "b"): [("ln_apply", 4, 2)], (1, "a"): [("ln_apply", 4, 3)],
                               (1, "e"): [("xt", 4, 2)], (1, "b"): [("xt", 4, 3)]})
    while rest and any(belongs(i, 0) for items in rest for i in items):
        o.extend(rest.pop(0))
    weave([("moe3", 0, 0, 2), ("moe3", 0, 2, 4), ("moe3", 0, 4, 6), ("moe3", 0, 6, 8)], rest)
    o.extend([("y3", 0), ("moe3", 1, 0, 4), ("z3", 0), ("moe3", 1, 4, 8), ("norm3", 0), ("y3", 1), ("z3", 1),
              ("norm3", 1)])


_order()


def nth(*item):
    return [i for i in ORDER if i[0] == item[0]].index(item) + 1


def masked(e0, e1):
    return range(e0 + (e0 > 0), min(e1 + 1, E))


USES = []
for _i in ORDER:
    _k = _i[0]
    if _k in ("xt", "q", "PV", "r2", "r4", "g2", "f0", "f2", "vp", "y3"):
        USES.append((_i, "act"))
    elif _k == "backT":
        USES.append((_i, "back"))
    elif _k in ("r1", "r3", "g1", "back1", "z3", "kvT"):
        USES.append((_i, "dve"))
    elif _k in ("kv0", "kp0"):
        USES.append((_i + ("k",), "act"))
        USES.append((_i + ("v",), "dve"))
    elif _k == "moe1":
        for _e in range(*_i[2:]):
            USES.append((("bc1", _i[1], _e), "act"))
    elif _k == "moe3":
        for _e in masked(*_i[2:]):
            USES.append((("bc3", _i[1], _e), "dve"))
BANK = {}
_last = {}
_shared = 0
for _u, _ in USES:
    if _u[0] == "kv0":
        _bank = ("scores", 2 * (_u[1] % 2) + (_u[2] == "v"))
    else:
        _bank = ("general", _shared % 2)
        _shared += 1
    BANK[_u] = (_bank, _last.get(_bank))
    _last[_bank] = _u
USE = {u: (k, eng, [v[1] for v in USES[:k + 1]].count(eng)) for k, (u, eng) in enumerate(USES)}


def build(nc, x_in, kv_in, sqw_in, col_in, row_in, w1_in, w2_in, w3_in, wo3_in, b13_in, mask3_in, k8_in,
          fb2_in, esel_in, out):
    with ExitStack() as ctx:
        def sb(name, shape, dt=F32):
            return ctx.enter_context(nc.sbuf_tensor(name, shape, dt))

        def sem(name):
            return ctx.enter_context(nc.semaphore(name))

        x = sb("x", [P, B * NT, P])
        xn = sb("xn", [P, B * NT, P])
        xnT = sb("xnT", [P, U, UQ])
        oT = sb("oT", [P, UQ])
        scr = sb("scr", [P, 2, SQ])
        Kp = [sb("Kp0", [P, B, HK]), None]
        Vp = sb("Vp", [P, 2, B, len(CH), P])
        PT = sb("PT", [P, 2, len(CH), UQ])
        kv = sb("kv", [P, KV_N])
        sqw = sb("sqw", [P, SQW_N])
        col = sb("col", [P, COL_N])
        row = sb("row", [P, ROW_N])
        with ExitStack() as first_experts:
            w1 = first_experts.enter_context(nc.sbuf_tensor("w1", [P, E, 2 * F1], F32))
        w3_hi = sb("w3_hi", [P, E, F1], F32R)
        w3_lo = sb("w3_lo", [P, E, F1], F32R)
        w2 = sb("w2", [P, E, FT, P])
        esel = sb("esel", [P, E, P], BF16)
        kvs = sb("kvs", [P, 2, B * SK])
        ones3 = sb("ones3", [P, P], BF16)
        maskrow = sb("maskrow", [P, B, HK], BF16)
        mrow = sb("mrow", [P, B * SK])
        msplit = sb("msplit", [P, 2, B * SK], BF16)
        msel = sb("msel", [P, B * SK], BF16)
        mint = sb("mint", [P, B * SK], I32)
        keep3 = sb("keep3", [P, B * SK])
        w8 = sb("w8", [P, P], BF16)
        k8in = sb("k8in", [P, P], BF16)
        k8 = sb("k8", [P, P], BF16)
        fb2 = sb("fb2", [P, P], BF16)
        xb = sb("xb", [P, U, UQ], BF16)
        xq8 = xb[:, 0:U // 2, :].rearrange("p u n -> p (u n)").bitcast(FP8).rearrange("p (u n) -> p u n", u=U)
        y16 = sb("y16", [P, UQ], F16)
        y2 = y16[:, :].bitcast(BF16)
        selT = sb("selT", [P, B, SQ], BF16)
        b13s = sb("b13s", [P, F1], BF16)
        tg = sb("tg", [P, 10])
        st = sb("st", [P, B * NT, 6])
        mv = sb("mv", [P, B * NT, 2])
        ve = sb("ve", [P, B * NT])
        rstd = sb("rstd", [P, B * NT])
        mhalf = sb("mhalf", [P, NT])
        mx = sb("mx", [P, 3, H])
        den = sb("den", [P, 3, H])
        rden = sb("rden", [P, 3, H])
        sc = sb("sc", [P, 4])
        lg = sb("lg", [P, B, NT, E])
        oh = sb("oh", [P, 2, NT, E])
        s24 = sb("s24", [P, B, NT, 3, E])
        sbf = sb("sbf", [P, NT, E], BF16)
        m12 = sb("m12", [P, B, 8, NT])

        ffa = PT[:, :, :, :].rearrange("p r c n -> p (r c n)")
        gel = ffa[:, 0:2 * SQ].rearrange("p (r n) -> p r n", r=2)
        gg = ffa[:, 2 * SQ:4 * SQ].rearrange("p (r n) -> p r n", r=2)
        pbc = ffa[:, 4 * SQ:6 * SQ].rearrange("p (r n) -> p r n", r=2)
        ytmp = ffa[:, 6 * SQ:8 * SQ].rearrange("p (r n) -> p r n", r=2)
        acc = ffa[:, 8 * SQ:10 * SQ].rearrange("p (r n) -> p r n", r=2)
        inter = ffa[:, 0:FT * SQ].rearrange("p (f n) -> p f n", f=FT)
        yT3 = ffa[:, 6 * SQ:8 * SQ].rearrange("p (r n) -> p r n", r=2)
        zz = ffa[:, 8 * SQ:10 * SQ].rearrange("p (r i n) -> p r i n", r=2, i=NT)
        nbd = 2 * 2 * B * SK
        kbd = ffa[:, 0:nbd].rearrange("p (r h n) -> p r h n", r=2, h=2)
        vbd = ffa[:, nbd:2 * nbd].rearrange("p (r h n) -> p r h n", r=2, h=2)
        b13 = scr[:, 0, :]
        hr = scr[:, 0, :].rearrange("p (b i n) -> p b i n", b=B, i=NT)
        hT = scr[0:64, 1, :]
        w3 = kv[:, 0:E * F1].rearrange("p (e f) -> p e f", e=E)
        wo3 = sb("wo3", [P, FT, P])

        with ExitStack() as attention:
            place = lambda name, shape: attention.enter_context(nc.sbuf_tensor(name, shape, F32))
            Vb = place("Vb", [P, B, HK])
            Kp[1] = place("Kp1", [P, B, HK])
            probs = place("probs", [P, 3, HK])
        w_hi = sb("w_hi", [P, 2, 2 * F1], F32R)
        sb("gap_v", [P, B * HK - 4 * F1])
        w_lo = sb("w_lo", [P, 2, 2 * F1], F32R)
        sb("gap_k", [P, B * HK - 4 * F1 + HK])
        x_part = sb("x_part", [P, B, HK], F32R)
        x_hi = [x_part[:, b, 0:SQ] for b in range(B)]
        x_lo = [x_part[:, b, SQ:2 * SQ] for b in range(B)]
        x3_hi, x3_lo = w_lo[:, :, 0:SQ], w_lo[:, :, SQ:2 * SQ]
        xm_hi, xm_lo = w_hi[:, :, 0:SQ], w_hi[:, :, SQ:2 * SQ]

        SC = [ctx.enter_context(nc.psum_tensor(f"SC{i}", [P, 512], F32)) for i in range(4)]
        TB = [ctx.enter_context(nc.psum_tensor(f"TB{i}", [P, 512], F32)) for i in range(2)]
        MB = [ctx.enter_context(nc.psum_tensor(f"MB{i}", [P, 512], F32)) for i in range(2)]

        ld_x = sem("ld_x")
        ld_kv = sem("ld_kv")
        ld_kvj = [sem(f"ld_kv{j}") for j in range(4)]
        ld_ident = sem("ld_ident")
        ld_b13 = sem("ld_b13")
        ld_sqw = sem("ld_sqw")
        ld_col = sem("ld_col")
        ld_row = sem("ld_row")
        ld_small = sem("ld_small")
        ld_w1 = sem("ld_w1")
        ld_w3 = sem("ld_w3")
        w_high = sem("w_high")
        w_split = sem("w_split")
        x_split = sem("x_split")
        w3_high = sem("w3_high")
        w3_split = sem("w3_split")
        x3_split = sem("x3_split")
        const_ready = sem("const_ready")
        misc_full = sem("misc_full")
        evac_act = sem("evac_act")
        evac_dve = sem("evac_dve")
        evac_back = sem("evac_back")
        dve_chain = sem("dve_chain")
        gates_ready = sem("gates_ready")
        var_ready = sem("var_ready")
        rstd_ready = sem("rstd_ready")
        xn_ready = sem("xn_ready")
        x_new = sem("x_new")
        w8_ready = sem("w8_ready")
        mask_split = sem("mask_split")
        mask_ready = sem("mask_ready")
        kbd_zero = sem("kbd_zero")
        blocks_ready = sem("blocks_ready")
        scores_full = sem("scores_full")
        scores_taken = sem("scores_taken")
        exp_ready = sem("exp_ready")
        rden_ready = sem("rden_ready")
        probs_ready = sem("probs_ready")
        pt_full = sem("pt_full")
        pt_copied = sem("pt_copied")
        quant_ready = sem("quant_ready")
        y_rounded = sem("y_rounded")
        h_ready = sem("h_ready")
        hg_ready = sem("hg_ready")
        gap_ready = sem("gap_ready")
        gap_exp = sem("gap_exp")
        sel_ready = sem("sel_ready")
        x12_full = sem("x12_full")
        gelu_ready = sem("gelu_ready")
        g_ready = sem("g_ready")
        y_step = sem("y_step")
        ytmp_ready = sem("ytmp_ready")
        acc_done = sem("acc_done")
        pre3_full = sem("pre3_full")
        inter_ready = sem("inter_ready")
        mm3 = sem("mm3")
        out_ready = sem("out_ready")
        stored = sem("stored")

        ctxT = kv[:, 0:KV["ctxT"][1]]

        def weight0(name, j):
            at = KV[f"j{j}"][0] + P * ["k", "v", "q", "out"].index(name)
            return kv[:, at:at + P]

        def sq(name):
            return sqw[:, SQW[name][0]:SQW[name][1]]

        def colv(name, i=0):
            return col[:, COL[name][0] + i:COL[name][0] + i + 1]

        def rowv(name):
            return row[:, ROW[name][0]:ROW[name][1]]

        def over_tiles(ap, n, tiles=UT):
            return ap.rearrange("p (a n) -> p a n", a=1).broadcast_to([P, tiles, n])

        def batch(ap, b):
            return ap[:, b * U // B:(b + 1) * U // B, :].rearrange("p u n -> p (u n)")

        ident = sq("ident")
        def bank(item, c):
            return SC[(3 * (nth("S", *item) - 1) + c) % 4]

        def bank_of(key):
            (where, n), _ = BANK[key]
            return SC[n] if where == "scores" else MB[n]

        def acquire(pe, key):
            _, before = BANK[key]
            if before:
                emptied(pe, before)
            return bank_of(key)

        def emptied(eng, key):
            _, who, n = USE[key]
            eng.wait_ge({"act": evac_act, "dve": evac_dve, "back": evac_back}[who], n)

        def filled(eng, key):
            k, _, _ = USE[key]
            eng.wait_ge(misc_full, k + 1)
            return bank_of(key)

        block = ctx.enter_context(nc.Block())

        @block.sync
        def _(sp):
            sp.dma_start(x[:, :, :], x_in).then_inc(ld_x, 16)
            sp.dma_start(kv[:, 0:KV["j0"][0]], kv_in[:, 0:KV["j0"][0]]).then_inc(ld_kv, 16)
            for j in range(0, 8, 2):
                at = slice(KV[f"j{j}"][0], KV[f"j{j + 1}"][1])
                sp.dma_start(kv[:, at], kv_in[:, at]).then_inc(ld_kvj[j // 2], 16)
            sp.dma_start(sqw[:, P:], sqw_in[:, P:]).then_inc(ld_sqw, 16)
            emptied(sp, ("kv0", 1, "v"))
            sp.dma_start(w1[:, :, :], w1_in).then_inc(ld_w1, 16)
            sp.dma_start(w2[:, :, :, :], w2_in).then_inc(ld_w1, 16)
            sp.dma_start(wo3[:, :, :], wo3_in).then_inc(ld_w3, 16)
            emptied(sp, ("r4", B - 1))
            sp.dma_start(b13, b13_in).then_inc(ld_b13, 16)
            emptied(sp, ("kp0", 7, "v"))
            emptied(sp, ("kvT", 3))
            sp.dma_start(w3[:, :, :], w3_in).then_inc(ld_w3, 16)
            for b in range(B):
                sp.wait_ge(out_ready, b + 1)
                sp.dma_start(out[:, b * NT:(b + 1) * NT], x[:, b * NT:(b + 1) * NT, :]).then_inc(stored, 16)
            sp.wait_ge(stored, 16 * B)

        @block.gpsimd
        def _(pool):
            pool.memset(mhalf[:, :], -0.5)
            pool.memset(kbd[:, :, :, :], 0.0)
            pool.memset(vbd[:, :, :, :], 0.0).then_inc(kbd_zero, 1)
            pool.memset(maskrow[:, :, :], 0.0)
            pool.memset(selT[:, :, :], 0.0)
            pool.memset(ones3[:, :], 0.0).then_inc(const_ready, 1)
            pool.wait_ge(const_ready, 1)
            for r in range(3):
                pool.memset(ones3[32 * r:32 * r + 1, :], 1.0).then_inc(const_ready, 1)
                pool.wait_ge(const_ready, r + 2)
            stats = 0

            def low_part(m):
                pool.wait_ge(w_high, m + 1)
                if m >= 2:
                    pool.wait_ge(x12_full, FT * (m - 1))
                pool.tensor_tensor(w_lo[:, m % 2], w1[:, m % E, :], w_hi[:, m % 2].bitcast(F32),
                                   ALU.subtract).then_inc(w_split, 1)

            for item in ORDER:
                kind = item[0]
                if kind in ("ln_stats", "r1", "norm3"):
                    n = UT if kind == "ln_stats" else NT
                    at = slice(item[-1] * n, (item[-1] + 1) * n)
                    stats += 1
                    pool.wait_ge(var_ready, stats)
                    pool.tensor_tensor(rstd[:, at], ve[:, at], mhalf[:, 0:n], ALU.pow).then_inc(rstd_ready, 1)
                elif kind == "N":
                    k = nth(*item) - 1
                    pool.wait_ge(rden_ready, k + 1)
                    pv = probs[:, k % 3, :].rearrange("p (h k) -> p h k", h=H)
                    pool.tensor_tensor(pv, pv, rden[:, k % 3, :].rearrange("p (h a) -> p h a", a=1)
                                       .broadcast_to([P, H, SK]), ALU.mult).then_inc(probs_ready, 1)
                elif kind == "blk":
                    _, l, which, b = item
                    emptied(pool, ("kvT", l))
                    if which == 0 and l >= 2:
                        pool.wait_ge(scores_full, 3 * nth("S", l - 2, U - 1, UT - 1))
                    if which == 1:
                        filled(pool, ("vp", l - 1, 1, 2))
                    dst = (Kp[l % 2], Vb)[which]
                    pool.tensor_tensor(
                        dst[:, b, :].rearrange("p (h k) -> p h k", h=H),
                        kvs[:, which, b * SK:(b + 1) * SK].rearrange("p (a k) -> p a k", a=1)
                        .broadcast_to([P, H, SK]),
                        col[:, COL["headmask"][0]:COL["headmask"][1]].rearrange("p (h a) -> p h a", a=1)
                        .broadcast_to([P, H, SK]), ALU.mult).then_inc(blocks_ready, 1)
                elif kind == "moe1":
                    _, b, e0, e1 = item

                    def add(e, par, first):
                        pool.wait_ge(ytmp_ready, e + (E * b + 1))
                        if first:
                            pool.tensor_copy(acc[:, b, :], ytmp[:, par, :]).then_inc(acc_done, 1)
                        else:
                            pool.wait_ge(acc_done, e + E * b)
                            pool.tensor_tensor(acc[:, b, :], acc[:, b, :], ytmp[:, par, :],
                                               ALU.add).then_inc(acc_done, 1)

                    for e in range(e0, e1):
                        if E * b + e + 1 < B * E:
                            low_part(E * b + e + 1)
                        add(e, e % 2, e == 0)
                elif kind == "w3split":
                    at = slice(item[1] * E // 4, (item[1] + 1) * E // 4)
                    pool.wait_ge(w3_high, item[1] + 1)
                    pool.tensor_tensor(w3_lo[:, at, :], w3[:, at, :], w3_hi[:, at, :].bitcast(F32),
                                       ALU.subtract).then_inc(w3_split, 1)
                elif kind == "wsplit":
                    pool.wait_ge(scores_full, 3 * nth("S", 1, U - 1, UT - 1))
                    low_part(0)

        @block.scalar
        def _(act):
            act.dma_start(sqw[:, 0:P], sqw_in[:, 0:P]).then_inc(ld_ident, 16)
            act.dma_start(col[:, :], col_in).then_inc(ld_col, 16)
            act.dma_start(row[:, :], row_in.partition_broadcast(P)).then_inc(ld_row, 16)
            act.dma_start(mint[:, :], mask3_in.partition_broadcast(P)).then_inc(ld_small, 16)
            act.dma_start(k8in[:, :], k8_in).then_inc(ld_small, 16)
            act.dma_start(fb2[:, :], fb2_in.partition_broadcast(P)).then_inc(ld_small, 16)
            act.dma_start(esel[:, :, :], esel_in).then_inc(ld_small, 16)
            act.wait_ge(ld_row, 16)
            act.activation(tg[:, 0:9], rowv("gates"), ACT.Tanh).then_inc(gates_ready, 1)
            act.wait_ge(ld_col, 16)

            def high_part(m):
                act.activation(w_hi[:, m % 2], w1[:, m % E, :], ACT.Copy).then_inc(w_high, 1)

            for item in ORDER:
                kind = item[0]
                if kind == "kv0":
                    j = item[1]
                    ps = filled(act, item + ("k",))
                    act.wait_ge(kbd_zero, 1)
                    if j >= 2:
                        filled(act, ("kp0", j - 2, "k"))
                    for hh in range(2):
                        last = act.activation(kbd[64 * hh:64 * hh + 64, j % 2, hh, :],
                                              ps[64 * hh:64 * hh + 64, 0:B * SK], ACT.Copy, scale=SCALE0)
                    last.then_inc(evac_act, 1)
                elif kind == "kp0":
                    j = item[1]
                    ps = filled(act, item + ("k",))
                    act.activation(
                        Kp[0][:, :, :].rearrange("p b (h k) -> p h b k", h=H)[:, 2 * j:2 * j + 2],
                        ps[:, 0:4 * SK].rearrange("p (h b k) -> p h b k", h=2, b=B), ACT.Copy).then_inc(evac_act, 1)
                elif kind == "vp":
                    _, l, b, g = item
                    c0, c1 = GROUPS[g]
                    ps = filled(act, item)
                    if l >= 2:
                        filled(act, ("PV", l - 2, U - 1))
                    n = min(P, CH[c1 - 1][1])
                    if n == P:
                        act.activation(Vp[:, l % 2, b, c0:c1, :], ps[:, 0:P * (c1 - c0)]
                                       .rearrange("p (c n) -> p c n", n=P), ACT.Copy).then_inc(evac_act, 1)
                    else:
                        act.activation(Vp[:, l % 2, b, c0:c1 - 1, :], ps[:, 0:P * (c1 - c0 - 1)]
                                       .rearrange("p (c n) -> p c n", n=P), ACT.Copy)
                        act.activation(Vp[0:n, l % 2, b, c1 - 1, :], ps[0:n, P * (c1 - c0 - 1):P * (c1 - c0)],
                                       ACT.Copy).then_inc(evac_act, 1)
                elif kind == "xt":
                    _, s, u = item
                    ps = filled(act, item)
                    if s == 0:
                        act.activation(xnT[:, u, :], ps[:, 0:UQ], ACT.Identity, bias=colv("ln_b"),
                                       scale=colv("ln_g")).then_inc(evac_act, 1)
                    elif s == 1:
                        act.activation(xq8[:, u, :], ps[:, 0:UQ], ACT.Copy, saturate=False).then_inc(evac_act, 1)
                    elif s == 5:
                        act.activation(xb[:, u, :], ps[:, 0:UQ], ACT.Copy).then_inc(evac_act, 1)
                    else:
                        act.activation(xnT[:, u, :], ps[:, 0:UQ], ACT.Copy).then_inc(evac_act, 1)
                elif kind == "q":
                    _, l, u = item
                    ps = filled(act, item)
                    if l == 3:
                        act.activation(xnT[:, u, :], ps[:, 0:UQ], ACT.Copy).then_inc(evac_act, 1)
                    else:
                        act.activation(xnT[:, u, :], ps[:, 0:UQ], ACT.Identity,
                                       bias=colv(f"bq{l}")).then_inc(evac_act, 1)
                elif kind == "X":
                    k = nth(*item) - 1
                    for c, (k0, k1) in enumerate(HALVES):
                        act.wait_ge(scores_taken, 3 * k + 2 + c)
                        act.activation(probs[:, k % 3, k0:k1], probs[:, k % 3, k0:k1],
                                       ACT.Exp).then_inc(exp_ready, 1)
                elif kind == "T":
                    _, l, u, i = item
                    k = nth(*item) - 1
                    half = nth("PV", l, u) % 2
                    for g, (c0, c1) in enumerate(GROUPS):
                        act.wait_ge(pt_full, 3 * k + g + 1)
                        ps = TB[(3 * k + g) % 2]
                        n = CH[c1 - 1][1]
                        full = c1 - c0 if n == P else c1 - c0 - 1
                        ins = act.activation(PT[:, half, c0:c0 + full, i * P:(i + 1) * P],
                                             ps[:, 0:P * full].rearrange("p (c n) -> p c n", n=P), ACT.Copy)
                        if n < P:
                            ins = act.activation(PT[0:n, half, c1 - 1, i * P:(i + 1) * P],
                                                 ps[0:n, P * full:P * full + P], ACT.Copy)
                        ins.then_inc(pt_copied, 1)
                elif kind == "PV":
                    _, l, b = item
                    ps = filled(act, item)
                    if l == 1:
                        act.activation(oT[:, :], ps[:, 0:UQ], ACT.Copy).then_inc(evac_act, 1)
                    else:
                        act.activation(oT[:, :], ps[:, 0:UQ], ACT.Identity, bias=colv(f"bo{l}")).then_inc(evac_act, 1)
                elif kind == "f0":
                    ps = filled(act, item)
                    if nth_f(*item) > 1:
                        act.wait_ge(x_new, nth_f(*item) - 1)
                    act.activation(y16[:, :], ps[:, 0:UQ], ACT.Copy).then_inc(evac_act, 1)
                elif kind == "f2":
                    ps = filled(act, item)
                    act.wait_ge(x_new, nth_f(*item) - 1)
                    act.activation(y2, ps[:, 0:UQ], ACT.Copy, scale=sc[:, 1:2]).then_inc(evac_act, 1)
                elif kind == "r1b":
                    act.wait_ge(h_ready, nth(*item))
                    act.activation(hr[:, item[1]], hr[:, item[1]], ACT.Gelu_apprx_tanh).then_inc(hg_ready, 1)
                elif kind == "r2":
                    ps = filled(act, item)
                    act.activation(hT, ps[0:64, :], ACT.Copy).then_inc(evac_act, 1)
                elif kind == "r3x":
                    b = item[1]
                    act.wait_ge(gap_ready, nth(*item))
                    act.activation(m12[:, b, 3, :], m12[:, b, 2, :], ACT.Exp).then_inc(gap_exp, 1)
                elif kind in ("r4", "g2"):
                    ps = filled(act, item)
                    act.activation(selT[0:3 * E, item[1], :], ps[0:3 * E, :], ACT.Copy).then_inc(evac_act, 1)
                elif kind == "moe1":
                    _, b, e0, e1 = item
                    for e in range(e0, e1):
                        m = E * b + e
                        for j in range(FT):
                            n = FT * m + j
                            act.wait_ge(x12_full, n + 1)
                            if n >= 2:
                                act.wait_ge(g_ready, n - 1)
                            act.activation(gel[:, n % 2, :], SC[2 * (n % 2) + 1][:, :], ACT.Gelu_apprx_tanh,
                                           bias=colv("b1", 2 * FT * e + FT + j)).then_inc(gelu_ready, 1)
                            if j == 0:
                                ps = filled(act, ("bc1", b, e))
                                if m >= 2:
                                    act.wait_ge(ytmp_ready, m - 1)
                                act.activation(pbc[:, m % 2, :], ps[:, :], ACT.Copy).then_inc(evac_act, 1)
                            elif j == 1 and m + 1 < B * E:
                                high_part(m + 1)
                elif kind == "mrow":
                    _, l, b = item
                    act.wait_ge(mask_split, (l + 1) // 2)
                    if l == 3 and b == 0:
                        act.wait_ge(scores_full, 3 * nth("S", 1, U - 1, UT - 1))
                    act.activation(maskrow[:, b, :].rearrange("p (h k) -> p h k", h=H),
                                     msel[:, b * SK:(b + 1) * SK].rearrange("p (a k) -> p a k", a=1)
                                     .broadcast_to([P, H, SK]), ACT.Copy).then_inc(mask_ready, 1)
                elif kind == "w3split":
                    at = slice(item[1] * E // 4, (item[1] + 1) * E // 4)
                    act.wait_ge(ld_w3, 32)
                    act.wait_ge(x12_full, B * E * FT)
                    act.activation(w3_hi[:, at, :], w3[:, at, :], ACT.Copy).then_inc(w3_high, 1)
                elif kind == "wsplit":
                    act.wait_ge(ld_w1, 32)
                    filled(act, ("vp", 2, B - 1, 2))
                    high_part(0)
                elif kind == "moe3" and item[3] == E:
                    b = item[1]
                    for f in range(FT):
                        if f < FT - 1:
                            act.wait_ge(pre3_full, (FT - 1) * b + f + 1)
                        else:
                            act.wait_ge(mm3, E * (b + 1))
                        if b and f == 0:
                            filled(act, ("y3", b - 1))
                        act.activation(inter[:, f, :], SC[f][:, :], ACT.Gelu).then_inc(inter_ready, 1)
                elif kind == "y3":
                    ps = filled(act, item)
                    act.activation(yT3[:, item[1], :], ps[:, :], ACT.Identity, bias=colv("fbo3")).then_inc(evac_act, 1)

        @block.vector
        def _(dve):
            count = [0]
            stats = [0]

            def link(ins):
                count[0] += 1
                ins.then_inc(dve_chain, 1)
                dve.wait_ge(dve_chain, count[0])

            def round8(dst, u, t):
                link(dve.tensor_scalar(t.bitcast(I32), u.bitcast(I32), 0x7F800000, None, ALU.bitwise_and))
                link(dve.tensor_scalar(t, t, 2.0 ** -6, MAGIC, ALU.max, ALU.mult))
                link(dve.tensor_tensor(u, u, t, ALU.add))
                link(dve.tensor_tensor(u, u, t, ALU.subtract))
                link(dve.tensor_scalar(t, u, OVER8, 0.0, ALU.mult, ALU.mult))
                return dve.tensor_tensor(dst, u, t, ALU.add)

            def row_stats(src, tiles, eps):
                for t in tiles:
                    ins = dve.bn_stats(st[:, t, :], src(t))
                link(ins)
                for t in tiles:
                    ins = dve.bn_aggr(mv[:, t, :], st[:, t, :])
                link(ins)
                at = slice(tiles[0], tiles[-1] + 1)
                dve.tensor_scalar(ve[:, at], mv[:, at, 1], eps, None, ALU.add).then_inc(var_ready, 1)
                stats[0] += 1
                return stats[0]

            def normalise(dst, src, tiles, nth_stats):
                dve.wait_ge(rstd_ready, nth_stats)
                for t in tiles:
                    ins = dve.tensor_scalar(dst(t), src(t), mv[:, t, 0:1], rstd[:, t:t + 1],
                                            ALU.subtract, ALU.mult)
                return ins

            def unit(u):
                return range(u * UT, (u + 1) * UT)

            def update(tiles, y, gate):
                at = x[:, tiles[0]:tiles[-1] + 1, :].rearrange("p i n -> p (i n)")
                return dve.scalar_tensor_tensor(out=at, in0=y, scalar=gate, in1=at, op0=ALU.mult, op1=ALU.add)

            def over_experts(ap):
                return ap.rearrange("p (i a) -> p i a", a=1).broadcast_to([P, NT, E])

            dve.wait_ge(ld_row, 16)
            dve.wait_ge(gates_ready, 1)
            link(dve.tensor_tensor(tg[:, 9:10], tg[:, 0:1], tg[:, 8:9], ALU.mult))
            link(dve.reciprocal(sc[:, 0:1], rowv("s_in")))
            dve.tensor_tensor(sc[:, 1:2], rowv("s_in"), rowv("s_k"), ALU.mult)
            link(dve.reciprocal(sc[:, 2:3], rowv("s_k")))
            dve.wait_ge(ld_x, 16)
            pending = {}
            for item in ORDER:
                kind = item[0]
                if kind == "ln_stats":
                    _, s, u = item
                    src = xn if s == 0 else x
                    pending[u] = row_stats(lambda t: src[:, t, :], unit(u), 1e-5)
                elif kind == "ln_apply":
                    _, s, u = item
                    src = xn if s == 0 else x
                    if s > 0:
                        filled(dve, ("xt", s - 1, u))
                    ins = normalise(lambda t: xn[:, t, :], lambda t: src[:, t, :], unit(u), pending[u])
                    if s == -1:
                        link(ins)
                    else:
                        ins.then_inc(xn_ready, 1)
                elif kind == "kv0":
                    j = item[1]
                    ps = filled(dve, item + ("v",))
                    dve.wait_ge(kbd_zero, 1)
                    if j >= 2:
                        filled(dve, ("kp0", j - 2, "v"))
                    for hh in range(2):
                        last = dve.tensor_copy(vbd[64 * hh:64 * hh + 64, j % 2, hh, :],
                                               ps[64 * hh:64 * hh + 64, 0:B * SK])
                    last.then_inc(evac_dve, 1)
                elif kind == "kp0":
                    j = item[1]
                    ps = filled(dve, item + ("v",))
                    dve.tensor_copy(Vb[:, :, :].rearrange("p b (h k) -> p h b k", h=H)[:, 2 * j:2 * j + 2],
                                    ps[:, 0:4 * SK].rearrange("p (h b k) -> p h b k", h=2, b=B)
                                    ).then_inc(evac_dve, 1)
                elif kind == "conv8":
                    dve.wait_ge(ld_sqw, 16)
                    u, t = scr[:, 0, 0:P], scr[:, 1, 0:P]
                    link(dve.tensor_scalar(u, sq("w8T"), 448.0, -448.0, ALU.min, ALU.max))
                    round8(w8[:, :], u, t).then_inc(w8_ready, 1)
                    dve.wait_ge(w8_ready, 1)
                elif kind == "conv3a":
                    dve.wait_ge(ld_b13, 16)
                    total3 = scr[:, 1, :]
                    third = [colv("third", r) for r in range(3)]
                    link(dve.tensor_copy(b13s[:, :], b13))
                    dve.tensor_scalar(total3, b13s[:, :], third[0], None, ALU.mult)
                    link(dve.tensor_tensor(b13, b13, b13s[:, :], ALU.subtract))
                elif kind == "conv3b":
                    total3 = scr[:, 1, :]
                    third = [colv("third", r) for r in range(3)]
                    link(dve.tensor_copy(b13s[:, :], b13))
                    link(dve.scalar_tensor_tensor(out=total3, in0=b13s[:, :], scalar=third[1], in1=total3,
                                                  op0=ALU.mult, op1=ALU.add))
                    link(dve.tensor_tensor(b13, b13, b13s[:, :], ALU.subtract))
                    link(dve.scalar_tensor_tensor(out=b13s[:, :], in0=b13, scalar=third[2], in1=total3,
                                                  op0=ALU.mult, op1=ALU.add))
                elif kind == "convk":
                    dve.wait_ge(ld_small, 64)
                    u, t = scr[:, 0, 0:P], scr[:, 1, 0:P]
                    link(dve.tensor_scalar(u, k8in[:, :], sc[:, 2:3], None, ALU.mult))
                    round8(k8[:, :], u, t).then_inc(w8_ready, 1)
                    dve.wait_ge(w8_ready, 2)
                elif kind == "kvT":
                    l = item[1]
                    ps = filled(dve, item)
                    if l >= 2:
                        dve.wait_ge(blocks_ready, 4 * (l - 1))
                    if l == 3:
                        dve.wait_ge(ld_small, 64)
                        link(dve.tensor_copy(mrow[:, :], mint[:, :]))
                        link(dve.tensor_scalar(keep3[:, :], mrow[:, :], 0.0, None, ALU.not_equal))
                    k_ps, v_ps = ps[:, 0:B * SK], ps[:, 256:256 + B * SK]
                    if l < 3:
                        dve.tensor_scalar(kvs[:, 0, :], k_ps, colv(f"bk{l}"), SCALE, ALU.add, ALU.mult)
                        dve.tensor_scalar(kvs[:, 1, :], v_ps, colv(f"bv{l}"), None, ALU.add).then_inc(evac_dve, 1)
                    else:
                        dve.scalar_tensor_tensor(out=kvs[:, 0, :], in0=k_ps, scalar=SCALE, in1=keep3[:, :],
                                                 op0=ALU.mult, op1=ALU.mult)
                        dve.tensor_copy(kvs[:, 1, :], v_ps).then_inc(evac_dve, 1)
                    if l in (1, 3):
                        if l == 1:
                            link(dve.tensor_scalar(mrow[:, :], rowv("mask1"), -3e38, 3e38, ALU.max, ALU.min))
                        else:
                            dve.wait_ge(mask_ready, B)
                            link(dve.tensor_scalar(mrow[:, :], keep3[:, :], 1e9, -1e9, ALU.mult, ALU.add))
                        link(dve.tensor_copy(msplit[:, 0, :], mrow[:, :]))
                        link(dve.tensor_tensor(mrow[:, :], mrow[:, :], msplit[:, 0, :], ALU.subtract))
                        link(dve.tensor_copy(msplit[:, 1, :], mrow[:, :]))
                        link(dve.tensor_tensor(mrow[:, :], mrow[:, :], msplit[:, 1, :], ALU.subtract))
                        for r in range(2):
                            dve.tensor_copy(msel[32 * r:32 * r + 32, :], msplit[32 * r:32 * r + 32, r, :])
                        dve.tensor_copy(msel[64:P, :], mrow[64:P, :]).then_inc(mask_split, 1)
                elif kind == "S":
                    k = nth(*item) - 1
                    r = k % 3
                    for c, (h0, h1) in enumerate(HEADS):
                        dve.wait_ge(scores_full, 3 * k + c + 1)
                        ins = dve.tensor_reduce(mx[:, r, h0:h1], bank(item[1:], c)[:, 0:SK * (h1 - h0)]
                                                .rearrange("p (h k) -> p h k", k=SK), AX.X, ALU.max)
                    link(ins)
                    if k >= 3:
                        dve.wait_ge(pt_full, 3 * (k - 2))
                    for c, (h0, h1) in enumerate(HEADS):
                        dve.tensor_tensor(
                            probs[:, r, SK * h0:SK * h1].rearrange("p (h k) -> p h k", k=SK),
                            bank(item[1:], c)[:, 0:SK * (h1 - h0)].rearrange("p (h k) -> p h k", k=SK),
                            mx[:, r, h0:h1].rearrange("p (h a) -> p h a", a=1).broadcast_to([P, h1 - h0, SK]),
                            ALU.subtract).then_inc(scores_taken, 1)
                elif kind == "N":
                    k = nth(*item) - 1
                    r = k % 3
                    for c, (k0, k1) in enumerate(HALVES):
                        dve.wait_ge(exp_ready, 2 * k + 1 + c)
                        ins = dve.tensor_reduce(den[:, r, k0 // SK:k1 // SK],
                                                probs[:, r, k0:k1].rearrange("p (h k) -> p h k", k=SK),
                                                AX.X, ALU.add)
                    link(ins)
                    dve.reciprocal(rden[:, r, :], den[:, r, :]).then_inc(rden_ready, 1)
                elif kind == "back":
                    _, l, u = item
                    ps = filled(dve, ("backT", l, u))
                    update(unit(u), ps[:, 0:UQ], tg[:, 9:10] if l == 0 else tg[:, l:l + 1]).then_inc(evac_back, 1)
                    emptied(dve, ("backT", l, u))
                elif kind in ("f0", "f2"):
                    u = item[1]
                    emptied(dve, item)
                    if kind == "f0":
                        yy = scr[:, 0, 0:UQ]
                        link(dve.tensor_tensor(yy.rearrange("p (i n) -> p i n", n=P),
                                               y16[:, :].rearrange("p (i n) -> p i n", n=P),
                                               over_tiles(rowv("fb0"), P), ALU.add))
                        update(unit(u), yy, tg[:, 4:5]).then_inc(x_new, 1)
                    else:
                        link(dve.tensor_tensor(y2.rearrange("p (i n) -> p i n", n=P),
                                               y2.rearrange("p (i n) -> p i n", n=P),
                                               over_tiles(fb2[:, :], P), ALU.add))
                        update(unit(u), y2, tg[:, 6:7]).then_inc(x_new, 1)
                    dve.wait_ge(x_new, nth_f(*item))
                elif kind == "quant":
                    u = item[1]
                    emptied(dve, ("xt", 5, u))
                    link(dve.tensor_scalar(scr[:, 0, 0:UQ], xb[:, u, :], sc[:, 0:1], None, ALU.mult))
                    round8(xb[:, u, :], scr[:, 0, 0:UQ], scr[:, 1, 0:UQ]).then_inc(quant_ready, 1)
                elif kind == "r1":
                    b = item[1]
                    ps = filled(dve, item)
                    dve.tensor_tensor(hr[:, b], ps[:, 0:NT * 64].rearrange("p (i n) -> p i n", n=64),
                                      over_tiles(rowv("br1"), 64, NT), ALU.add).then_inc(evac_dve, 1)
                    emptied(dve, item)
                    rows = lambda t: hr[:, b, t % NT, :]
                    pending[U + b] = row_stats(rows, range(b * NT, (b + 1) * NT), 1e-6)
                elif kind == "r1b":
                    b = item[1]
                    rows = lambda t: hr[:, b, t % NT, :]
                    link(normalise(rows, rows, range(b * NT, (b + 1) * NT), pending[U + b]))
                    link(dve.tensor_tensor(hr[:, b], hr[:, b], over_tiles(rowv("lns"), 64, NT), ALU.mult))
                    dve.tensor_tensor(hr[:, b], hr[:, b], over_tiles(rowv("lnb"), 64, NT), ALU.add).then_inc(h_ready, 1)
                elif kind in ("r3", "g1"):
                    b = item[1]
                    ps = filled(dve, item)
                    logits = ps[:, 0:NT * E].rearrange("p (i e) -> p i e", e=E)
                    rank = over_tiles(rowv("rank"), E, NT)

                    def first_max(v, best, dst, tmp):
                        link(dve.tensor_reduce(best, v, AX.X, ALU.max))
                        link(dve.tensor_tensor(dst, v, over_experts(best), ALU.is_equal))
                        link(dve.tensor_tensor(dst, dst, rank, ALU.mult))
                        link(dve.tensor_reduce(tmp, dst, AX.X, ALU.max))
                        return dve.tensor_tensor(dst, dst, over_experts(tmp), ALU.is_equal)

                    if kind == "r3":
                        dve.tensor_tensor(lg[:, b], logits, over_tiles(rowv("br2"), E, NT), ALU.add).then_inc(evac_dve, 1)
                    else:
                        dve.tensor_copy(lg[:, b], logits).then_inc(evac_dve, 1)
                    emptied(dve, item)
                    m = [m12[:, b, q, :] for q in range(8)]
                    link(first_max(lg[:, b], m[0], oh[:, 0], m[1]))
                    if kind == "r3":
                        link(dve.scalar_tensor_tensor(out=lg[:, b], in0=oh[:, 0], scalar=-3e38, in1=lg[:, b],
                                                      op0=ALU.mult, op1=ALU.add))
                        link(first_max(lg[:, b], m[4], oh[:, 1], m[1]))
                        dve.tensor_tensor(m[2], m[4], m[0], ALU.subtract).then_inc(gap_ready, 1)
                    else:
                        for part in range(3):
                            ins = dve.tensor_copy(s24[:, b, :, part, :], oh[:, 0])
                        ins.then_inc(sel_ready, 1)
                elif kind == "xsplit":
                    b = item[1]
                    emptied(dve, ("xt", 3, (b + 1) * U // B - 1))
                    dve.wait_ge(pt_full, 3 * nth("T", 1, U // B + b, 1 - b))
                    link(dve.tensor_copy(x_hi[b], batch(xnT, b)))
                    dve.tensor_tensor(x_lo[b], batch(xnT, b), x_hi[b].bitcast(F32), ALU.subtract).then_inc(x_split, 1)
                elif kind == "xsplit3":
                    b = item[1]
                    emptied(dve, ("xt", 7, (b + 1) * U // B - 1))
                    dve.wait_ge(scores_full, 3 * nth("S", 3, U - 1, UT - 1))
                    link(dve.tensor_copy(x3_hi[:, b, :], batch(xnT, b)))
                    dve.tensor_tensor(x3_lo[:, b, :], batch(xnT, b), x3_hi[:, b, :].bitcast(F32),
                                      ALU.subtract).then_inc(x3_split, 1)
                    dve.wait_ge(x3_split, b + 1)
                elif kind == "r3b":
                    b = item[1]
                    m = [m12[:, b, q, :] for q in range(8)]
                    dve.wait_ge(gap_exp, nth(*item))
                    link(dve.tensor_scalar(m[5], m[3], 1.0, None, ALU.add))
                    link(dve.reciprocal(m[6], m[5]))
                    link(dve.tensor_tensor(m[7], m[3], m[6], ALU.mult))
                    link(dve.tensor_tensor(oh[:, 0], oh[:, 0], over_experts(m[6]), ALU.mult))
                    link(dve.tensor_tensor(oh[:, 1], oh[:, 1], over_experts(m[7]), ALU.mult))
                    link(dve.tensor_tensor(oh[:, 0], oh[:, 0], oh[:, 1], ALU.add))
                    for part in range(3):
                        link(dve.tensor_copy(sbf[:, :, :], oh[:, 0]))
                        ins = dve.tensor_copy(s24[:, b, :, part, :], sbf[:, :, :])
                        if part < 2:
                            link(ins)
                            link(dve.tensor_tensor(oh[:, 0], oh[:, 0], s24[:, b, :, part, :], ALU.subtract))
                    ins.then_inc(sel_ready, 1)
                elif kind == "moe1":
                    _, b, e0, e1 = item

                    def weigh(e, par, copied):
                        dve.wait_ge(y_step, FT * e + (FT * E * b + FT))
                        dve.wait_ge(evac_act, copied)
                        if not (b == 0 and e0 < 3 and e1 < E):
                            dve.wait_ge(acc_done, e + (E * b - 1))
                        dve.scalar_tensor_tensor(out=ytmp[:, par, :], in0=TB[par][:, :],
                                                 scalar=col[:, bass.ds(e + COL["b2"][0], 1)], in1=pbc[:, par, :],
                                                 op0=ALU.add, op1=ALU.mult).then_inc(ytmp_ready, 1)

                    def expert(e, par, before):
                        for j in range(FT):
                            dve.wait_ge(gelu_ready, FT * e + (FT * E * b + j + 1))
                            if not (b == 0 and e0 == 0 and j < 2):
                                dve.wait_ge(y_step, FT * e + (FT * E * b + j - 1))
                            dve.scalar_tensor_tensor(out=gg[:, j % 2, :], in0=SC[2 * (j % 2)][:, :],
                                                     scalar=col[:, bass.ds(e * 2 * FT + (COL["b1"][0] + j), 1)],
                                                     in1=gel[:, j % 2, :], op0=ALU.add,
                                                     op1=ALU.mult).then_inc(g_ready, 1)
                            if j == 0 and before is not None:
                                weigh(e - 1, 1 - par, before)

                    if e1 - e0 > 1:
                        taken = USE["bc1", b, e0][2] - e0
                        with dve.Fori(e0, e1, 2) as e:
                            expert(e, 0, e + (taken - 1))
                            expert(e + 1, 1, e + taken)
                    else:
                        expert(e0, e0 % 2, USE["bc1", b, e0 - 1][2] if e0 else None)
                    if e1 == E:
                        weigh(E - 1, (E - 1) % 2, USE["bc1", b, E - 1][2])
                elif kind == "back1":
                    u = item[1]
                    ps = filled(dve, item)
                    update(unit(u), ps[:, 0:UQ], tg[:, 5:6]).then_inc(evac_dve, 1)
                    emptied(dve, item)
                elif kind == "moe3":
                    b = item[1]
                    for e in masked(*item[2:]):
                        n = E * b + e
                        ps = filled(dve, ("bc3", b, e))
                        if n >= 2:
                            dve.wait_ge(mm3, n - 1)
                        for part, rows in ((xm_hi, x3_hi), (xm_lo, x3_lo)):
                            ins = dve.scalar_tensor_tensor(out=part[:, n % 2, :], in0=ps[:, :], scalar=1.0,
                                                           in1=rows[:, b, :].bitcast(F32), op0=ALU.min,
                                                           op1=ALU.mult)
                        ins.then_inc(evac_dve, 1)
                elif kind == "z3":
                    b = item[1]
                    ps = filled(dve, item)
                    dve.tensor_tensor(zz[:, b], ps[:, :].rearrange("p (i n) -> p i n", n=P),
                                      xn[:, b * NT:(b + 1) * NT, :], ALU.add).then_inc(evac_dve, 1)
                    emptied(dve, item)
                elif kind == "norm3":
                    b = item[1]
                    tiles = range(b * NT, (b + 1) * NT)
                    rows = lambda t: zz[:, b, t % NT, :]
                    n = row_stats(rows, tiles, 1e-12)
                    for t in tiles:
                        ins = dve.scalar_tensor_tensor(out=rows(t), in0=rows(t), scalar=mv[:, t, 0:1],
                                                       in1=rowv("gamma"), op0=ALU.subtract, op1=ALU.mult)
                    link(ins)
                    dve.wait_ge(rstd_ready, n)
                    for t in tiles:
                        ins = dve.scalar_tensor_tensor(out=rows(t), in0=rows(t), scalar=rstd[:, t:t + 1],
                                                       in1=rowv("beta"), op0=ALU.mult, op1=ALU.add)
                    link(ins)
                    update(tiles, zz[:, b].rearrange("p i n -> p (i n)"), tg[:, 7:8]).then_inc(out_ready, 1)

        @block.tensor
        def _(pe):
            pe.wait_ge(ld_ident, 16)
            pe.wait_ge(ld_kv, 16)
            for item in ORDER:
                kind = item[0]
                if kind == "kv0":
                    j = item[1]
                    if j % 2 == 0:
                        pe.wait_ge(ld_kvj[j // 2], 16)
                    for which in "kv":
                        ps = acquire(pe, item + (which,))
                        pe.matmul(ps[:, 0:B * SK], weight0(which, j), ctxT,
                                  start=True, stop=True).then_inc(misc_full, 1)
                elif kind == "kp0":
                    j = item[1]
                    for which, w, src in (("k", "q", kbd), ("v", "out", vbd)):
                        ps = acquire(pe, item + (which,))
                        emptied(pe, ("kv0", j, which))
                        pe.matmul(ps[:, 0:4 * SK], weight0(w, j), src[:, j % 2].rearrange("p h n -> p (h n)"),
                                  start=True, stop=True).then_inc(misc_full, 1)
                elif kind == "vp":
                    _, l, b, g = item
                    c0, c1 = GROUPS[g]
                    ps = acquire(pe, item)
                    if l == 0:
                        emptied(pe, ("kp0", 7, "v"))
                    else:
                        pe.wait_ge(blocks_ready, 4 * (l - 1) + b + 1)
                    for c in range(c0, c1):
                        k0, n = CH[c]
                        dst = ps[0:n, P * (c - c0):P * (c - c0) + P]
                        src = Vb[:, b, k0:k0 + n]
                        if l < 2:
                            ins = pe.transpose(dst, src, ident)
                        else:
                            ins = pe.matmul(dst, src, sq(f"wo{l}"), start=True, stop=True)
                    ins.then_inc(misc_full, 1)
                elif kind == "xt":
                    _, s, u = item
                    ps = acquire(pe, item)
                    pe.wait_ge(xn_ready, nth_x(s, u))
                    for i in range(UT):
                        ins = pe.transpose(ps[:, i * P:(i + 1) * P], xn[:, u * UT + i, :], ident)
                    ins.then_inc(misc_full, 1)
                elif kind == "q":
                    _, l, u = item
                    ps = acquire(pe, item)
                    emptied(pe, ("xt", 2 * l, u))
                    pe.matmul(ps[:, 0:UQ], sq(f"wq{l}"), xnT[:, u, :], start=True, stop=True).then_inc(misc_full, 1)
                elif kind == "kvT":
                    l = item[1]
                    ps = acquire(pe, item)
                    pe.wait_ge(ld_sqw, 16)
                    pe.matmul(ps[:, 0:B * SK], sq(f"wk{l}"), ctxT, start=True, stop=True)
                    pe.matmul(ps[:, 256:256 + B * SK], sq(f"wv{l}"), ctxT,
                              start=True, stop=True).then_inc(misc_full, 1)
                elif kind == "S":
                    _, l, u, i = item
                    k = nth(*item) - 1
                    if i == 0:
                        emptied(pe, ("q", l, u) if l else ("xt", 0, u))
                    if l == 0 and k == 0:
                        emptied(pe, ("kp0", 7, "k"))
                    if l and u == 0 and i == 0:
                        pe.wait_ge(blocks_ready, 4 * l)
                        if l in (1, 3):
                            pe.wait_ge(mask_ready, B * (l + 1) // 2)
                        if l == 2:
                            pe.wait_ge(g_ready, B * E * FT)
                    q = xnT[:, u, i * P:(i + 1) * P]
                    for c, (h0, h1) in enumerate(HEADS):
                        n = 3 * k + c
                        if n >= 4:
                            pe.wait_ge(scores_taken, n - 3)
                        dst = bank(item[1:], c)[:, 0:SK * (h1 - h0)]
                        masked = l in (1, 3)
                        ins = pe.matmul(dst, q, Kp[l % 2][:, u * B // U, SK * h0:SK * h1], start=True, stop=not masked)
                        if masked:
                            ins = pe.matmul(dst, ones3[:, :], maskrow[:, u * B // U, SK * h0:SK * h1], start=False, stop=True)
                        ins.then_inc(scores_full, 1)
                elif kind == "T":
                    _, l, u, i = item
                    k = nth(*item) - 1
                    pe.wait_ge(probs_ready, k + 1)
                    if l == 2 and u == 0 and i == 0:
                        pe.wait_ge(ytmp_ready, B * E)
                    for g, (c0, c1) in enumerate(GROUPS):
                        n = 3 * k + g
                        if n >= 2:
                            pe.wait_ge(pt_copied, n - 1)
                        for c in range(c0, c1):
                            k0, m = CH[c]
                            ins = pe.transpose(TB[n % 2][0:m, P * (c - c0):P * (c - c0) + P],
                                               probs[:, k % 3, k0:k0 + m], ident)
                        ins.then_inc(pt_full, 1)
                elif kind == "PV":
                    _, l, u = item
                    ps = acquire(pe, item)
                    emptied(pe, ("vp", l, u * B // U, 2))
                    half = nth(*item) % 2
                    starts = [c0 for c0, _ in GROUPS]
                    for c, (k0, m) in enumerate(CH):
                        if c in starts:
                            pe.wait_ge(pt_copied, 3 * (nth("T", l, u, UT - 1) - 1) + starts.index(c) + 1)
                        ins = pe.matmul(ps[:, 0:UQ], Vp[0:m, l % 2, u * B // U, c, :], PT[0:m, half, c, :],
                                        start=(c == 0), stop=(c == len(CH) - 1))
                    ins.then_inc(misc_full, 1)
                elif kind == "backT":
                    _, l, u = item
                    ps = acquire(pe, item)
                    emptied(pe, ("PV", l, u))
                    for i in range(UT):
                        ins = pe.transpose(ps[:, i * P:(i + 1) * P], oT[:, i * P:(i + 1) * P], ident)
                    ins.then_inc(misc_full, 1)
                elif kind in ("f0", "f2"):
                    u = item[1]
                    ps = acquire(pe, item)
                    pe.wait_ge(w8_ready, 1 if kind == "f0" else 2)
                    if kind == "f0":
                        emptied(pe, ("xt", 1, u))
                    else:
                        pe.wait_ge(quant_ready, nth("quant", u))
                    src, w = (xq8, w8) if kind == "f0" else (xb, k8)
                    for i in range(UT):
                        ins = pe.matmul(ps[:, i * P:(i + 1) * P], src[:, u, i * P:(i + 1) * P], w[:, :],
                                        start=True, stop=True)
                    ins.then_inc(misc_full, 1)
                elif kind in ("r1", "g1"):
                    b = item[1]
                    ps = acquire(pe, item)
                    emptied(pe, ("xt", 3 if kind == "r1" else 7, (b + 1) * U // B - 1))
                    w, n = (sq("wr1"), 64) if kind == "r1" else (sq("wrT3"), E)
                    for i in range(NT):
                        ins = pe.matmul(ps[:, i * n:(i + 1) * n], batch(xnT, b)[:, i * P:(i + 1) * P], w,
                                        start=True, stop=True)
                    ins.then_inc(misc_full, 1)
                elif kind == "r2":
                    b = item[1]
                    ps = acquire(pe, item)
                    pe.wait_ge(hg_ready, nth("r1b", b))
                    for i in range(NT):
                        ins = pe.transpose(ps[0:64, i * P:(i + 1) * P], hr[:, b, i, :], ident)
                    ins.then_inc(misc_full, 1)
                elif kind == "r3":
                    b = item[1]
                    ps = acquire(pe, item)
                    emptied(pe, ("r2", b))
                    for i in range(NT):
                        ins = pe.matmul(ps[:, i * E:(i + 1) * E], hT[:, i * P:(i + 1) * P], sq("wr2")[0:64, :],
                                        start=True, stop=True)
                    ins.then_inc(misc_full, 1)
                elif kind in ("r4", "g2"):
                    b = item[1]
                    ps = acquire(pe, item)
                    pe.wait_ge(sel_ready, nth("g1", b) + B if kind == "g2" else nth("r3", b))
                    for i in range(NT):
                        ins = pe.transpose(ps[0:3 * E, i * P:(i + 1) * P],
                                           s24[:, b, i].rearrange("p t e -> p (t e)"), ident)
                    ins.then_inc(misc_full, 1)
                elif kind == "moe1":
                    _, b, e0, e1 = item

                    def up(n):
                        e, j = divmod(n - FT * E * b, FT)
                        if n >= 2:
                            pe.wait_ge(g_ready, n - 1)
                        if j == 0:
                            pe.wait_ge(w_split, E * b + e + 1)
                        for half in range(2):
                            at = slice(half * F1 + j * P, half * F1 + (j + 1) * P)
                            hi, lo = w_hi[:, e % 2, at], w_lo[:, e % 2, at]
                            dst = SC[2 * (n % 2) + half][:, :]
                            pe.matmul(dst, hi, x_hi[b], start=True, stop=False)
                            pe.matmul(dst, hi, x_lo[b], start=False, stop=False)
                            ins = pe.matmul(dst, lo, x_hi[b], start=False, stop=True)
                        ins.then_inc(x12_full, 1)

                    if e0 == 0:
                        if b == 0:
                            pe.wait_ge(ld_w1, 32)
                            pe.wait_ge(ld_small, 64)
                            pe.wait_ge(scores_taken, 3 * nth("S", 1, U - 1, UT - 1))
                            pe.wait_ge(pt_copied, 3 * nth("T", 1, U - 1, UT - 1))
                        pe.wait_ge(x_split, b + 1)
                        up(FT * E * b)
                    for e in range(e0, e1):
                        m = E * b + e
                        ps = acquire(pe, ("bc1", b, e))
                        emptied(pe, ("r4", b))
                        pe.matmul(ps[:, :], esel[:, e, :], selT[:, b, :], start=True,
                                  stop=True).then_inc(misc_full, 1)
                        for j in range(FT):
                            n = FT * m + j
                            if not (e == E - 1 and j == FT - 1):
                                up(n + 1)
                            pe.wait_ge(g_ready, n + 1)
                            if j == 0 and m >= 2:
                                pe.wait_ge(ytmp_ready, m - 1)
                            pe.matmul(TB[m % 2][:, :], w2[:, e, j, :], gg[:, n % 2, :], start=(j == 0),
                                      stop=(j == FT - 1)).then_inc(y_step, 1)
                elif kind == "back1":
                    u = item[1]
                    ps = acquire(pe, item)
                    b, within = divmod(u * UQ, SQ)
                    pe.wait_ge(acc_done, E * (b + 1))
                    for i in range(UT):
                        at = within + i * P
                        ins = pe.transpose(ps[:, i * P:(i + 1) * P], acc[:, b, at:at + P], ident)
                    ins.then_inc(misc_full, 1)
                elif kind == "moe3":
                    _, b, e0, e1 = item
                    if b == 0 and e0 == 0:
                        pe.wait_ge(w3_split, 4)
                        pe.wait_ge(scores_taken, 3 * nth("S", 3, U - 1, UT - 1))

                    def share(e):
                        ps = acquire(pe, ("bc3", b, e))
                        pe.matmul(ps[:, :], esel[:, e, :], selT[:, b, :], start=True,
                                  stop=True).then_inc(misc_full, 1)

                    emptied(pe, ("g2", b))
                    if e0 == 0:
                        share(0)
                        for f in range(FT):
                            if b:
                                pe.wait_ge(inter_ready, f + 1)
                            pe.matmul(SC[f][:, :], b13s[:, f * P:(f + 1) * P], selT[:, b, :],
                                      start=True, stop=False)
                    for e in range(e0, e1):
                        if e + 1 < E:
                            share(e + 1)
                        emptied(pe, ("bc3", b, e))
                        for f in range(FT):
                            hi, lo = w3_hi[:, e, f * P:(f + 1) * P], w3_lo[:, e, f * P:(f + 1) * P]
                            pe.matmul(SC[f][:, :], hi, xm_hi[:, e % 2, :], start=False, stop=False)
                            pe.matmul(SC[f][:, :], hi, xm_lo[:, e % 2, :], start=False, stop=False)
                            ins = pe.matmul(SC[f][:, :], lo, xm_hi[:, e % 2, :], start=False, stop=(e == E - 1))
                            if e == E - 1 and f < FT - 1:
                                ins.then_inc(pre3_full, 1)
                        ins.then_inc(mm3, 1)
                elif kind == "y3":
                    b = item[1]
                    ps = acquire(pe, item)
                    for f in range(FT):
                        pe.wait_ge(inter_ready, FT * b + f + 1)
                        ins = pe.matmul(ps[:, :], wo3[:, f, :], inter[:, f, :], start=(f == 0), stop=(f == FT - 1))
                    ins.then_inc(misc_full, 1)
                elif kind == "z3":
                    b = item[1]
                    ps = acquire(pe, item)
                    emptied(pe, ("y3", b))
                    for i in range(NT):
                        ins = pe.transpose(ps[:, i * P:(i + 1) * P], yT3[:, b, i * P:(i + 1) * P], ident)
                    ins.then_inc(misc_full, 1)


def nth_x(s, u):
    return [i for i in ORDER if i[0] == "ln_apply" and i[1] >= 0].index(("ln_apply", s, u)) + 1


def nth_f(*item):
    return [i for i in ORDER if i[0] in ("f0", "f2")].index(item) + 1


def kernel(**inputs):
    import numpy as _np
    import concourse.bacc as _bacc
    from concourse import mybir as _mybir
    from concourse.bass_utils import run_bass_kernel_spmd as _run

    a = {k: _np.asarray(v) for k, v in inputs.items()}
    f32 = _np.float32

    def tiles(w):
        n = w.shape[0] // P
        return w.reshape(n, P, w.shape[1]).transpose(1, 0, 2).reshape(P, n * w.shape[1])

    def padded(w, rows=P):
        z = _np.zeros((rows,) + w.shape[1:], w.dtype)
        z[: w.shape[0]] = w
        return z

    wkv = a["L0_xattn_w_kv"]
    four = [wkv[:, :1024], wkv[:, 1024:], tiles(a["L0_xattn_w_q"].T), tiles(a["L0_xattn_w_out"])]
    kvp = _np.concatenate([a["ctx_1024"].reshape(B * SK, P).T]
                          + [w[:, j * P:(j + 1) * P] for j in range(8) for w in four], axis=1)
    eye = _np.eye(P, dtype=f32)
    sqwp = _np.concatenate(
        [eye, a["L0_ffn_weight"].T, a["L1_xattn_Wq"], a["L1_xattn_Wk"], a["L1_xattn_Wv"]]
        + [a[f"L{l}_xattn_W{n}"].T for l in (2, 3) for n in "qkvo"]
        + [a["L1_ffn_Wr1"], padded(a["L1_ffn_Wr2"]), a["L3_ffn_Wr"].T], axis=1)
    heads = _np.zeros((P, H), f32)
    for h in range(H):
        heads[8 * h:8 * h + 8, h] = 1.0
    third = _np.zeros((P, 3), f32)
    for r in range(3):
        third[E * r:E * r + E, r] = 1.0
    vec = ["L0_xattn_ln_gamma", "L0_xattn_ln_beta", "L0_xattn_b_out", "L1_xattn_bq", "L1_xattn_bk", "L1_xattn_bv",
           "L2_xattn_bq", "L2_xattn_bk", "L2_xattn_bv", "L2_xattn_bo", "L3_xattn_bo", "L3_ffn_bo"]
    colp = _np.concatenate([a[n].reshape(P, 1) for n in vec]
                           + [a["L1_ffn_b2"].T, a["L1_ffn_b1"].reshape(E, 2 * FT, P).transpose(2, 0, 1)
                              .reshape(P, 2 * FT * E), heads, third], axis=1)
    rowp = _np.concatenate([a["L0_ffn_bias"], a["L1_ffn_br1"], a["L1_ffn_ln_scale"], a["L1_ffn_ln_bias"],
                            a["L1_ffn_br2"], a["L3_ffn_gamma"], a["L3_ffn_beta"], a["g_xattn"], a["g_ffn"],
                            a["L0_xattn_gate"], a["L2_ffn_input_scale"], a["L2_ffn_kernel_scale"],
                            a["mask_Bx1x1xS2_ff0"].reshape(-1), _np.arange(E, 0, -1).astype(f32)]).reshape(1, -1)
    sel = _np.zeros((P, E, P), f32)
    for e in range(E):
        for r in range(3):
            sel[E * r + e, e, :] = 1.0
    bf = a["L2_ffn_kernel"].dtype
    arrays = {
        "x_in": a["x"].reshape(B * NT, P, P).transpose(1, 0, 2),
        "kv_in": kvp, "sqw_in": sqwp, "col_in": colp, "row_in": rowp,
        "w1_in": a["L1_ffn_W1"].transpose(1, 0, 2),
        "w2_in": a["L1_ffn_W2"].reshape(E, FT, P, P).transpose(2, 0, 1, 3),
        "w3_in": a["L3_ffn_W1"].transpose(1, 0, 2),
        "wo3_in": a["L3_ffn_Wo"].reshape(FT, P, P).transpose(1, 0, 2),
        "b13_in": padded(_np.concatenate([a["L3_ffn_b1"]] * 3, axis=0)),
        "mask3_in": a["mask_BxS2_ik0"].reshape(1, -1),
        "k8_in": a["L2_ffn_kernel"], "fb2_in": a["L2_ffn_bias"].reshape(1, -1),
        "esel_in": sel.astype(bf),
    }
    arrays = {k: _np.ascontiguousarray(v) for k, v in arrays.items()}
    nc = _bacc.Bacc("TRN2", target_bir_lowering=False, num_devices=1)
    args = [nc.dram_tensor(k, v.shape, _mybir.dt.from_np(v.dtype), kind="ExternalInput").ap()
            for k, v in arrays.items()]
    out = nc.dram_tensor("out", (P, B * NT, P), _mybir.dt.float32, kind="ExternalOutput").ap()
    build(nc, *args, out)
    r = _run(nc, [arrays], core_ids=[0])
    return r.results[0]["out"].transpose(1, 0, 2).reshape(B, SQ, P)
```
